# Optimizing a Trainium2 kernel written in Bass

```python
import numpy as np
import jax
import jax.numpy as jnp

def _softmax(x, axis=-1):
    return jax.nn.softmax(x, axis=axis)

def _gelu(x):
    return jax.nn.gelu(x, approximate=True)

def _silu(x):
    return jax.nn.silu(x)

def _sigmoid(x):
    return jax.nn.sigmoid(x)

def _layernorm(x, axis=-1, eps=1e-05):
    m = jnp.mean(x, axis=axis, keepdims=True)
    v = jnp.var(x, axis=axis, keepdims=True)
    return (x - m) / jnp.sqrt(v + eps)

def _scatter_add(tgt, idx, src, axis=0):
    return tgt.at[idx].add(src)

def _segment_sum(src, seg, n):
    return jax.ops.segment_sum(src, seg, n)
kernel_name = 'mk_flamingo_gated_d4_seqx_r8_277054'

def setup_inputs(seed: int=0):
    np.random.seed(seed)
    _w = jnp.asarray

    def _rec_inputs():
        import jax
        import jax.numpy as jnp
        _rk = jax.random.key(seed)
        x = -0.0002928 + 1 * jax.random.normal(jax.random.fold_in(_rk, 1), (16, 64, 256), jnp.float32)
        _lenS = 64 - jax.random.randint(jax.random.fold_in(_rk, 7), (16,), 0, max(1, 64 // 4) + 1, jnp.int32)
        _lenS2 = 64 - jax.random.randint(jax.random.fold_in(_rk, 8), (16,), 0, max(1, 64 // 4) + 1, jnp.int32)
        _ctx_2048P = jax.random.normal(jax.random.fold_in(_rk, 11), (16, 16, 256), jnp.float32)
        _ctx_2048c = jax.random.dirichlet(jax.random.fold_in(_rk, 511), 0.3 * jnp.ones((16,), jnp.float32), (16, 64))
        _ctx_2048t = jnp.einsum('bsk,bkd->bsd', _ctx_2048c, _ctx_2048P)
        _ctx_2048t = _ctx_2048t * jax.lax.rsqrt(jnp.mean(jnp.square(_ctx_2048t)) + 1e-12) * 0.953939
        ctx_2048 = 4.13588e-05 + 0.999923 * (_ctx_2048t + 0.3 * jax.random.normal(jax.random.fold_in(_rk, 611), (16, 64, 256), jnp.float32))
        _validS = jnp.arange(64)[None, :] < _lenS[:, None]
        _validS2 = jnp.arange(64)[None, :] < _lenS2[:, None]
        _causal = jnp.tril(jnp.ones((64, 64), dtype=bool))
        mask_1xSxS2_ff0 = jnp.where(jnp.ones((1, 64, 64), dtype=bool), 0.0, -1000000000.0).astype(jnp.float32)
        _g = jax.random.normal(jax.random.fold_in(_rk, 9001), (2, 4), jnp.float32)
        _g = jnp.sign(_g) * jnp.maximum(jnp.abs(_g), 1.0) + (_g == 0) * 1.0
        g_xattn = _g[0]
        g_ffn = _g[1]
        return (x, ctx_2048, mask_1xSxS2_ff0, g_xattn, g_ffn)
    x, ctx_2048, mask_1xSxS2_ff0, g_xattn, g_ffn = _rec_inputs()

    def _L0_xattn_setup():
        import jax, jax.numpy as jnp
        import numpy as np
        H = 256
        NH = 16
        NKV = 4
        HD = 128
        GROUPS = NH // NKV
        EPS = 1e-06
        B, S, SE = (1, 256, 512)

        def _rmsnorm(x, w, eps=EPS):
            xf = x.astype(jnp.float32)
            var = jnp.mean(xf * xf, axis=-1, keepdims=True)
            return (xf * jax.lax.rsqrt(var + eps)).astype(x.dtype) * w
        key = jax.random.key(seed)
        ks = jax.random.split(key, 12)
        sc = 0.02
        return {'hidden_states': jax.random.normal(ks[0], (B, S, H), jnp.float32), 'encoder_hidden_states': jax.random.normal(ks[1], (B, SE, H), jnp.float32), 'attention_mask': jnp.zeros((B, S, SE), jnp.float32), 'Wq': jax.random.normal(ks[2], (H, NH * HD), jnp.float32) * sc, 'bq': jax.random.normal(ks[3], (NH * HD,), jnp.float32) * sc, 'Wk': jax.random.normal(ks[4], (H, NKV * HD), jnp.float32) * sc, 'bk': jax.random.normal(ks[5], (NKV * HD,), jnp.float32) * sc, 'Wv': jax.random.normal(ks[6], (H, NKV * HD), jnp.float32) * sc, 'bv': jax.random.normal(ks[7], (NKV * HD,), jnp.float32) * sc, 'Wo': jax.random.normal(ks[8], (NH * HD, H), jnp.float32) * sc, 'qn_w': jnp.ones((HD,), jnp.float32), 'kn_w': jnp.ones((HD,), jnp.float32)}
    _L0_xattn_all = _L0_xattn_setup()
    _L0_xattn_in = {k: v for k, v in _L0_xattn_all.items() if k in ('Wq', 'bq', 'Wk', 'bk', 'Wv', 'bv', 'Wo', 'qn_w', 'kn_w')}
    del _L0_xattn_all

    def _L0_ffn_setup():
        import jax, jax.numpy as jnp
        import numpy as np
        NUM_EXPERTS = 32
        TOP_K = 8
        SELECT_TOP_K = 4
        THRESHOLD = 0.5
        HIDDEN = 256
        D_FF = 96

        def _moe_forward(hidden_states, gate_weight, gate_up_proj, down_proj, similarity):
            B, S_len, H = hidden_states.shape
            E, K, Ssel = (NUM_EXPERTS, TOP_K, SELECT_TOP_K)
            x = hidden_states.reshape(-1, H)
            router_logits = x @ gate_weight.T
            router_probs = jax.nn.softmax(router_logits.astype(jnp.float32), axis=-1).astype(router_logits.dtype)
            router_top_value, router_indices = jax.lax.top_k(router_probs, K)
            routing_weights = router_top_value / jnp.clip(jnp.sum(router_top_value, axis=-1, keepdims=True), 1e-12, None)
            sim = similarity.astype(jnp.float32)
            sim = sim.at[jnp.arange(E), jnp.arange(E)].set(1.0)
            prim = router_indices[:, :Ssel]
            sec = router_indices[:, Ssel:]
            sim_cand = sim[sec[:, :, None], prim[:, None, :]]
            best_sim = jnp.max(sim_cand, axis=-1)
            best_i = jnp.argmax(sim_cand, axis=-1)
            prim_rep = jnp.broadcast_to(prim[:, None, :], sim_cand.shape)
            best_primary = jnp.take_along_axis(prim_rep, best_i[..., None], axis=-1)[..., 0]
            new_sec = jnp.where(best_sim < THRESHOLD, sec, best_primary) if THRESHOLD > 0.0 else best_primary
            rerouted_indices = jnp.concatenate([prim, new_sec], axis=1)
            combine = jnp.sum(jax.nn.one_hot(rerouted_indices, E, dtype=routing_weights.dtype) * routing_weights[..., None], axis=1)

            def expert_step(y, params):
                wgu, wd, cw = params
                gu = x @ wgu.T
                g, u = jnp.split(gu, 2, axis=-1)
                h = jax.nn.silu(g) * u
                y = y + h @ wd.T * cw[:, None]
                return (y, None)
            y0 = jnp.zeros_like(x)
            y, _ = jax.lax.scan(expert_step, y0, (gate_up_proj, down_proj, combine.T))
            return y.reshape(B, S_len, H)
        key = jax.random.key(seed)
        ks = jax.random.split(key, 5)
        hidden_states = jax.random.normal(ks[0], (4, 256, HIDDEN), dtype=jnp.float32)
        gate_weight = jax.random.normal(ks[1], (NUM_EXPERTS, HIDDEN), dtype=jnp.float32) * 0.02
        gate_up_proj = jax.random.normal(ks[2], (NUM_EXPERTS, 2 * D_FF, HIDDEN), dtype=jnp.float32) * 0.02
        down_proj = jax.random.normal(ks[3], (NUM_EXPERTS, HIDDEN, D_FF), dtype=jnp.float32) * 0.02
        similarity = jax.random.uniform(ks[4], (NUM_EXPERTS, NUM_EXPERTS), dtype=jnp.float32)
        return {'hidden_states': hidden_states, 'gate_weight': gate_weight, 'gate_up_proj': gate_up_proj, 'down_proj': down_proj, 'similarity': similarity}
    _L0_ffn_all = _L0_ffn_setup()
    _L0_ffn_in = {k: v for k, v in _L0_ffn_all.items() if k in ('gate_weight', 'gate_up_proj', 'down_proj', 'similarity')}
    del _L0_ffn_all

    def _L1_xattn_setup():
        import jax, jax.numpy as jnp
        import numpy as np
        B, S, DIM, HD = (4, 128, 256, 128)
        H = DIM // HD
        GN_EPS = 0.001

        def _decay_masks(n_heads, seq_len):
            gam = 1.0 - 2.0 ** (-5.0 - jnp.arange(n_heads, dtype=jnp.float32))
            idx = jnp.arange(seq_len, dtype=jnp.float32)
            expo = idx[None, :] - idx[:, None]
            D = jnp.where(expo[None, :, :] <= 0, gam[:, None, None] ** expo[None, :, :], 0.0)
            return D / jnp.sqrt(D.sum(axis=-1))[:, None, :]
        key = jax.random.key(seed)
        ks = jax.random.split(key, 8)
        x = jax.random.normal(ks[0], (B, S, DIM), dtype=jnp.float32)
        k = jax.random.normal(ks[1], (B, S, DIM), dtype=jnp.float32)
        v = jax.random.normal(ks[2], (B, S, DIM), dtype=jnp.float32)
        Wh = jax.random.normal(ks[3], (H, HD, HD), dtype=jnp.float32) / np.sqrt(HD)
        wg_w = jax.random.normal(ks[4], (DIM, DIM), dtype=jnp.float32) / np.sqrt(DIM)
        wo_w = jax.random.normal(ks[5], (DIM, DIM), dtype=jnp.float32) / np.sqrt(DIM)
        gn_gamma = jnp.ones((DIM,), dtype=jnp.float32)
        gn_beta = jnp.zeros((DIM,), dtype=jnp.float32)
        return {'x': x, 'k': k, 'v': v, 'Wh': Wh, 'wg_w': wg_w, 'wo_w': wo_w, 'gn_gamma': gn_gamma, 'gn_beta': gn_beta}
    _L1_xattn_all = _L1_xattn_setup()
    _L1_xattn_in = {k: v for k, v in _L1_xattn_all.items() if k in ('Wh', 'wg_w', 'wo_w', 'gn_gamma', 'gn_beta')}
    del _L1_xattn_all

    def _L1_ffn_setup():
        import jax, jax.numpy as jnp
        import numpy as np
        HIDDEN = 256
        INTER = 704
        B, S = (2, 256)

        def _ternary(key, shape):
            return jax.random.randint(key, shape, -1, 2).astype(jnp.float32)
        key = jax.random.key(seed)
        ks = jax.random.split(key, 7)
        x = jax.random.normal(ks[0], (B, S, HIDDEN), dtype=jnp.float32)
        gate_w = _ternary(ks[1], (INTER, HIDDEN))
        up_w = _ternary(ks[2], (INTER, HIDDEN))
        down_w = _ternary(ks[3], (HIDDEN, INTER))
        gate_s = jax.random.uniform(ks[4], (INTER,), minval=0.01, maxval=0.1, dtype=jnp.float32)
        up_s = jax.random.uniform(ks[5], (INTER,), minval=0.01, maxval=0.1, dtype=jnp.float32)
        down_s = jax.random.uniform(ks[6], (HIDDEN,), minval=0.01, maxval=0.1, dtype=jnp.float32)
        return {'x': x, 'gate_w': gate_w, 'up_w': up_w, 'down_w': down_w, 'gate_s': gate_s, 'up_s': up_s, 'down_s': down_s}
    _L1_ffn_all = _L1_ffn_setup()
    _L1_ffn_in = {k: v for k, v in _L1_ffn_all.items() if k in ('gate_w', 'up_w', 'down_w', 'gate_s', 'up_s', 'down_s')}
    del _L1_ffn_all

    def _L2_xattn_setup():
        import jax, jax.numpy as jnp
        import numpy as np
        D_MODEL = 256
        NUM_HEADS = 16
        HEAD_DIM = D_MODEL // NUM_HEADS

        def _fq_sym(x, axis):
            s = jnp.max(jnp.abs(x), axis=axis, keepdims=True) / 127.0
            s = jnp.maximum(s, 1e-08)
            q = jnp.clip(jnp.round(x / s), -127.0, 127.0) * s
            return x + jax.lax.stop_gradient(q - x)

        def _fq_unsigned(x, axis):
            s = jnp.max(x, axis=axis, keepdims=True) / 255.0
            s = jnp.maximum(s, 1e-08)
            q = jnp.clip(jnp.round(x / s), 0.0, 255.0) * s
            return x + jax.lax.stop_gradient(q - x)
        key = jax.random.key(seed)
        ks = jax.random.split(key, 8)
        B, N, M, C = (2, 256, 64, D_MODEL)
        return {'x': jax.random.normal(ks[0], (B, N, C), jnp.float32), 'cond': jax.random.normal(ks[1], (B, M, C), jnp.float32), 'Wq': jax.random.normal(ks[2], (C, C), jnp.float32) * 0.02, 'bq': jnp.zeros((C,), jnp.float32), 'Wkv': jax.random.normal(ks[3], (C, 2 * C), jnp.float32) * 0.02, 'bkv': jnp.zeros((2 * C,), jnp.float32), 'Wp': jax.random.normal(ks[4], (C, C), jnp.float32) * 0.02, 'bp': jnp.zeros((C,), jnp.float32)}
    _L2_xattn_all = _L2_xattn_setup()
    _L2_xattn_in = {k: v for k, v in _L2_xattn_all.items() if k in ('Wq', 'bq', 'Wkv', 'bkv', 'Wp', 'bp')}
    del _L2_xattn_all

    def _L2_ffn_setup():
        import jax, jax.numpy as jnp
        import numpy as np
        B, S, H = (1, 256, 256)
        E, K, I = (16, 4, 176)
        IS = 352
        CAP = 128
        key = jax.random.key(seed)
        ks = jax.random.split(key, 8)
        sc = 0.02
        return {'hidden_states': jax.random.normal(ks[0], (B, S, H), jnp.float32), 'gate_w': jax.random.normal(ks[1], (E, H), jnp.float32) * sc, 'w_gate': jax.random.normal(ks[2], (E, H, I), jnp.float32) * sc, 'w_up': jax.random.normal(ks[3], (E, H, I), jnp.float32) * sc, 'w_down': jax.random.normal(ks[4], (E, I, H), jnp.float32) * sc, 'sw_gate': jax.random.normal(ks[5], (H, IS), jnp.float32) * sc, 'sw_up': jax.random.normal(ks[6], (H, IS), jnp.float32) * sc, 'sw_down': jax.random.normal(ks[7], (IS, H), jnp.float32) * sc}
    _L2_ffn_all = _L2_ffn_setup()
    _L2_ffn_in = {k: v for k, v in _L2_ffn_all.items() if k in ('gate_w', 'w_gate', 'w_up', 'w_down', 'sw_gate', 'sw_up', 'sw_down')}
    del _L2_ffn_all

    def _L3_xattn_setup():
        import jax, jax.numpy as jnp
        import numpy as np
        FP8_MAX = 448.0
        EPS = 1e-05

        def _fp8_roundtrip(x):
            return x.astype(jnp.float8_e4m3fn).astype(jnp.float32)

        def _div_clamp_fp8(x, scale):
            y = jnp.clip(x.astype(jnp.float32) / scale, -FP8_MAX, FP8_MAX)
            y = y.astype(jnp.bfloat16).astype(jnp.float32)
            return _fp8_roundtrip(y)

        def _ln(x, w, b):
            mu = jnp.mean(x, axis=-1, keepdims=True)
            var = jnp.mean(jnp.square(x - mu), axis=-1, keepdims=True)
            return (x - mu) * jax.lax.rsqrt(var + EPS) * w + b

        def _fp8_linear_pertensor(x, wq, w_scale, in_scale):
            xq = _div_clamp_fp8(x, in_scale)
            return jnp.einsum('bsi,oi->bso', xq * in_scale, wq) * w_scale

        def _gqa(q, k, v):
            scale = 1.0 / np.sqrt(q.shape[-1])
            scores = jnp.einsum('bsghd,btgd->bghst', q, k) * scale
            p = jax.nn.softmax(scores, axis=-1)
            return jnp.einsum('bghst,btgd->bsghd', p, v)
        key = jax.random.key(seed)
        ks = jax.random.split(key, 8)
        B, S, SC, H, NH, G, D = (2, 256, 64, 256, 16, 8, 128)

        def qw(k, out_f, in_f):
            w = jax.random.normal(k, (out_f, in_f), jnp.float32) * 0.02
            sc = jnp.max(jnp.abs(w)) / FP8_MAX
            return (_fp8_roundtrip(w / sc), sc.astype(jnp.float32))
        wq, wq_s = qw(ks[0], NH * D, H)
        wqx, wqx_s = qw(ks[1], NH * D, H)
        wk, wk_s = qw(ks[2], G * D, H)
        wv, wv_s = qw(ks[3], G * D, H)
        wproj, wp_s = qw(ks[4], H, 2 * NH * D)
        return {'hidden_states': jax.random.normal(ks[5], (B, S, H), jnp.float32), 'cond': jax.random.normal(ks[6], (B, SC, H), jnp.float32), 'ln_w': jnp.ones((H,), jnp.float32), 'ln_b': jnp.zeros((H,), jnp.float32), 'wq': wq, 'wq_scale': wq_s, 'q_in_scale': jnp.full((H,), 0.05, jnp.float32), 'wqx': wqx, 'wqx_scale': wqx_s, 'qx_in_scale': jnp.full((H,), 0.05, jnp.float32), 'wk': wk, 'wk_scale': wk_s, 'k_in_scale': jnp.full((H,), 0.05, jnp.float32), 'wv': wv, 'wv_scale': wv_s, 'v_in_scale': jnp.full((H,), 0.05, jnp.float32), 'w_kv_x': jax.random.normal(ks[7], (2 * G * D, H), jnp.float32) * 0.02, 'qln_w': jnp.ones((D,), jnp.float32), 'qln_b': jnp.zeros((D,), jnp.float32), 'kln_w': jnp.ones((D,), jnp.float32), 'kln_b': jnp.zeros((D,), jnp.float32), 'qxln_w': jnp.ones((D,), jnp.float32), 'qxln_b': jnp.zeros((D,), jnp.float32), 'kxln_w': jnp.ones((D,), jnp.float32), 'kxln_b': jnp.zeros((D,), jnp.float32), 'wproj': wproj, 'proj_w_scale': wp_s, 'proj_in_scale': jnp.asarray(0.05, jnp.float32), 'proj_smooth': jnp.full((2 * NH * D,), 0.05, jnp.float32)}
    _L3_xattn_all = _L3_xattn_setup()
    _L3_xattn_in = {k: v for k, v in _L3_xattn_all.items() if k in ('ln_w', 'ln_b', 'wq', 'wq_scale', 'q_in_scale', 'wqx', 'wqx_scale', 'qx_in_scale', 'wk', 'wk_scale', 'k_in_scale', 'wv', 'wv_scale', 'v_in_scale', 'w_kv_x', 'qln_w', 'qln_b', 'kln_w', 'kln_b', 'qxln_w', 'qxln_b', 'kxln_w', 'kxln_b', 'wproj', 'proj_w_scale', 'proj_in_scale', 'proj_smooth')}
    del _L3_xattn_all

    def _L3_ffn_setup():
        import jax, jax.numpy as jnp
        import numpy as np
        E, H, I = (8, 256, 512)
        TOP_K = 1
        B, S = (1, 256)
        key = jax.random.key(seed)
        ks = jax.random.split(key, 7)
        std = 0.02
        return {'hidden_states': jax.random.normal(ks[0], (B, S, H), dtype=jnp.float32), 'router_w': jax.random.normal(ks[1], (E, H), dtype=jnp.float32) * std, 'gate_up_proj': jax.random.normal(ks[2], (E, H, 2 * I), dtype=jnp.float32) * std, 'down_proj': jax.random.normal(ks[3], (E, I, H), dtype=jnp.float32) * std, 'shared_gate_w': jax.random.normal(ks[4], (H, I), dtype=jnp.float32) * std, 'shared_up_w': jax.random.normal(ks[5], (H, I), dtype=jnp.float32) * std, 'shared_down_w': jax.random.normal(ks[6], (I, H), dtype=jnp.float32) * std}
    _L3_ffn_all = _L3_ffn_setup()
    _L3_ffn_in = {k: v for k, v in _L3_ffn_all.items() if k in ('router_w', 'gate_up_proj', 'down_proj', 'shared_gate_w', 'shared_up_w', 'shared_down_w')}
    del _L3_ffn_all
    return {'x': x, 'ctx_2048': ctx_2048, 'mask_1xSxS2_ff0': mask_1xSxS2_ff0, 'g_xattn': g_xattn, 'g_ffn': g_ffn, 'L0_xattn_Wq': _L0_xattn_in['Wq'], 'L0_xattn_bq': _L0_xattn_in['bq'], 'L0_xattn_Wk': _L0_xattn_in['Wk'], 'L0_xattn_bk': _L0_xattn_in['bk'], 'L0_xattn_Wv': _L0_xattn_in['Wv'], 'L0_xattn_bv': _L0_xattn_in['bv'], 'L0_xattn_Wo': _L0_xattn_in['Wo'], 'L0_xattn_qn_w': _L0_xattn_in['qn_w'], 'L0_xattn_kn_w': _L0_xattn_in['kn_w'], 'L0_ffn_gate_weight': _L0_ffn_in['gate_weight'], 'L0_ffn_gate_up_proj': _L0_ffn_in['gate_up_proj'], 'L0_ffn_down_proj': _L0_ffn_in['down_proj'], 'L0_ffn_similarity': _L0_ffn_in['similarity'], 'L1_xattn_Wh': _L1_xattn_in['Wh'], 'L1_xattn_wg_w': _L1_xattn_in['wg_w'], 'L1_xattn_wo_w': _L1_xattn_in['wo_w'], 'L1_xattn_gn_gamma': _L1_xattn_in['gn_gamma'], 'L1_xattn_gn_beta': _L1_xattn_in['gn_beta'], 'L1_ffn_gate_w': _L1_ffn_in['gate_w'], 'L1_ffn_up_w': _L1_ffn_in['up_w'], 'L1_ffn_down_w': _L1_ffn_in['down_w'], 'L1_ffn_gate_s': _L1_ffn_in['gate_s'], 'L1_ffn_up_s': _L1_ffn_in['up_s'], 'L1_ffn_down_s': _L1_ffn_in['down_s'], 'L2_xattn_Wq': _L2_xattn_in['Wq'], 'L2_xattn_bq': _L2_xattn_in['bq'], 'L2_xattn_Wkv': _L2_xattn_in['Wkv'], 'L2_xattn_bkv': _L2_xattn_in['bkv'], 'L2_xattn_Wp': _L2_xattn_in['Wp'], 'L2_xattn_bp': _L2_xattn_in['bp'], 'L2_ffn_gate_w': _L2_ffn_in['gate_w'], 'L2_ffn_w_gate': _L2_ffn_in['w_gate'], 'L2_ffn_w_up': _L2_ffn_in['w_up'], 'L2_ffn_w_down': _L2_ffn_in['w_down'], 'L2_ffn_sw_gate': _L2_ffn_in['sw_gate'], 'L2_ffn_sw_up': _L2_ffn_in['sw_up'], 'L2_ffn_sw_down': _L2_ffn_in['sw_down'], 'L3_xattn_ln_w': _L3_xattn_in['ln_w'], 'L3_xattn_ln_b': _L3_xattn_in['ln_b'], 'L3_xattn_wq': _L3_xattn_in['wq'], 'L3_xattn_wq_scale': _L3_xattn_in['wq_scale'], 'L3_xattn_q_in_scale': _L3_xattn_in['q_in_scale'], 'L3_xattn_wqx': _L3_xattn_in['wqx'], 'L3_xattn_wqx_scale': _L3_xattn_in['wqx_scale'], 'L3_xattn_qx_in_scale': _L3_xattn_in['qx_in_scale'], 'L3_xattn_wk': _L3_xattn_in['wk'], 'L3_xattn_wk_scale': _L3_xattn_in['wk_scale'], 'L3_xattn_k_in_scale': _L3_xattn_in['k_in_scale'], 'L3_xattn_wv': _L3_xattn_in['wv'], 'L3_xattn_wv_scale': _L3_xattn_in['wv_scale'], 'L3_xattn_v_in_scale': _L3_xattn_in['v_in_scale'], 'L3_xattn_w_kv_x': _L3_xattn_in['w_kv_x'], 'L3_xattn_qln_w': _L3_xattn_in['qln_w'], 'L3_xattn_qln_b': _L3_xattn_in['qln_b'], 'L3_xattn_kln_w': _L3_xattn_in['kln_w'], 'L3_xattn_kln_b': _L3_xattn_in['kln_b'], 'L3_xattn_qxln_w': _L3_xattn_in['qxln_w'], 'L3_xattn_qxln_b': _L3_xattn_in['qxln_b'], 'L3_xattn_kxln_w': _L3_xattn_in['kxln_w'], 'L3_xattn_kxln_b': _L3_xattn_in['kxln_b'], 'L3_xattn_wproj': _L3_xattn_in['wproj'], 'L3_xattn_proj_w_scale': _L3_xattn_in['proj_w_scale'], 'L3_xattn_proj_in_scale': _L3_xattn_in['proj_in_scale'], 'L3_xattn_proj_smooth': _L3_xattn_in['proj_smooth'], 'L3_ffn_router_w': _L3_ffn_in['router_w'], 'L3_ffn_gate_up_proj': _L3_ffn_in['gate_up_proj'], 'L3_ffn_down_proj': _L3_ffn_in['down_proj'], 'L3_ffn_shared_gate_w': _L3_ffn_in['shared_gate_w'], 'L3_ffn_shared_up_w': _L3_ffn_in['shared_up_w'], 'L3_ffn_shared_down_w': _L3_ffn_in['shared_down_w']}

def reference(x, ctx_2048, mask_1xSxS2_ff0, g_xattn, g_ffn, L0_xattn_Wq, L0_xattn_bq, L0_xattn_Wk, L0_xattn_bk, L0_xattn_Wv, L0_xattn_bv, L0_xattn_Wo, L0_xattn_qn_w, L0_xattn_kn_w, L0_ffn_gate_weight, L0_ffn_gate_up_proj, L0_ffn_down_proj, L0_ffn_similarity, L1_xattn_Wh, L1_xattn_wg_w, L1_xattn_wo_w, L1_xattn_gn_gamma, L1_xattn_gn_beta, L1_ffn_gate_w, L1_ffn_up_w, L1_ffn_down_w, L1_ffn_gate_s, L1_ffn_up_s, L1_ffn_down_s, L2_xattn_Wq, L2_xattn_bq, L2_xattn_Wkv, L2_xattn_bkv, L2_xattn_Wp, L2_xattn_bp, L2_ffn_gate_w, L2_ffn_w_gate, L2_ffn_w_up, L2_ffn_w_down, L2_ffn_sw_gate, L2_ffn_sw_up, L2_ffn_sw_down, L3_xattn_ln_w, L3_xattn_ln_b, L3_xattn_wq, L3_xattn_wq_scale, L3_xattn_q_in_scale, L3_xattn_wqx, L3_xattn_wqx_scale, L3_xattn_qx_in_scale, L3_xattn_wk, L3_xattn_wk_scale, L3_xattn_k_in_scale, L3_xattn_wv, L3_xattn_wv_scale, L3_xattn_v_in_scale, L3_xattn_w_kv_x, L3_xattn_qln_w, L3_xattn_qln_b, L3_xattn_kln_w, L3_xattn_kln_b, L3_xattn_qxln_w, L3_xattn_qxln_b, L3_xattn_kxln_w, L3_xattn_kxln_b, L3_xattn_wproj, L3_xattn_proj_w_scale, L3_xattn_proj_in_scale, L3_xattn_proj_smooth, L3_ffn_router_w, L3_ffn_gate_up_proj, L3_ffn_down_proj, L3_ffn_shared_gate_w, L3_ffn_shared_up_w, L3_ffn_shared_down_w):
    import jax
    import jax.numpy as jnp

    def _L0_xattn_ref(hidden_states, encoder_hidden_states, attention_mask, Wq, bq, Wk, bk, Wv, bv, Wo, qn_w, kn_w):
        import jax, jax.numpy as jnp
        import numpy as np
        H = 256
        NH = 16
        NKV = 4
        HD = 128
        GROUPS = NH // NKV
        EPS = 1e-06
        B, S, SE = (1, 256, 512)

        def _rmsnorm(x, w, eps=EPS):
            xf = x.astype(jnp.float32)
            var = jnp.mean(xf * xf, axis=-1, keepdims=True)
            return (xf * jax.lax.rsqrt(var + eps)).astype(x.dtype) * w
        b, s, _ = hidden_states.shape
        se = encoder_hidden_states.shape[1]
        q = (hidden_states @ Wq + bq).reshape(b, s, NH, HD).transpose(0, 2, 1, 3)
        k = (encoder_hidden_states @ Wk + bk).reshape(b, se, NKV, HD).transpose(0, 2, 1, 3)
        v = (encoder_hidden_states @ Wv + bv).reshape(b, se, NKV, HD).transpose(0, 2, 1, 3)
        k = jnp.repeat(k, GROUPS, axis=1)
        v = jnp.repeat(v, GROUPS, axis=1)
        q = _rmsnorm(q, qn_w)
        k = _rmsnorm(k, kn_w)
        scale = 1.0 / np.sqrt(HD).astype(np.float32)
        scores = jnp.einsum('bhsd,bhed->bhse', q, k) * scale
        scores = scores + attention_mask[:, None, :, :]
        probs = jax.nn.softmax(scores.astype(jnp.float32), axis=-1).astype(q.dtype)
        out = jnp.einsum('bhse,bhed->bhsd', probs, v)
        out = out.transpose(0, 2, 1, 3).reshape(b, s, NH * HD)
        return out @ Wo

    def _L0_ffn_ref(hidden_states, gate_weight, gate_up_proj, down_proj, similarity):
        import jax, jax.numpy as jnp
        import numpy as np
        NUM_EXPERTS = 32
        TOP_K = 8
        SELECT_TOP_K = 4
        THRESHOLD = 0.5
        HIDDEN = 256
        D_FF = 96

        def _moe_forward(hidden_states, gate_weight, gate_up_proj, down_proj, similarity):
            B, S_len, H = hidden_states.shape
            E, K, Ssel = (NUM_EXPERTS, TOP_K, SELECT_TOP_K)
            x = hidden_states.reshape(-1, H)
            router_logits = x @ gate_weight.T
            router_probs = jax.nn.softmax(router_logits.astype(jnp.float32), axis=-1).astype(router_logits.dtype)
            router_top_value, router_indices = jax.lax.top_k(router_probs, K)
            routing_weights = router_top_value / jnp.clip(jnp.sum(router_top_value, axis=-1, keepdims=True), 1e-12, None)
            sim = similarity.astype(jnp.float32)
            sim = sim.at[jnp.arange(E), jnp.arange(E)].set(1.0)
            prim = router_indices[:, :Ssel]
            sec = router_indices[:, Ssel:]
            sim_cand = sim[sec[:, :, None], prim[:, None, :]]
            best_sim = jnp.max(sim_cand, axis=-1)
            best_i = jnp.argmax(sim_cand, axis=-1)
            prim_rep = jnp.broadcast_to(prim[:, None, :], sim_cand.shape)
            best_primary = jnp.take_along_axis(prim_rep, best_i[..., None], axis=-1)[..., 0]
            new_sec = jnp.where(best_sim < THRESHOLD, sec, best_primary) if THRESHOLD > 0.0 else best_primary
            rerouted_indices = jnp.concatenate([prim, new_sec], axis=1)
            combine = jnp.sum(jax.nn.one_hot(rerouted_indices, E, dtype=routing_weights.dtype) * routing_weights[..., None], axis=1)

            def expert_step(y, params):
                wgu, wd, cw = params
                gu = x @ wgu.T
                g, u = jnp.split(gu, 2, axis=-1)
                h = jax.nn.silu(g) * u
                y = y + h @ wd.T * cw[:, None]
                return (y, None)
            y0 = jnp.zeros_like(x)
            y, _ = jax.lax.scan(expert_step, y0, (gate_up_proj, down_proj, combine.T))
            return y.reshape(B, S_len, H)
        return _moe_forward(hidden_states, gate_weight, gate_up_proj, down_proj, similarity)

    def _L1_xattn_ref(x, k, v, Wh, wg_w, wo_w, gn_gamma, gn_beta):
        import jax, jax.numpy as jnp
        import numpy as np
        B, S, DIM, HD = (4, 128, 256, 128)
        H = DIM // HD
        GN_EPS = 0.001

        def _decay_masks(n_heads, seq_len):
            gam = 1.0 - 2.0 ** (-5.0 - jnp.arange(n_heads, dtype=jnp.float32))
            idx = jnp.arange(seq_len, dtype=jnp.float32)
            expo = idx[None, :] - idx[:, None]
            D = jnp.where(expo[None, :, :] <= 0, gam[:, None, None] ** expo[None, :, :], 0.0)
            return D / jnp.sqrt(D.sum(axis=-1))[:, None, :]
        b, s, dim = x.shape
        h, hd, _ = Wh.shape
        xh = x.reshape(b, s, h, hd)
        kh = k.reshape(b, s, h, hd)
        vh = v.reshape(b, s, h, hd)
        Q = jnp.einsum('bshd,hde->bshe', xh, Wh)
        K = jnp.einsum('bshd,hde->bshe', kh, Wh)
        V = jnp.einsum('bshd,hde->bshe', vh, Wh)
        scores = jnp.einsum('bshe,bthe->bhst', Q, K) / jnp.sqrt(jnp.float32(hd))
        Dn = _decay_masks(h, s)
        masked = scores * Dn[None, :, :, :]
        A = jnp.maximum(jnp.abs(masked.sum(axis=0)), 1.0)
        O = jnp.einsum('hst,bthe->bshe', A, V).reshape(b, s, dim)
        mu = O.mean(axis=-1, keepdims=True)
        var = O.var(axis=-1, keepdims=True)
        Y = (O - mu) / jnp.sqrt(var + GN_EPS) * gn_gamma + gn_beta
        W = jax.nn.relu(x @ wg_w)
        return W * Y @ wo_w

    def _L1_ffn_ref(x, gate_w, up_w, down_w, gate_s, up_s, down_s):
        import jax, jax.numpy as jnp
        import numpy as np
        HIDDEN = 256
        INTER = 704
        B, S = (2, 256)

        def _ternary(key, shape):
            return jax.random.randint(key, shape, -1, 2).astype(jnp.float32)
        b, s, h = x.shape
        xf = x.reshape(b * s, h)
        g = jnp.einsum('th,ih->ti', xf, gate_w) * gate_s
        u = jnp.einsum('th,ih->ti', xf, up_w) * up_s
        hdn = jax.nn.silu(g) * u
        out = jnp.einsum('ti,hi->th', hdn, down_w) * down_s
        return out.reshape(b, s, -1)

    def _L2_xattn_ref(x, cond, Wq, bq, Wkv, bkv, Wp, bp):
        import jax, jax.numpy as jnp
        import numpy as np
        D_MODEL = 256
        NUM_HEADS = 16
        HEAD_DIM = D_MODEL // NUM_HEADS

        def _fq_sym(x, axis):
            s = jnp.max(jnp.abs(x), axis=axis, keepdims=True) / 127.0
            s = jnp.maximum(s, 1e-08)
            q = jnp.clip(jnp.round(x / s), -127.0, 127.0) * s
            return x + jax.lax.stop_gradient(q - x)

        def _fq_unsigned(x, axis):
            s = jnp.max(x, axis=axis, keepdims=True) / 255.0
            s = jnp.maximum(s, 1e-08)
            q = jnp.clip(jnp.round(x / s), 0.0, 255.0) * s
            return x + jax.lax.stop_gradient(q - x)
        B, N, C = x.shape
        H, hd = (NUM_HEADS, HEAD_DIM)
        q = (x @ Wq + bq).reshape(1, B * N, H, hd)
        kv = (cond @ Wkv + bkv).reshape(1, -1, 2, H, hd)
        k, v = (kv[:, :, 0], kv[:, :, 1])
        scale = 1.0 / np.sqrt(hd).astype(np.float32)
        q = jnp.transpose(q * scale, (0, 2, 1, 3))
        k = jnp.transpose(k, (0, 2, 1, 3))
        v = jnp.transpose(v, (0, 2, 1, 3))
        q = _fq_sym(q, axis=-1)
        k = _fq_sym(k, axis=-1)
        v = _fq_sym(v, axis=2)
        attn = jnp.einsum('bhqd,bhkd->bhqk', q, k)
        attn = jax.nn.softmax(attn.astype(jnp.float32), axis=-1)
        attn = _fq_unsigned(attn, axis=-1)
        out = jnp.einsum('bhqk,bhkd->bhqd', attn, v)
        out = jnp.transpose(out, (0, 2, 1, 3)).reshape(B, N, C)
        return out @ Wp + bp

    def _L2_ffn_ref(hidden_states, gate_w, w_gate, w_up, w_down, sw_gate, sw_up, sw_down):
        import jax, jax.numpy as jnp
        import numpy as np
        B, S, H = (1, 256, 256)
        E, K, I = (16, 4, 176)
        IS = 352
        CAP = 128
        b, s, h = hidden_states.shape
        x = hidden_states.reshape(-1, h)
        T = x.shape[0]
        scores = jax.nn.softmax(x @ gate_w.T, axis=-1)
        topk_w, topk_i = jax.lax.top_k(scores, K)
        topk_w = topk_w / (topk_w.sum(-1, keepdims=True) + 1e-20)
        flat_i = topk_i.reshape(-1)
        flat_w = topk_w.reshape(-1)
        order = jnp.argsort(flat_i)
        se = flat_i[order]
        counts = jax.ops.segment_sum(jnp.ones_like(flat_i), flat_i, num_segments=E)
        starts = jnp.cumsum(counts) - counts
        rank = jnp.arange(T * K) - starts[se]
        tok = order // K
        slot = jnp.where(rank < CAP, rank, CAP)
        buf = jnp.full((E, CAP + 1), T, dtype=jnp.int32).at[se, slot].set(tok)[:, :CAP]
        wbuf = jnp.zeros((E, CAP + 1), x.dtype).at[se, slot].set(flat_w[order])[:, :CAP]
        xpad = jnp.concatenate([x, jnp.zeros((1, h), x.dtype)], axis=0)
        xg = xpad[buf]
        gact = jax.nn.silu(jnp.einsum('ech,ehi->eci', xg, w_gate))
        mid = gact * jnp.einsum('ech,ehi->eci', xg, w_up)
        eout = jnp.einsum('eci,eih->ech', mid, w_down) * wbuf[..., None]
        y = jnp.zeros((T + 1, h), x.dtype).at[buf.reshape(-1)].add(eout.reshape(-1, h))[:T]
        shared = jax.nn.silu(x @ sw_gate) * (x @ sw_up) @ sw_down
        return (y + shared).reshape(b, s, h)

    def _L3_xattn_ref(hidden_states, cond, ln_w, ln_b, wq, wq_scale, q_in_scale, wqx, wqx_scale, qx_in_scale, wk, wk_scale, k_in_scale, wv, wv_scale, v_in_scale, w_kv_x, qln_w, qln_b, kln_w, kln_b, qxln_w, qxln_b, kxln_w, kxln_b, wproj, proj_w_scale, proj_in_scale, proj_smooth):
        import jax, jax.numpy as jnp
        import numpy as np
        FP8_MAX = 448.0
        EPS = 1e-05

        def _fp8_roundtrip(x):
            return x.astype(jnp.float8_e4m3fn).astype(jnp.float32)

        def _div_clamp_fp8(x, scale):
            y = jnp.clip(x.astype(jnp.float32) / scale, -FP8_MAX, FP8_MAX)
            y = y.astype(jnp.bfloat16).astype(jnp.float32)
            return _fp8_roundtrip(y)

        def _ln(x, w, b):
            mu = jnp.mean(x, axis=-1, keepdims=True)
            var = jnp.mean(jnp.square(x - mu), axis=-1, keepdims=True)
            return (x - mu) * jax.lax.rsqrt(var + EPS) * w + b

        def _fp8_linear_pertensor(x, wq, w_scale, in_scale):
            xq = _div_clamp_fp8(x, in_scale)
            return jnp.einsum('bsi,oi->bso', xq * in_scale, wq) * w_scale

        def _gqa(q, k, v):
            scale = 1.0 / np.sqrt(q.shape[-1])
            scores = jnp.einsum('bsghd,btgd->bghst', q, k) * scale
            p = jax.nn.softmax(scores, axis=-1)
            return jnp.einsum('bghst,btgd->bsghd', p, v)
        b, s, _ = hidden_states.shape
        sc = cond.shape[1]
        d = qln_w.shape[0]
        nh = wq.shape[0] // d
        g = wk.shape[0] // d
        hpg = nh // g
        ln_out = _ln(hidden_states, ln_w, ln_b)
        q = _fp8_linear_pertensor(ln_out, wq, wq_scale, q_in_scale).reshape(b, s, g, hpg, d)
        q = _ln(q, qln_w, qln_b)
        k = _fp8_linear_pertensor(ln_out, wk, wk_scale, k_in_scale).reshape(b, s, g, d)
        k = _ln(k, kln_w, kln_b)
        v = _fp8_linear_pertensor(ln_out, wv, wv_scale, v_in_scale).reshape(b, s, g, d)
        core = _gqa(q, k, v).reshape(b, s, nh * d)
        qx = _fp8_linear_pertensor(ln_out, wqx, wqx_scale, qx_in_scale).reshape(b, s, g, hpg, d)
        qx = _ln(qx, qxln_w, qxln_b)
        kvx = jnp.einsum('bsi,oi->bso', cond, w_kv_x)
        kx, vx = jnp.split(kvx, 2, axis=-1)
        kx = _ln(kx.reshape(b, sc, g, d), kxln_w, kxln_b)
        vx = vx.reshape(b, sc, g, d)
        xout = _gqa(qx, kx, vx).reshape(b, s, nh * d)
        cat = jnp.concatenate([core, xout], axis=-1)
        catq = _div_clamp_fp8(cat, proj_smooth)
        return jnp.einsum('bsi,oi->bso', catq, wproj) * (proj_in_scale * proj_w_scale)

    def _L3_ffn_ref(hidden_states, router_w, gate_up_proj, down_proj, shared_gate_w, shared_up_w, shared_down_w):
        import jax, jax.numpy as jnp
        import numpy as np
        E, H, I = (8, 256, 512)
        TOP_K = 1
        B, S = (1, 256)
        orig_shape = hidden_states.shape
        x = hidden_states.reshape(-1, H)
        T = x.shape[0]
        logits = x @ router_w.T
        top_vals, top_idx = jax.lax.top_k(logits, TOP_K)
        scores = jnp.full_like(logits, -jnp.inf)
        scores = scores.at[jnp.arange(T)[:, None], top_idx].set(top_vals)
        scores = jax.nn.sigmoid(scores.astype(jnp.float32)).astype(logits.dtype)
        xr = x[None, :, :] * scores.T[:, :, None]
        gate_up = jnp.einsum('eth,ehf->etf', xr, gate_up_proj)
        gate, up = jnp.split(gate_up, 2, axis=-1)
        routed = jnp.einsum('etf,efh->eth', up * jax.nn.silu(gate), down_proj)
        routed_sum = routed.sum(axis=0)
        shared = jax.nn.silu(x @ shared_gate_w) * (x @ shared_up_w) @ shared_down_w
        return (shared + routed_sum).reshape(orig_shape)
    x = x + jnp.tanh(g_xattn[0]) * _L0_xattn_ref(_layernorm(x, axis=-1), ctx_2048, mask_1xSxS2_ff0, L0_xattn_Wq, L0_xattn_bq, L0_xattn_Wk, L0_xattn_bk, L0_xattn_Wv, L0_xattn_bv, L0_xattn_Wo, L0_xattn_qn_w, L0_xattn_kn_w)
    x = x + jnp.tanh(g_ffn[0]) * _L0_ffn_ref(_layernorm(x, axis=-1), L0_ffn_gate_weight, L0_ffn_gate_up_proj, L0_ffn_down_proj, L0_ffn_similarity)
    x = x + jnp.tanh(g_xattn[1]) * _L1_xattn_ref(_layernorm(x, axis=-1), ctx_2048, ctx_2048, L1_xattn_Wh, L1_xattn_wg_w, L1_xattn_wo_w, L1_xattn_gn_gamma, L1_xattn_gn_beta)
    x = x + jnp.tanh(g_ffn[1]) * _L1_ffn_ref(_layernorm(x, axis=-1), L1_ffn_gate_w, L1_ffn_up_w, L1_ffn_down_w, L1_ffn_gate_s, L1_ffn_up_s, L1_ffn_down_s)
    x = x + jnp.tanh(g_xattn[2]) * _L2_xattn_ref(_layernorm(x, axis=-1), ctx_2048, L2_xattn_Wq, L2_xattn_bq, L2_xattn_Wkv, L2_xattn_bkv, L2_xattn_Wp, L2_xattn_bp)
    x = x + jnp.tanh(g_ffn[2]) * _L2_ffn_ref(_layernorm(x, axis=-1), L2_ffn_gate_w, L2_ffn_w_gate, L2_ffn_w_up, L2_ffn_w_down, L2_ffn_sw_gate, L2_ffn_sw_up, L2_ffn_sw_down)
    x = x + jnp.tanh(g_xattn[3]) * _L3_xattn_ref(_layernorm(x, axis=-1), ctx_2048, L3_xattn_ln_w, L3_xattn_ln_b, L3_xattn_wq, L3_xattn_wq_scale, L3_xattn_q_in_scale, L3_xattn_wqx, L3_xattn_wqx_scale, L3_xattn_qx_in_scale, L3_xattn_wk, L3_xattn_wk_scale, L3_xattn_k_in_scale, L3_xattn_wv, L3_xattn_wv_scale, L3_xattn_v_in_scale, L3_xattn_w_kv_x, L3_xattn_qln_w, L3_xattn_qln_b, L3_xattn_kln_w, L3_xattn_kln_b, L3_xattn_qxln_w, L3_xattn_qxln_b, L3_xattn_kxln_w, L3_xattn_kxln_b, L3_xattn_wproj, L3_xattn_proj_w_scale, L3_xattn_proj_in_scale, L3_xattn_proj_smooth)
    x = x + jnp.tanh(g_ffn[3]) * _L3_ffn_ref(_layernorm(x, axis=-1), L3_ffn_router_w, L3_ffn_gate_up_proj, L3_ffn_down_proj, L3_ffn_shared_gate_w, L3_ffn_shared_up_w, L3_ffn_shared_down_w)
    return x

_drawn_inputs = setup_inputs


def setup_inputs(seed=0):
    import zlib

    import numpy as np

    out = dict(_drawn_inputs(seed))
    spreads = {'L0_xattn_qn_w': (1.0, 0.6),
     'L0_xattn_kn_w': (1.0, 0.6),
     'L1_xattn_gn_gamma': (1.0, 0.2),
     'L1_xattn_gn_beta': (0.0, 0.1),
     'L2_xattn_bq': (0.0, 0.8),
     'L2_xattn_bkv': (0.0, 0.392),
     'L2_xattn_bp': (0.0, 0.1),
     'L3_xattn_ln_w': (1.0, 0.6),
     'L3_xattn_ln_b': (0.0, 0.42),
     'L3_xattn_q_in_scale': (0.05000000074505806, 0.6),
     'L3_xattn_qx_in_scale': (0.05000000074505806, 0.6),
     'L3_xattn_k_in_scale': (0.05000000074505806, 0.6),
     'L3_xattn_v_in_scale': (0.05000000074505806, 0.6),
     'L3_xattn_qln_w': (1.0, 0.6),
     'L3_xattn_qln_b': (0.0, 0.8),
     'L3_xattn_kln_w': (1.0, 0.6),
     'L3_xattn_kln_b': (0.0, 2.0),
     'L3_xattn_qxln_w': (1.0, 0.6),
     'L3_xattn_qxln_b': (0.0, 0.8),
     'L3_xattn_kxln_w': (1.0, 0.6),
     'L3_xattn_kxln_b': (0.0, 2.0),
     'L3_xattn_proj_smooth': (0.05000000074505806, 0.6)}
    factors = {'g_ffn': 31.504,
     'L0_xattn_bq': 8.0,
     'L0_xattn_bk': 8.0,
     'L0_xattn_bv': 3.88,
     'L0_ffn_gate_weight': 8.0,
     'L0_ffn_gate_up_proj': 8.0,
     'L0_ffn_down_proj': 8.0,
     'L0_ffn_similarity': 8.0,
     'L2_xattn_Wq': 8.0,
     'L2_xattn_Wkv': 6.843,
     'L2_ffn_gate_w': 8.0,
     'L2_ffn_w_gate': 8.0,
     'L2_ffn_w_up': 8.0,
     'L2_ffn_w_down': 8.0,
     'L2_ffn_sw_gate': 4.887,
     'L2_ffn_sw_up': 4.841,
     'L2_ffn_sw_down': 4.838,
     'L3_ffn_router_w': 8.0,
     'L3_ffn_gate_up_proj': 8.0,
     'L3_ffn_down_proj': 8.0,
     'L3_ffn_shared_gate_w': 3.674,
     'L3_ffn_shared_up_w': 3.655,
     'L3_ffn_shared_down_w': 3.631}
    for name, (base, spread) in spreads.items():
        noise = np.random.default_rng([zlib.crc32(name.encode()), seed]).standard_normal(out[name].shape)
        drawn = base * np.exp(spread * noise) if base else spread * noise
        out[name] = jnp.asarray(drawn.astype(out[name].dtype))
    for name, factor in factors.items():
        out[name] = (out[name] * factor).astype(out[name].dtype)
    return out
```

```python
from contextlib import ExitStack, contextmanager

import numpy as np

import concourse.bass as bass
from concourse import mybir

F32 = mybir.dt.float32
BF16 = mybir.dt.bfloat16
U16 = mybir.dt.uint16
U32 = mybir.dt.uint32
ALU = mybir.AluOpType
ACT = mybir.ActivationFunctionType
X, XY = mybir.AxisListType.X, mybir.AxisListType.XY

P = 128
BATCH, SEQ, HID = 16, 64, 256
TOK = BATCH * SEQ
NT = TOK // P
KC = HID // P
HD = 128
NH = 16
HALF = TOK // 2
ROUND = 1.5 * 2.0 ** 23
FP8_LEAST = 1.5 * 2.0 ** -6
FP8_STEP = 2.0 ** 20


class Chain:

    def __init__(self, eng, sem, base=0):
        self.eng, self.sem, self.base, self.n = eng, sem, base, 0

    def add(self, ins):
        self.n += 1
        ins.then_inc(self.sem, 1)

    def join(self):
        self.eng.wait_ge(self.sem, self.base + self.n)

    def after(self, ins):
        self.add(ins)
        self.join()


class Core:

    def __init__(self, nc, ctx, dram):
        self.nc, self.dram, self.count = nc, dram, 0
        self.live = ctx
        self.psum = ctx.enter_context(nc.psum_tensor("psum", [P, 8, 512], F32))
        self.resid = self.sb(ctx, "resid", [P, NT, HID])
        self.norm = self.sb(ctx, "norm", [P, NT, HID])
        self.xT = self.sb(ctx, "xT", [P, KC, TOK])
        self.ctxT = self.sb(ctx, "ctxT", [P, KC, TOK])
        self.ident = self.sb(ctx, "ident", [P, P])
        self.identb = self.sb(ctx, "identb", [P, P], BF16)
        self.gate = self.sb(ctx, "gate", [P, 8])
        self.stats = self.sb(ctx, "stats", [P, NT, 6])
        self.mv = self.sb(ctx, "mv", [P, NT, 2])
        self.ve = self.sb(ctx, "ve", [P, NT])
        self.rstd = self.sb(ctx, "rstd", [P, NT])
        self.mhalf = self.sb(ctx, "mhalf", [P, 64])

    def sb(self, ctx, name, shape, dt=F32):
        self.count += 1
        return ctx.enter_context(self.nc.sbuf_tensor(f"{name}_{self.count}", shape, dt))

    def sem(self, ctx, name):
        self.count += 1
        s = self.stage.enter_context(self.nc.semaphore(f"{name}_{self.count}"))
        self.used.append(s)
        return s

    @contextmanager
    def new_stage(self):
        with ExitStack() as self.stage:
            self.used = []
            yield
            with self.nc.Block() as block:
                @block.gpsimd
                def _(pool):
                    nums = [s.num for s in self.used]
                    pool.sem_clear(range(min(nums), max(nums) + 1))


def bc(ap, shape):
    return ap.unsqueeze(len(ap.shape)).to_broadcast(shape)



def start(c):
    nc, d = c.nc, c.dram
    with ExitStack() as st:
        x_in, ctx_in, gates_in, ident_set, ident_ready, gates_ready, consts = (c.sem(st, n) for n in (
            "x_in", "ctx_in", "gates_in", "ident_set", "ident_ready", "gates_ready", "consts"))
        raw = c.sb(st, "gate_raw", [P, 8])
        with nc.Block() as block:
            @block.sync
            def _(sp):
                sp.dma_start(c.norm[:], d["ctx_2048"].rearrange("(t p) d -> p t d", p=P)).then_inc(ctx_in, 16)
                sp.dma_start(c.resid[:], d["x"].rearrange("(t p) d -> p t d", p=P)).then_inc(x_in, 16)
                sp.wait_ge(x_in, 16)

            @block.scalar
            def _(act):
                act.dma_start(raw[:, 0:4], d["g_xattn"].partition_broadcast(P)).then_inc(gates_in, 16)
                act.dma_start(raw[:, 4:8], d["g_ffn"].partition_broadcast(P)).then_inc(gates_in, 16)
                act.wait_ge(gates_in, 32)
                nc.scalar.activation(c.gate[:], raw[:], ACT.Tanh).then_inc(gates_ready, 1)
                act.wait_ge(ctx_in, 16)

            @block.vector
            def _(dve):
                nc.vector.memset(c.mhalf[:], -0.5).then_inc(consts, 1)

            @block.gpsimd
            def _(pool):
                nc.gpsimd.memset(c.ident[:], 0.0).then_inc(ident_set, 1)
                pool.wait_ge(ident_set, 1)
                nc.gpsimd.affine_select(out=c.ident[:], in_=c.ident[:], compare_op=ALU.not_equal, fill=1.0, base=0,
                                        pattern=[[-1, P]], channel_multiplier=1).then_inc(ident_set, 1)
                pool.wait_ge(ident_set, 2)
                nc.gpsimd.tensor_copy(c.identb[:], c.ident[:]).then_inc(ident_ready, 1)
        transpose_tokens(c, c.norm, c.ctxT)


def finish(c, out):
    nc = c.nc
    with ExitStack() as st:
        stored = c.sem(st, "stored")
        with nc.Block() as block:
            @block.sync
            def _(sp):
                sp.dma_start(out.rearrange("(t p) d -> p t d", p=P), c.resid[:]).then_inc(stored, 16)
                sp.wait_ge(stored, 16)



def pe_transpose_tokens(c, pe, src, ready, transposed):
    for t in range(NT):
        if ready is not None:
            pe.wait_ge(ready, t + 1)
        for k in range(KC):
            last = c.nc.tensor.transpose(c.psum[:, t // 2, k * 256 + t % 2 * P:k * 256 + t % 2 * P + P],
                                         src[:, t, k * P:(k + 1) * P], c.ident[:])
        last.then_inc(transposed, 1)


def act_store_transposed(c, act, dst, transposed, stored):
    for g in range(NT // 2):
        act.wait_ge(transposed, 2 * g + 2)
        c.nc.scalar.activation(dst[:, :, g * 256:(g + 1) * 256],
                               c.psum[:, g, :].rearrange("p (k n) -> p k n", k=KC), ACT.Copy).then_inc(stored, 1)


def transpose_tokens(c, src, dst):
    nc = c.nc
    with ExitStack() as st:
        transposed, stored = c.sem(st, "transposed"), c.sem(st, "stored")
        with nc.Block() as block:
            @block.tensor
            def _(pe):
                pe_transpose_tokens(c, pe, src, None, transposed)

            @block.scalar
            def _(act):
                act_store_transposed(c, act, dst, transposed, stored)


def layernorm(c, src, dst, dstT, eps=1e-5):
    nc = c.nc
    with ExitStack() as st:
        chain_s, var_ready, rstd_ready, norm_ready, transposed, stored = (c.sem(st, n) for n in (
            "ln_chain", "var_ready", "rstd_ready", "norm_ready", "transposed", "stored"))
        with nc.Block() as block:
            @block.vector
            def _(dve):
                chain = Chain(dve, chain_s)
                for t in range(NT):
                    chain.add(nc.vector.bn_stats(c.stats[:, t, :], src[:, t, :]))
                chain.join()
                for t in range(NT):
                    chain.add(nc.vector.bn_aggr(c.mv[:, t, :], c.stats[:, t, :]))
                chain.join()
                nc.vector.tensor_scalar(c.ve[:], c.mv[:, :, 1], eps, None, ALU.add).then_inc(var_ready, 1)
                dve.wait_ge(rstd_ready, 1)
                for t in range(NT):
                    nc.vector.tensor_scalar(dst[:, t, :], src[:, t, :], c.mv[:, t, 0:1], c.rstd[:, t:t + 1],
                                            ALU.subtract, ALU.mult).then_inc(norm_ready, 1)

            @block.gpsimd
            def _(pool):
                pool.wait_ge(var_ready, 1)
                nc.gpsimd.tensor_tensor(c.rstd[:], c.ve[:], c.mhalf[:, 0:NT], ALU.pow).then_inc(rstd_ready, 1)

            if dstT is not None:
                @block.tensor
                def _(pe):
                    pe_transpose_tokens(c, pe, dst, norm_ready, transposed)

                @block.scalar
                def _(act):
                    act_store_transposed(c, act, dstT, transposed, stored)



def ffn(c, name, chunks, f, xT, acc, comb=None, per_expert=1, scaled=False):
    nc, d = c.nc, c.dram
    unroll = max(2, per_expert)
    wdn = HID + (2 if scaled else 0)
    with ExitStack() as st:
        gu_in = [c.sem(st, f"gu_in{b}") for b in range(2)]
        dn_in = [c.sem(st, f"dn_in{b}") for b in range(2)]
        gu_ready, act_ready, h_ready, dn_ready, acc_done = (c.sem(st, n) for n in (
            "gu_ready", "act_ready", "h_ready", "dn_ready", "acc_done"))
        wgu = c.sb(st, "wgu", [P, 2, KC, 2 * f])
        wd = c.sb(st, "wd", [f, 2, wdn])
        sg = c.sb(st, "silu", [f, 2, HALF])
        hT = c.sb(st, "hT", [f, 2, HALF])
        with nc.Block() as block:
            @block.sync
            def _(sp):
                sp.sem_inc(dn_ready, 4)
                with sp.Fori(0, chunks // unroll) as i:
                    for u in range(unroll):
                        j, b = unroll * i + u, u % 2
                        sp.wait_ge(dn_ready, 2 * j + 2)
                        sp.dma_start(wgu[:, b], d[name + "_gu"][bass.ds(j, 1)].rearrange("o p k f -> p (o k) f")
                                     ).then_inc(gu_in[b], 16)
                        sp.dma_start(wd[:, b], d[name + "_dn"][bass.ds(j, 1)].rearrange("o p k -> p (o k)")
                                     ).then_inc(dn_in[b], 16)

            @block.tensor
            def _(pe):
                with pe.Fori(0, chunks // unroll) as i:
                    for c_ in range(unroll):
                        j, b = unroll * i + c_, c_ % 2
                        landed = 16 * (unroll // 2 * i + c_ // 2 + 1)
                        pe.wait_ge(gu_in[b], landed)
                        for half in range(2):
                            pe.wait_ge(h_ready, 2 * j + half + 1)
                            for u in range(2):
                                for k in range(KC):
                                    last = nc.tensor.matmul(c.psum[0:f, 2 * half + u, :],
                                                            wgu[:, b, k, u * f:(u + 1) * f],
                                                            xT[:, k, half * HALF:(half + 1) * HALF],
                                                            start=k == 0, stop=k == KC - 1)
                            last.then_inc(gu_ready, 1)
                        pe.wait_ge(dn_in[b], landed)
                        for half in range(2):
                            pe.wait_ge(h_ready, 2 * j + half + 3)
                            pe.wait_ge(acc_done, 2 * j + half + 1)
                            for q in range(4):
                                last = nc.tensor.matmul(c.psum[:, 4 + 2 * half + q // 2,
                                                               q % 2 * HID:(q % 2 + 1) * HID],
                                                        hT[:, half, q * P:(q + 1) * P], wd[:, b, 0:HID],
                                                        start=True, stop=True)
                            last.then_inc(dn_ready, 1)

            @block.scalar
            def _(act):
                with act.Fori(0, chunks // unroll) as i:
                    for u in range(unroll):
                        j, b = unroll * i + u, u % 2
                        if scaled:
                            act.wait_ge(dn_in[b], 16 * (unroll // 2 * i + u // 2 + 1))
                        for half in range(2):
                            act.wait_ge(gu_ready, 2 * j + half + 1)
                            act.wait_ge(h_ready, 2 * j + half + 1)
                            scale = wd[:, b, HID:HID + 1] if scaled else 1.0
                            nc.scalar.activation(sg[:, half], c.psum[0:f, 2 * half, :], ACT.Silu,
                                                 scale=scale).then_inc(act_ready, 1)

            @block.vector
            def _(dve):
                dve.sem_inc(h_ready, 2)
                dve.sem_inc(acc_done, 2)
                with dve.Fori(0, chunks // unroll) as i:
                    for u in range(unroll):
                        j, b = unroll * i + u, u % 2
                        for half in range(2):
                            dve.wait_ge(act_ready, 2 * j + half + 1)
                            dve.wait_ge(dn_ready, 2 * j + 4)
                            if scaled:
                                ins = nc.vector.scalar_tensor_tensor(
                                    out=hT[:, half], in0=c.psum[0:f, 2 * half + 1, :],
                                    scalar=wd[:, b, HID + 1:HID + 2], in1=sg[:, half], op0=ALU.mult, op1=ALU.mult)
                            else:
                                ins = nc.vector.tensor_tensor(hT[:, half], c.psum[0:f, 2 * half + 1, :], sg[:, half],
                                                              ALU.mult)
                            ins.then_inc(h_ready, 1)
                        for half in range(2):
                            dve.wait_ge(dn_ready, 2 * j + half + 5)
                            dve.wait_ge(acc_done, 2 * j + half + 1)
                            for q in range(4):
                                t = 4 * half + q
                                dn = c.psum[:, 4 + 2 * half + q // 2, q % 2 * HID:(q % 2 + 1) * HID]
                                if comb is None:
                                    if q % 2:
                                        continue
                                    dn = c.psum[:, 4 + 2 * half + q // 2, :].rearrange("p (t n) -> p t n", t=2)
                                    last = nc.vector.tensor_tensor(acc[:, t:t + 2, :], dn, acc[:, t:t + 2, :], ALU.add)
                                else:
                                    e = j if per_expert == 1 else i
                                    last = nc.vector.scalar_tensor_tensor(
                                        out=acc[:, t, :], in0=dn, scalar=comb[:, t, bass.ds(e, 1)],
                                        in1=acc[:, t, :], op0=ALU.mult, op1=ALU.add)
                            last.then_inc(acc_done, 1)


def zero(c, *bufs):
    nc = c.nc
    with ExitStack() as st:
        cleared = c.sem(st, "cleared")
        with nc.Block() as block:
            @block.gpsimd
            def _(pool):
                for b in bufs:
                    nc.gpsimd.memset(b[:], 0.0).then_inc(cleared, 1)


def add_gated(c, acc, gate, col_scale=None):
    nc = c.nc
    with ExitStack() as st:
        scaled_s, added = c.sem(st, "scaled"), c.sem(st, "added")
        with nc.Block() as block:
            @block.vector
            def _(dve):
                if col_scale is not None:
                    nc.vector.tensor_tensor(acc[:], acc[:], col_scale[:].unsqueeze(1).to_broadcast([P, NT, HID]),
                                            ALU.mult).then_inc(scaled_s, 1)
                    dve.wait_ge(scaled_s, 1)
                nc.vector.scalar_tensor_tensor(out=c.resid[:], in0=acc[:], scalar=c.gate[:, gate:gate + 1],
                                               in1=c.resid[:], op0=ALU.mult, op1=ALU.add).then_inc(added, 1)



def softmax_rows(c, dve, chain, logits, p, small, exp_go, exp_done, n, turn=1):
    v = c.nc.vector
    chain.after(v.tensor_reduce(small[:, 0, :], logits, X, ALU.max))
    v.tensor_tensor(p[:], logits, bc(small[:, 0, :], [P, NT, n]), ALU.subtract).then_inc(exp_go, 1)
    dve.wait_ge(exp_done, turn)
    chain.after(v.tensor_reduce(small[:, 0, :], p[:], X, ALU.add))
    chain.after(v.reciprocal(small[:, 1, :], small[:, 0, :]))
    chain.after(v.tensor_tensor(p[:], p[:], bc(small[:, 1, :], [P, NT, n]), ALU.mult))


def top_onehots(c, chain, values, top, idx, idxf, iota, onehot, k, n):
    v = c.nc.vector
    for t in range(NT):
        chain.add(v.max(top[:, t, :], values[:, t, :]))
    chain.join()
    for t in range(NT):
        chain.add(v.max_index(idx[:, t, :], top[:, t, :], values[:, t, :]))
    chain.join()
    chain.after(v.tensor_copy(idxf[:], idx[:]))
    for i in range(k):
        chain.add(v.tensor_tensor(onehot[:, :, i, :], iota[:].unsqueeze(1).to_broadcast([P, NT, n]),
                                  idxf[:, :, i:i + 1].to_broadcast([P, NT, n]), ALU.is_equal))
    chain.join()


def pe_logits(c, pe, wr, bank, n):
    for t in range(NT):
        for k in range(KC):
            last = c.nc.tensor.matmul(c.psum[:, bank, t * n:(t + 1) * n], c.xT[:, k, t * P:(t + 1) * P],
                                      wr[:, k, :], start=k == 0, stop=k == KC - 1)
    return last


def router0(c, comb):
    nc, d, E, K, S = c.nc, c.dram, 32, 8, 4
    with ExitStack() as st:
        wr_in, sim_in, consts, bd_ready, chain_s, logits_ready, exp_go, exp_done, oh_ready, oh_turned, oh_stored, \
            rows_ready = (c.sem(st, n) for n in (
                "wr_in", "sim_in", "consts", "bd_ready", "chain", "logits_ready", "exp_go", "exp_done", "oh_ready",
                "oh_turned", "oh_stored", "rows_ready"))
        wr = c.sb(st, "wr", [P, KC, E])
        simbd = c.sb(st, "simbd", [P, P])
        iota = c.sb(st, "iota", [P, E])
        p = c.sb(st, "p", [P, NT, E])
        small = c.sb(st, "small", [P, 2, NT])
        top = c.sb(st, "top", [P, NT, K])
        rw = c.sb(st, "rw", [P, NT, K])
        idx = c.sb(st, "idx", [P, NT, K], U32)
        idxf = c.sb(st, "idxf", [P, NT, K])
        oh = c.sb(st, "oh", [P, NT, K, E])
        secT = c.sb(st, "secT", [P, NT, P])
        cand4 = c.sb(st, "cand4", [P, NT, S, E])
        cand = c.sb(st, "cand", [P, NT * S, S])
        best = c.sb(st, "best", [P, NT * S])
        eq = c.sb(st, "eq", [P, NT * S, S])
        seen = c.sb(st, "seen", [P, NT * S])
        moved = c.sb(st, "moved", [P, NT, S])
        coef = c.sb(st, "coef", [P, NT, K])
        add = c.sb(st, "add", [P, NT, S])
        with nc.Block() as block:
            @block.sync
            def _(sp):
                sp.dma_start(wr[:], d["L0_router"]).then_inc(wr_in, 16)
                sp.wait_ge(bd_ready, 1)
                for j in range(S):
                    sp.dma_start(simbd[j * E:(j + 1) * E, j * E:(j + 1) * E],
                                 d["L0_ffn_similarity"]).then_inc(sim_in, 16)

            @block.gpsimd
            def _(pool):
                nc.gpsimd.iota(iota[:], pattern=[[1, E]], base=0, channel_multiplier=0,
                               allow_small_or_imprecise_dtypes=True).then_inc(consts, 1)

            @block.tensor
            def _(pe):
                pe.wait_ge(wr_in, 16)
                pe_logits(c, pe, wr, 0, E).then_inc(logits_ready, 1)
                pe.wait_ge(oh_ready, 1)
                for t in range(NT):
                    last = nc.tensor.transpose(c.psum[:, 1 + t // 4, t % 4 * P:(t % 4 + 1) * P],
                                               oh[:, t, S:K, :], c.ident[:])
                last.then_inc(oh_turned, 1)
                pe.wait_ge(oh_stored, 2)
                pe.wait_ge(sim_in, 16 * S)
                for t in range(NT):
                    last = nc.tensor.matmul(c.psum[:, 3 + t // 4, t % 4 * P:(t % 4 + 1) * P], secT[:, t, :],
                                            simbd[:], start=True, stop=True)
                last.then_inc(rows_ready, 1)

            @block.scalar
            def _(act):
                act.wait_ge(exp_go, 1)
                nc.scalar.activation(p[:], p[:], ACT.Exp).then_inc(exp_done, 1)
                act.wait_ge(oh_turned, 1)
                for h in range(2):
                    nc.scalar.activation(secT[:, 4 * h:4 * h + 4, :],
                                         c.psum[:, 1 + h, :].rearrange("p (t n) -> p t n", t=4),
                                         ACT.Copy).then_inc(oh_stored, 1)

            @block.vector
            def _(dve):
                v, chain = nc.vector, Chain(dve, chain_s)
                v.memset(simbd[:], 0.0).then_inc(bd_ready, 1)
                dve.wait_ge(logits_ready, 1)
                logits = c.psum[:, 0, 0:NT * E].rearrange("p (t e) -> p t e", t=NT)
                softmax_rows(c, dve, chain, logits, p, small, exp_go, exp_done, E)
                dve.wait_ge(consts, 1)
                top_onehots(c, chain, p, top, idx, idxf, iota, oh, K, E)
                v.tensor_reduce(small[:, 0, :], top[:], X, ALU.add).then_inc(oh_ready, 1)
                dve.wait_ge(oh_ready, 1)
                chain.after(v.tensor_scalar(small[:, 0, :], small[:, 0, :], 1e-12, None, ALU.max))
                chain.after(v.reciprocal(small[:, 1, :], small[:, 0, :]))
                chain.after(v.tensor_tensor(rw[:], top[:], bc(small[:, 1, :], [P, NT, K]), ALU.mult))
                dve.wait_ge(rows_ready, 1)
                for i in range(S):
                    for h in range(2):
                        rows = c.psum[:, 3 + h, :].rearrange("p (t j e) -> p t j e", t=4, j=S)
                        chain.add(v.tensor_tensor(
                            cand4[:, 4 * h:4 * h + 4], rows,
                            oh[:, 4 * h:4 * h + 4, i, :].unsqueeze(2).to_broadcast([P, 4, S, E]), ALU.mult))
                    chain.join()
                    chain.after(v.tensor_reduce(cand[:, :, i], cand4[:].rearrange("p t j e -> p (t j) e"), X, ALU.add))
                chain.after(v.tensor_reduce(best[:], cand[:], X, ALU.max))
                chain.after(v.tensor_tensor(eq[:], cand[:], bc(best[:], [P, NT * S, S]), ALU.is_equal))
                chain.after(v.tensor_copy(seen[:], eq[:, :, 0]))
                for i in range(1, S):
                    chain.after(v.scalar_tensor_tensor(out=eq[:, :, i], in0=seen[:], scalar=0.5, in1=eq[:, :, i],
                                                       op0=ALU.is_lt, op1=ALU.mult))
                    chain.after(v.tensor_tensor(seen[:], seen[:], eq[:, :, i], ALU.max))
                best3 = best[:].rearrange("p (t j) -> p t j", j=S)
                chain.after(v.scalar_tensor_tensor(out=coef[:, :, S:K], in0=best3, scalar=0.5, in1=rw[:, :, S:K],
                                                   op0=ALU.is_lt, op1=ALU.mult))
                chain.after(v.tensor_tensor(moved[:], rw[:, :, S:K], coef[:, :, S:K], ALU.subtract))
                eq4 = eq[:].rearrange("p (t j) i -> p t j i", j=S)
                chain.after(v.tensor_tensor(eq4, eq4, bc(moved[:], [P, NT, S, S]), ALU.mult))
                chain.after(v.tensor_reduce(add[:], eq[:].rearrange("p (t j) i -> p t i j", j=S), X, ALU.add))
                chain.after(v.tensor_tensor(coef[:, :, 0:S], rw[:, :, 0:S], add[:], ALU.add))
                for i in range(K):
                    chain.add(v.tensor_tensor(oh[:, :, i, :], oh[:, :, i, :],
                                              coef[:, :, i:i + 1].to_broadcast([P, NT, E]), ALU.mult))
                chain.join()
                chain.after(v.tensor_reduce(comb[:], oh[:].rearrange("p t k e -> p t e k"), X, ALU.add))


def router2(c, comb):
    nc, d, E, K, CAP = c.nc, c.dram, 16, 4, 128
    with ExitStack() as st:
        wr_in, consts, chain_s, logits_ready, exp_go, exp_done, mask_ready, rank_ready = (c.sem(st, n) for n in (
            "wr_in", "consts", "chain", "logits_ready", "exp_go", "exp_done", "mask_ready", "rank_ready"))
        wr = c.sb(st, "wr", [P, KC, E])
        iota = c.sb(st, "iota", [P, E])
        ones = c.sb(st, "ones", [P, P])
        before = c.sb(st, "before", [P, P])
        p = c.sb(st, "p", [P, NT, E])
        small = c.sb(st, "small", [P, 2, NT])
        top = c.sb(st, "top", [P, NT, 8])
        rw = c.sb(st, "rw", [P, NT, K])
        idx = c.sb(st, "idx", [P, NT, 8], U32)
        idxf = c.sb(st, "idxf", [P, NT, 8])
        oh = c.sb(st, "oh", [P, NT, K, E])
        mask = c.sb(st, "mask", [P, NT, E])
        with nc.Block() as block:
            @block.sync
            def _(sp):
                sp.dma_start(wr[:], d["L2_router"]).then_inc(wr_in, 16)

            @block.gpsimd
            def _(pool):
                nc.gpsimd.iota(iota[:], pattern=[[1, E]], base=0, channel_multiplier=0,
                               allow_small_or_imprecise_dtypes=True).then_inc(consts, 1)
                nc.gpsimd.memset(ones[:], 1.0).then_inc(consts, 1)
                nc.gpsimd.memset(before[:], 1.0).then_inc(consts, 1)
                pool.wait_ge(consts, 3)
                nc.gpsimd.affine_select(out=before[:], in_=before[:], compare_op=ALU.is_gt, fill=0.0, base=0,
                                        pattern=[[1, P]], channel_multiplier=-1).then_inc(consts, 1)

            @block.tensor
            def _(pe):
                pe.wait_ge(wr_in, 16)
                pe_logits(c, pe, wr, 0, E).then_inc(logits_ready, 1)
                pe.wait_ge(consts, 4)
                pe.wait_ge(mask_ready, 1)
                for t in range(NT):
                    for s in range(t + 1):
                        last = nc.tensor.matmul(c.psum[:, 1, t * E:(t + 1) * E], before[:] if s == t else ones[:],
                                                mask[:, s, :], start=s == 0, stop=s == t)
                last.then_inc(rank_ready, 1)

            @block.scalar
            def _(act):
                act.wait_ge(exp_go, 1)
                nc.scalar.activation(p[:], p[:], ACT.Exp).then_inc(exp_done, 1)

            @block.vector
            def _(dve):
                v, chain = nc.vector, Chain(dve, chain_s)
                dve.wait_ge(logits_ready, 1)
                logits = c.psum[:, 0, 0:NT * E].rearrange("p (t e) -> p t e", t=NT)
                softmax_rows(c, dve, chain, logits, p, small, exp_go, exp_done, E)
                dve.wait_ge(consts, 4)
                top_onehots(c, chain, p, top, idx, idxf, iota, oh, K, E)
                v.tensor_reduce(mask[:], oh[:].rearrange("p t k e -> p t e k"), X, ALU.add).then_inc(mask_ready, 1)
                chain.after(v.tensor_reduce(small[:, 0, :], top[:, :, 0:K], X, ALU.add))
                chain.after(v.tensor_scalar(small[:, 0, :], small[:, 0, :], 1e-20, None, ALU.add))
                chain.after(v.reciprocal(small[:, 1, :], small[:, 0, :]))
                chain.after(v.tensor_tensor(rw[:], top[:, :, 0:K], bc(small[:, 1, :], [P, NT, K]), ALU.mult))
                dve.wait_ge(mask_ready, 1)
                for i in range(K):
                    chain.add(v.tensor_tensor(oh[:, :, i, :], oh[:, :, i, :],
                                              rw[:, :, i:i + 1].to_broadcast([P, NT, E]), ALU.mult))
                chain.join()
                chain.after(v.tensor_reduce(comb[:], oh[:].rearrange("p t k e -> p t e k"), X, ALU.add))
                dve.wait_ge(rank_ready, 1)
                rank = c.psum[:, 1, 0:NT * E].rearrange("p (t e) -> p t e", t=NT)
                chain.after(v.scalar_tensor_tensor(out=comb[:], in0=rank, scalar=CAP - 0.5, in1=comb[:],
                                                   op0=ALU.is_lt, op1=ALU.mult))


def router3(c, comb, scaledT):
    nc, d, E = c.nc, c.dram, 8
    with ExitStack() as st:
        wr_in, consts, chain_s, logits_ready, top_ready, exp_done, scaled, turned, stored = (c.sem(st, n) for n in (
            "wr_in", "consts", "chain", "logits_ready", "top_ready", "exp_done", "scaled", "turned", "stored"))
        wr = c.sb(st, "wr", [P, KC, E])
        iota = c.sb(st, "iota", [P, E])
        logits = c.sb(st, "logits", [P, NT, E])
        top = c.sb(st, "top", [P, NT, 8])
        idx = c.sb(st, "idx", [P, NT, 8], U32)
        idxf = c.sb(st, "idxf", [P, NT, 8])
        sig = c.sb(st, "sig", [P, 2, NT])
        oh = c.sb(st, "oh", [P, NT, 1, E])
        with nc.Block() as block:
            @block.sync
            def _(sp):
                sp.dma_start(wr[:], d["L3_router"]).then_inc(wr_in, 16)

            @block.gpsimd
            def _(pool):
                nc.gpsimd.iota(iota[:], pattern=[[1, E]], base=0, channel_multiplier=0,
                               allow_small_or_imprecise_dtypes=True).then_inc(consts, 1)

            @block.tensor
            def _(pe):
                pe.wait_ge(wr_in, 16)
                pe_logits(c, pe, wr, 7, E).then_inc(logits_ready, 1)
                pe_transpose_tokens(c, pe, c.norm, scaled, turned)

            @block.scalar
            def _(act):
                act.wait_ge(top_ready, 1)
                nc.scalar.activation(sig[:, 0, :], top[:, :, 0], ACT.Exp, scale=-1.0).then_inc(exp_done, 1)
                act_store_transposed(c, act, scaledT, turned, stored)

            @block.vector
            def _(dve):
                v, chain = nc.vector, Chain(dve, chain_s)
                dve.wait_ge(logits_ready, 1)
                chain.after(v.tensor_copy(logits[:], c.psum[:, 7, 0:NT * E].rearrange("p (t e) -> p t e", t=NT)))
                dve.wait_ge(consts, 1)
                top_onehots(c, chain, logits, top, idx, idxf, iota, oh, 1, E)
                v.tensor_copy(comb[:], oh[:, :, 0, :]).then_inc(top_ready, 1)
                dve.wait_ge(exp_done, 1)
                chain.after(v.tensor_scalar(sig[:, 1, :], sig[:, 0, :], 1.0, None, ALU.add))
                chain.after(v.reciprocal(sig[:, 0, :], sig[:, 1, :]))
                for t in range(NT):
                    v.tensor_scalar(c.norm[:, t, :], c.norm[:, t, :], sig[:, 0, t:t + 1], None,
                                    ALU.mult).then_inc(scaled, 1)



def ffn0(c):
    layernorm(c, c.resid, c.norm, c.xT)
    with ExitStack() as st:
        comb, acc = c.sb(st, "comb", [P, NT, 32]), c.sb(st, "acc", [P, NT, HID])
        zero(c, acc)
        router0(c, comb)
        ffn(c, "L0", 32, 96, c.xT, acc, comb=comb)
        add_gated(c, acc, 4)


def ffn1(c):
    nc = c.nc
    layernorm(c, c.resid, c.norm, c.xT)
    with ExitStack() as st:
        acc, down_s = c.sb(st, "acc", [P, NT, HID]), c.sb(st, "down_s", [P, HID])
        s_in = c.sem(st, "down_s_in")
        with nc.Block() as block:
            @block.sync
            def _(sp):
                sp.dma_start(down_s[:], c.dram["L1_ffn_down_s"].partition_broadcast(P)).then_inc(s_in, 16)
                sp.wait_ge(s_in, 16)
        zero(c, acc)
        ffn(c, "L1", 8, 88, c.xT, acc, scaled=True)
        add_gated(c, acc, 5, down_s)


def ffn2(c):
    layernorm(c, c.resid, c.norm, c.xT)
    with ExitStack() as st:
        comb, acc = c.sb(st, "comb", [P, NT, 16]), c.sb(st, "acc", [P, NT, HID])
        zero(c, acc)
        router2(c, comb)
        ffn(c, "L2", 32, 88, c.xT, acc, comb=comb, per_expert=2)
        ffn(c, "L2s", 4, 88, c.xT, acc)
        add_gated(c, acc, 6)


def ffn3(c):
    layernorm(c, c.resid, c.norm, c.xT)
    with ExitStack() as st:
        comb, acc = c.sb(st, "comb", [P, NT, 8]), c.sb(st, "acc", [P, NT, HID])
        scaledT = c.sb(st, "scaledT", [P, KC, TOK])
        zero(c, acc)
        router3(c, comb, scaledT)
        ffn(c, "L3", 32, 128, scaledT, acc, comb=comb, per_expert=4)
        ffn(c, "L3s", 4, 128, c.xT, acc)
        add_gated(c, acc, 7)



def order(text):
    return [(s.rstrip("0123456789"), int(s[len(s.rstrip("0123456789")):] or 0)) for s in text.split()]


ORDER0 = {
    "pe": order("P0 P1 T0 P2 P3 T2 P4 T3 S0 P5 T4 T5 R0 S1 A0 R1 A1 F"),
    "act": order("N0 T0 N2 T2 N3 T3 N4 X0 N5 T4 T5 R0 X1 O0 R1 O1"),
    "dve": order("E0 V0 E1 E2 V2 E3 V3 E4 V4 M0 E5 V5 Q0 M1 Q1 F"),
    "pool": order("R0 R2 R3 R4 R5"),
}
ORDER3 = {
    "pe": order("P0 P1 T0 P2 T1 P3 P4 P5 T4 P6 T5 S0 P7 T6 P8 T7 R0 S1 P9 T8 A0 P10 T9 R1 P11 A1 P12 P13 T12 P14 "
                "T13 S2 P15 T14 T15 R2 S3 A2 R3 A3 F"),
    "act": order("E0 E1 T0 E2 T1 E3 E4 E5 T4 E6 T5 E7 X0 T6 E8 T7 R0 E9 X1 T8 E10 T9 R1 E11 E12 E13 T12 E14 T13 "
                 "E15 X2 T14 T15 R2 X3 R3"),
    "dve": order("V0 V1 N0 N1 V4 N4 V5 N5 V6 M0 N6 Z V7 N7 Q0 V8 M1 N8 O0 V9 N9 Q1 O1 V12 N12 V13 N13 V14 M2 N14 V15 "
                 "N15 Q2 M3 Q3 O2 O3 F"),
    "pool": order("R0 R1 R4 R5 R6 R7 R8 R9 Z R12 O0 R13 R14 R15 O1 O2 O3"),
}



def heads_attention(c, steps, sources, blocks, units, kv_heads, eps, w_out, out_scale, mask=None, quant=None):
    nc = c.nc
    ps, G = c.psum, kv_heads
    NB, NU = len(blocks), len(units)
    normed = [j for j, b in enumerate(blocks) if b["normed"]]
    NN = len(normed)
    per_kv = NH // G
    scale = HD ** -0.5
    with ExitStack() as st:
        (x_ready, zb_ready, z_ready, proj_ready, evacuated, ve_ready, rstd_ready, norm_ready, turned, stored, scores_ready,
         exp_go, exp_done, probs_ready, pt_turned, pt_stored, o_ready, o_read, yo_ready, a_ready,
         out_ready, resid_done, dve_chain, pool_chain) = (c.sem(st, n) for n in (
             "x_ready", "zb_ready", "z_ready", "proj_ready", "evacuated", "ve_ready", "rstd_ready", "norm_ready", "turned",
             "stored", "scores_ready", "exp_go", "exp_done", "probs_ready", "pt_turned", "pt_stored",
             "o_ready", "o_read", "yo_ready", "a_ready", "out_ready", "resid_done", "dve_chain", "pool_chain"))
        src = {n: c.sb(st, "src", [P, KC, P]) for n in sources} if quant is None else {
            "ctx": c.sb(st, "src", [P, KC, P])}
        if quant is not None:
            xq = c.sb(st, "xq", [P, 4, KC, P])
            xq_next = c.sb(st, "xq_next", [P, 4, KC, P])
            xb = c.sb(st, "xb", [P, 4, KC, P], BF16)
            xbig = c.sb(st, "xbig", [P, 4, KC, P], BF16)
            yo = c.sb(st, "yo", [P, 1024])
            yb = c.sb(st, "yb", [P, 2, 1024], BF16)
            ybig = c.sb(st, "ybig", [P, 2, 1024], BF16)
            ysum = c.sb(st, "ysum", [P, 1024])
            src.update({n: xq[:, s] for s, n in enumerate(("q", "k", "v", "qx"))})
        qs = c.sb(st, "qs", [P, 2, 512])
        st6 = c.sb(st, "st6", [P, 2, 4, 6])
        tmp = c.sb(st, "tmph", [P, 2, 4, 3])
        mean = c.sb(st, "meanh", [P, 2, 4])
        ve = c.sb(st, "veh", [P, 2, 4])
        rstd = c.sb(st, "rstdh", [P, 2, 4])
        probs = c.sb(st, "probs", [P, 2, 512])
        probsT = c.sb(st, "probsT", [P, 2, 512])
        mx = c.sb(st, "mx", [P, 2, 2, 8])
        attnT = c.sb(st, "attnT", [P, NH * NU // 2, P])

        with nc.Block() as block:
            @block.tensor
            def _(pe):
                def project(i, j):
                    b = blocks[j]
                    if j == 0:
                        pe.wait_ge(x_ready, i + 1)
                    pe.wait_ge(evacuated, i * NB + j + 1)
                    for k in range(KC):
                        last = nc.tensor.matmul(ps[:, j % 2, :], src[b["src"]][:, k, :], b["w"][:, k, :],
                                                start=k == 0, stop=k == KC - 1)
                    last.then_inc(proj_ready, 1)

                def turn(i, j):
                    n = normed.index(j)
                    pe.wait_ge(norm_ready, i * NN + n + 1)
                    pe.wait_ge(stored, i * NN + n + 1 + (n == 0 and NN % 2))
                    for h in range(4):
                        last = nc.tensor.transpose(ps[:, 2 + n % 2, h * P:(h + 1) * P],
                                                   qs[:, j % 2, h * HD:(h + 1) * HD], c.ident[:])
                    last.then_inc(turned, 1)

                def scores(i, u):
                    qT, kT = units[u]["qT"], units[u]["kT"]
                    pe.wait_ge(stored, i * NN + 3 + max(normed.index(j) for j in units[u]["needs"]))
                    pe.wait_ge(exp_go, i * NU + u)
                    if u == 0:
                        pe.wait_ge(resid_done, i)
                    for pair in range(4):
                        head = 8 * (u % 2) + 2 * pair
                        for r in range(2):
                            last = nc.tensor.matmul(
                                ps[:, 4, (pair * 2 + r) * 64:(pair * 2 + r + 1) * 64],
                                qT[:, r, head:head + 2, :],
                                kT[:, head // per_kv, r * 64:(r + 1) * 64], start=True, stop=True)
                    last.then_inc(scores_ready, 1)

                def turn_probs(i, u):
                    pe.wait_ge(probs_ready, i * NU + u + 1)
                    pe.wait_ge(pt_stored, i * NU + u)
                    for pair in range(4):
                        last = nc.tensor.transpose(ps[:, 5, pair * P:(pair + 1) * P],
                                                   probs[:, u % 2, pair * P:(pair + 1) * P], c.ident[:])
                    last.then_inc(pt_turned, 1)

                def values(i, u):
                    v = units[u]["v"]
                    pe.wait_ge(pt_stored, i * NU + u + 1)
                    pe.wait_ge(evacuated, i * NB + 3 + units[u]["v_block"])
                    pe.wait_ge(o_read, i * NU + u)
                    span = min(4, per_kv // 2)
                    for r in range(2):
                        for pair in range(0, 4, span):
                            g = (8 * (u % 2) + 2 * pair) // per_kv
                            last = nc.tensor.matmul(
                                ps[:, 6 + r, pair * P:(pair + span) * P],
                                v[r * 64:(r + 1) * 64, g * HD:(g + 1) * HD],
                                probsT[r * 64:(r + 1) * 64, u % 2, pair * P:(pair + span) * P],
                                start=True, stop=True)
                    last.then_inc(o_ready, 1)

                def output(i, _):
                    if quant is None:
                        pe.wait_ge(o_read, (i + 1) * NU)
                    else:
                        pe.wait_ge(a_ready, (i + 1) * NU + 2)
                    n = NH * NU // 2
                    for h in range(n):
                        last = nc.tensor.matmul(ps[:, 4, 0:HID], attnT[:, h, :], w_out[:, h, :],
                                                start=h == 0, stop=h == n - 1)
                    last.then_inc(out_ready, 1)

                do = {"P": project, "T": turn, "S": scores, "R": turn_probs, "A": values, "F": output}
                with pe.Fori(0, NT) as i:
                    for what, n in steps["pe"]:
                        do[what](i, n)

            @block.scalar
            def _(act):
                def evacuate(i, j):
                    b = blocks[j]
                    act.wait_ge(proj_ready, i * NB + j + 1)
                    dst = qs[:, j % 2, :] if b["normed"] else b["dst"]
                    nc.scalar.activation(dst, ps[:, j % 2, :], ACT.Copy,
                                         scale=1.0 if b["scale"] is None else b["scale"]).then_inc(evacuated, 1)

                def normalise(i, j):
                    n = normed.index(j)
                    act.wait_ge(rstd_ready, i * NN + n + 1)
                    act.wait_ge(evacuated, i * NB + 2 + j + 1)
                    for h in range(4):
                        part = qs[:, j % 2, h * HD:(h + 1) * HD]
                        last = nc.scalar.activation(part, part, ACT.Copy, scale=rstd[:, j % 2, h:h + 1])
                    last.then_inc(norm_ready, 1)

                def store(i, j):
                    n, b = normed.index(j), blocks[j]
                    act.wait_ge(turned, i * NN + n + 1)
                    nc.scalar.activation(b["dst"], ps[:, 2 + n % 2, :].rearrange("p (h r n) -> p h r n", h=4, r=2),
                                         ACT.Identity, scale=b["wT"],
                                         bias=0.0 if b["bT"] is None else b["bT"]).then_inc(stored, 1)

                def exps(i, u):
                    act.wait_ge(exp_go, i * NU + u + 1)
                    nc.scalar.activation(probs[:, u % 2, :], probs[:, u % 2, :], ACT.Exp,
                                         scale=scale if mask is None else 1.0).then_inc(exp_done, 1)

                def store_probs(i, u):
                    act.wait_ge(pt_turned, i * NU + u + 1)
                    nc.scalar.activation(probsT[:, u % 2, :], ps[:, 5, :], ACT.Copy).then_inc(pt_stored, 1)

                def store_out(i, u):
                    act.wait_ge(o_ready, i * NU + u + 1)
                    for r in range(2):
                        last = nc.scalar.activation(attnT[:, 8 * u:8 * u + 8, r * 64:(r + 1) * 64],
                                                    ps[:, 6 + r, :].rearrange("p (h n) -> p h n", h=8), ACT.Copy)
                    last.then_inc(o_read, 1)

                do = {"E": evacuate, "N": normalise, "T": store, "X": exps, "R": store_probs, "O": store_out}
                with act.Fori(0, NT) as i:
                    for what, n in steps["act"]:
                        do[what](i, n)

            @block.vector
            def _(dve):
                v = nc.vector

                def evacuate(i, j):
                    b = blocks[j]
                    dve.wait_ge(proj_ready, i * NB + j + 1)
                    dst = qs[:, j % 2, :] if b["normed"] else b["dst"]
                    v.tensor_tensor(dst, ps[:, j % 2, :], b["bias"], ALU.add).then_inc(evacuated, 1)

                def variance(i, j):
                    b = j % 2
                    dve.wait_ge(evacuated, i * NB + 2 + j + 1)
                    for h in range(4):
                        chain.add(v.bn_stats(st6[:, b, h, :], qs[:, b, h * HD:(h + 1) * HD]))
                    chain.join()
                    even, odd, t = st6[:, b, :, 1:3], st6[:, b, :, 4:6], tmp[:, b]
                    chain.add(v.tensor_tensor(t[:, :, 0:2], even, odd, ALU.add))
                    chain.after(v.tensor_tensor(t[:, :, 2], even[:, :, 0], odd[:, :, 0], ALU.subtract))
                    chain.add(v.scalar_tensor_tensor(out=t[:, :, 2], in0=t[:, :, 2], scalar=0.25, in1=t[:, :, 2],
                                                     op0=ALU.mult, op1=ALU.mult))
                    if quant is None:
                        chain.add(v.scalar_tensor_tensor(out=t[:, :, 0], in0=t[:, :, 0], scalar=0.25,
                                                         in1=t[:, :, 0], op0=ALU.mult, op1=ALU.mult))
                    else:
                        chain.add(v.tensor_scalar(mean[:, b, :], t[:, :, 0], 0.5, None, ALU.mult))
                    chain.after(v.tensor_scalar(t[:, :, 1], t[:, :, 1], 1.0 / HD, eps, ALU.mult, ALU.add))
                    if quant is None:
                        chain.after(v.tensor_tensor(t[:, :, 2], t[:, :, 2], t[:, :, 0], ALU.add))
                    v.tensor_tensor(ve[:, b, :], t[:, :, 1], t[:, :, 2], ALU.add).then_inc(ve_ready, 1)

                def normalise(i, j):
                    n, b = normed.index(j), j % 2
                    dve.wait_ge(rstd_ready, i * NN + n + 1)
                    for h in range(4):
                        part = qs[:, b, h * HD:(h + 1) * HD]
                        last = v.tensor_scalar(part, part, mean[:, b, h:h + 1], rstd[:, b, h:h + 1],
                                               ALU.subtract, ALU.mult)
                    last.then_inc(norm_ready, 1)

                def less_max(i, u):
                    dve.wait_ge(scores_ready, i * NU + u + 1)
                    s = ps[:, 4, :].rearrange("p (g k) -> p g k", k=64)
                    p, top = probs[:, u % 2, :].rearrange("p (g k) -> p g k", k=64), mx[:, u % 2, 0, :]
                    if mask is not None:
                        chain.after(v.scalar_tensor_tensor(out=p, in0=s, scalar=scale,
                                                           in1=mask[:].unsqueeze(1).to_broadcast([P, 8, 64]),
                                                           op0=ALU.mult, op1=ALU.add))
                        s = p
                    chain.after(v.tensor_reduce(top, s, X, ALU.max))
                    v.tensor_tensor(p, s, bc(top, [P, 8, 64]), ALU.subtract).then_inc(exp_go, 1)

                def normalise_probs(i, u):
                    dve.wait_ge(exp_done, i * NU + u + 1)
                    p = probs[:, u % 2, :].rearrange("p (g k) -> p g k", k=64)
                    chain.after(v.tensor_reduce(mx[:, u % 2, 0, :], p, X, ALU.add))
                    chain.after(v.reciprocal(mx[:, u % 2, 1, :], mx[:, u % 2, 0, :]))
                    v.tensor_tensor(p, p, bc(mx[:, u % 2, 1, :], [P, 8, 64]), ALU.mult).then_inc(probs_ready, 1)

                def scale_out(i, u):
                    dve.wait_ge(o_ready, i * NU + u + 1)
                    dve.wait_ge(a_ready, i * NU + u + 1)
                    for r in range(2):
                        last = v.tensor_tensor(yo[:, r * 512:(r + 1) * 512].rearrange("p (h n) -> p h n", h=8),
                                               ps[:, 6 + r, :].rearrange("p (h n) -> p h n", h=8),
                                               bc(quant["smooth"][:, 8 * u:8 * u + 8], [P, 8, 64]), ALU.mult)
                        if r == 0:
                            chain.add(last)
                    last.then_inc(o_read, 1)
                    chain.join()
                    dve.wait_ge(o_read, i * NU + u + 1)
                    chain.after(v.tensor_scalar(yb[:, u % 2, :], yo[:], -448.0, 448.0, ALU.max, ALU.min))
                    chain.after(v.tensor_scalar(ybig[:, u % 2, :].bitcast(U16), yb[:, u % 2, :].bitcast(U16), 0x7FFF,
                                                None, ALU.bitwise_and))
                    v.tensor_scalar(ybig[:, u % 2, :], ybig[:, u % 2, :], FP8_LEAST, FP8_STEP, ALU.max,
                                    ALU.mult).then_inc(yo_ready, 1)

                def next_inputs(tile):
                    chain.after(v.tensor_tensor(xq_next[:], sources["x"][:, :, tile].unsqueeze(1).to_broadcast(
                        [P, 4, KC, P]), bc(quant["in_inv"][:], [P, 4, KC, P]), ALU.mult))
                    chain.after(v.tensor_scalar(xb[:], xq_next[:], -448.0, 448.0, ALU.max, ALU.min))
                    chain.after(v.tensor_scalar(xbig[:].bitcast(U16), xb[:].bitcast(U16), 0x7FFF, None,
                                                ALU.bitwise_and))
                    v.tensor_scalar(xbig[:], xbig[:], FP8_LEAST, FP8_STEP, ALU.max, ALU.mult).then_inc(zb_ready, 1)

                def add_out(i, _):
                    dve.wait_ge(out_ready, i + 1)
                    v.scalar_tensor_tensor(out=c.resid[:, i, :], in0=ps[:, 4, 0:HID], scalar=out_scale,
                                           in1=c.resid[:, i, :], op0=ALU.mult, op1=ALU.add).then_inc(resid_done, 1)

                do = {"E": evacuate, "V": variance, "N": normalise, "M": less_max, "Q": normalise_probs,
                      "O": scale_out, "F": add_out,
                      "Z": lambda i, _: next_inputs(bass.ds((i + 1) % NT * P, P))}
                cost = {"V": 9 + (quant is None), "M": 1 + (mask is not None), "Q": 2, "O": 3, "Z": 3}
                per = 1 + sum(cost.get(what, 0) for what, _ in steps["dve"])
                dve.sem_inc(evacuated, 2)
                dve.sem_inc(stored, 2)
                chain = Chain(dve, dve_chain)
                if quant is not None:
                    next_inputs(slice(0, P))
                first = chain.n
                with dve.Fori(0, NT) as i:
                    chain = Chain(dve, dve_chain, first + i * per)
                    dve.wait_ge(proj_ready, i * NB)
                    if quant is None:
                        chain.after(v.tensor_copy(src["x"][:], sources["x"][:, :, bass.ds(i * P, P)]))
                    else:
                        dve.wait_ge(z_ready, i + 1)
                        chain.after(v.tensor_copy(xq[:], xq_next[:]))
                    v.tensor_copy(src["ctx"][:], sources["ctx"][:, :, bass.ds(i * P, P)]).then_inc(x_ready, 1)
                    for what, n in steps["dve"]:
                        do[what](i, n)
                    assert chain.n == per, (chain.n, per)

            @block.gpsimd
            def _(pool):
                g = nc.gpsimd

                def rstds(i, j):
                    pool.wait_ge(ve_ready, i * NN + normed.index(j) + 1)
                    g.tensor_tensor(rstd[:, j % 2, :], ve[:, j % 2, :], c.mhalf[:, 0:4], ALU.pow).then_inc(rstd_ready, 1)

                def quantise_out(i, u):
                    pool.wait_ge(yo_ready, i * NU + u + 1)
                    pool.wait_ge(a_ready, i * NU + u + 2)
                    if u == 0:
                        pool.wait_ge(out_ready, i)
                    chain.after(g.tensor_tensor(ysum[:], yb[:, u % 2, :], ybig[:, u % 2, :], ALU.add))
                    for r in range(2):
                        last = g.tensor_tensor(
                            attnT[:, 8 * u:8 * u + 8, r * 64:(r + 1) * 64],
                            ysum[:, r * 512:(r + 1) * 512].rearrange("p (h n) -> p h n", h=8),
                            ybig[:, u % 2, r * 512:(r + 1) * 512].rearrange("p (h n) -> p h n", h=8), ALU.subtract)
                        if r == 0:
                            chain.add(last)
                    last.then_inc(a_ready, 1)

                def round_inputs(i, _):
                    pool.wait_ge(zb_ready, i + 1)
                    chain.after(g.tensor_tensor(xq_next[:], xb[:], xbig[:], ALU.add))
                    chain.after(g.tensor_tensor(xq_next[:], xq_next[:], xbig[:], ALU.subtract))
                    g.tensor_tensor(xq_next[:], xq_next[:], bc(quant["in_scale"][:], [P, 4, KC, P]),
                                    ALU.mult).then_inc(z_ready, 1)

                if quant is not None:
                    pool.sem_inc(a_ready, 2)
                    chain = Chain(pool, pool_chain)
                    round_inputs(0, 0)
                    first, per = chain.n, sum({"O": 2, "Z": 2}.get(what, 0) for what, _ in steps["pool"])
                else:
                    first = per = 0
                with pool.Fori(0, NT) as i:
                    chain = Chain(pool, pool_chain, first + i * per)
                    for what, n in steps["pool"]:
                        if what == "Z":
                            round_inputs(i + 1, n)
                        else:
                            {"R": rstds, "O": quantise_out}[what](i, n)
                    assert chain.n == per, (chain.n, per)


def load(c, st, waits, name, shape, src=None):
    buf = c.sb(st, name, shape)
    waits.append((buf, c.dram[name] if src is None else src))
    return buf


def load_all(c, waits, also=None):
    nc = c.nc
    with ExitStack() as st:
        sp_in, act_in = c.sem(st, "sp_in"), c.sem(st, "act_in")
        with nc.Block() as block:
            @block.sync
            def _(sp):
                for buf, src in waits[0::2]:
                    sp.dma_start(buf[:], src).then_inc(sp_in, 16)
                sp.wait_ge(sp_in, 16 * len(waits[0::2]))

            @block.scalar
            def _(act):
                for buf, src in waits[1::2]:
                    act.dma_start(buf[:], src).then_inc(act_in, 16)
                act.wait_ge(act_in, 16 * len(waits[1::2]))


def by_head(qT, b):
    return qT[:, :, 4 * b:4 * b + 4, :].rearrange("p r h n -> p h r n")


def by_row(kT, b):
    return kT[:, 4 * b:4 * b + 4, :].rearrange("p h (r n) -> p h r n", r=2)


def attn0(c):
    layernorm(c, c.resid, c.norm, c.xT)
    with ExitStack() as st:
        w = []
        wq = load(c, st, w, "L0_wq", [P, KC, NH * HD])
        wk = load(c, st, w, "L0_wk", [P, KC, 4 * HD])
        wv = load(c, st, w, "L0_wv", [P, KC, 4 * HD])
        wo = load(c, st, w, "L0_wo", [P, NH, HID])
        bias = c.sb(st, "bias", [P, 6, 512])
        w.append((bias[:, 0:4].rearrange("p b n -> p (b n)"), c.dram["L0_xattn_bq"].partition_broadcast(P)))
        w.append((bias[:, 4], c.dram["L0_xattn_bk"].partition_broadcast(P)))
        w.append((bias[:, 5], c.dram["L0_xattn_bv"].partition_broadcast(P)))
        norms = load(c, st, w, "L0_norms", [P, 2])
        mask = c.sb(st, "mask", [P, SEQ])
        w.append((mask[0:64], c.dram["mask"]))
        w.append((mask[64:128], c.dram["mask"]))
        load_all(c, w)
        qT = c.sb(st, "qT", [P, 2, NH, SEQ])
        kT = c.sb(st, "kT", [P, 4, P])
        v = c.sb(st, "v", [P, 4 * HD])
        blocks = [dict(src="ctx", w=wk, normed=True, bias=bias[:, 4], dst=by_row(kT, 0), wT=norms[:, 1:2], bT=None),
                  dict(src="ctx", w=wv, normed=False, bias=bias[:, 5], dst=v[:])]
        blocks += [dict(src="x", w=wq[:, :, 512 * b:512 * b + 512], normed=True, bias=bias[:, b],
                        dst=by_head(qT, b), wT=norms[:, 0:1], bT=None) for b in range(4)]
        units = [dict(qT=qT, kT=kT, v=v, needs=[0, 2 + 2 * u, 3 + 2 * u], v_block=1) for u in range(2)]
        heads_attention(c, ORDER0, {"x": c.xT, "ctx": c.ctxT}, blocks, units, 4, 1e-6, wo, c.gate[:, 0:1], mask=mask)


def attn3(c):
    nc = c.nc
    layernorm(c, c.resid, c.norm, None)
    layernorm(c, c.norm, c.norm, c.xT)
    with ExitStack() as st:
        w = []
        wq = load(c, st, w, "L3_wq", [P, KC, NH * HD])
        wqx = load(c, st, w, "L3_wqx", [P, KC, NH * HD])
        wk = load(c, st, w, "L3_wk", [P, KC, 8 * HD])
        wv = load(c, st, w, "L3_wv", [P, KC, 8 * HD])
        wkvx = load(c, st, w, "L3_wkvx", [P, KC, 16 * HD])
        wproj = load(c, st, w, "L3_wproj", [P, 2 * NH, HID])
        ln = load(c, st, w, "L3_ln", [P, 2, KC])
        in_scale = load(c, st, w, "L3_in_scale", [P, 4, KC])
        norms = load(c, st, w, "L3_norms", [P, 4, 2])
        smooth = load(c, st, w, "L3_smooth", [P, 2 * NH])
        scales = c.sb(st, "scales", [P, 6])
        for n, s in enumerate(("wq_scale", "wk_scale", "wv_scale", "wqx_scale", "proj_w_scale", "proj_in_scale")):
            w.append((scales[:, n:n + 1], c.dram["L3_xattn_" + s].partition_broadcast(P)))
        load_all(c, w)
        in_inv = c.sb(st, "in_inv", [P, 4, KC])
        smooth_inv = c.sb(st, "smooth_inv", [P, 2 * NH])
        out_scale = c.sb(st, "out_scale", [P, 1])
        consts, affine = c.sem(st, "consts"), c.sem(st, "affine")
        with nc.Block() as block:
            @block.vector
            def _(dve):
                nc.vector.reciprocal(in_inv[:], in_scale[:]).then_inc(consts, 1)
                nc.vector.reciprocal(smooth_inv[:], smooth[:]).then_inc(consts, 1)
                nc.vector.tensor_tensor(out_scale[:], scales[:, 4:5], scales[:, 5:6], ALU.mult).then_inc(consts, 1)
                dve.wait_ge(consts, 3)
                nc.vector.tensor_tensor(out_scale[:], out_scale[:], c.gate[:, 3:4], ALU.mult).then_inc(consts, 1)

            @block.scalar
            def _(act):
                for k in range(KC):
                    nc.scalar.activation(c.xT[:, k, :], c.xT[:, k, :], ACT.Identity, scale=ln[:, 0, k:k + 1],
                                         bias=ln[:, 1, k:k + 1]).then_inc(affine, 1)
        qT = c.sb(st, "qT", [P, 2, NH, SEQ])
        kT = c.sb(st, "kT", [P, 8, P])
        v = c.sb(st, "v", [P, 8 * HD])
        vx = c.sb(st, "vx", [P, 8 * HD])

        def turned(src, w_, dst, n, scale):
            return [dict(src=src, w=w_[:, :, 512 * b:512 * b + 512], normed=True, scale=scale,
                         dst=dst(b), wT=norms[:, n, 0:1], bT=norms[:, n, 1:2])
                    for b in range(w_.shape[2] // 512 if src != "ctx" else 2)]

        def plain(src, w_, dst, scale, off=0):
            return [dict(src=src, w=w_[:, :, off + 512 * b:off + 512 * b + 512], normed=False, scale=scale,
                         dst=dst[:, 512 * b:512 * b + 512]) for b in range(2)]

        blocks = (turned("k", wk, lambda b: by_row(kT, b), 1, scales[:, 1:2]) + plain("v", wv, v, scales[:, 2:3])
                  + turned("q", wq, lambda b: by_head(qT, b), 0, scales[:, 0:1]) + turned("ctx", wkvx, lambda b: by_row(kT, b), 3, None)
                  + plain("ctx", wkvx, vx, None, 8 * HD) + turned("qx", wqx, lambda b: by_head(qT, b), 2, scales[:, 3:4]))
        units = [dict(qT=qT, kT=kT, v=v if u < 2 else vx, needs=[(5, 7, 13, 15)[u]], v_block=(2, 3, 10, 11)[u])
                 for u in range(4)]
        heads_attention(c, ORDER3, {"x": c.xT, "ctx": c.ctxT}, blocks, units, 8, 1e-5, wproj, out_scale[:, 0:1],
                        quant={"in_inv": in_inv, "in_scale": in_scale, "smooth": smooth_inv})



def decay_by_key():
    gam = (1.0 - 2.0 ** (-5.0 - np.arange(2, dtype=np.float32))).astype(np.float32)
    at = np.arange(SEQ, dtype=np.float32)
    expo = at[None, :] - at[:, None]
    m = np.where(expo[None] <= 0, gam[:, None, None] ** expo[None], 0.0).astype(np.float32)
    m = m / np.sqrt(m.sum(axis=-1, dtype=np.float32))[:, None, :]
    m = m.astype(np.float32).transpose(2, 0, 1)
    return np.ascontiguousarray(np.concatenate([m, m]))


def attn1(c):
    nc = c.nc
    layernorm(c, c.resid, c.norm, c.xT)
    with ExitStack() as st:
        w = []
        wh = load(c, st, w, "L1_wh", [P, 2, HD])
        wg = load(c, st, w, "L1_wg", [P, KC, HID])
        wo = load(c, st, w, "L1_wo", [P, KC, HID])
        decay = load(c, st, w, "L1_decay", [P, 2, SEQ])
        gamma = c.sb(st, "gamma", [P, HID])
        beta = c.sb(st, "beta", [P, HID])
        w.append((gamma, c.dram["L1_xattn_gn_gamma"].partition_broadcast(P)))
        w.append((beta, c.dram["L1_xattn_gn_beta"].partition_broadcast(P)))
        load_all(c, w)
        qT = c.sb(st, "qT", [P, 2, TOK])
        kT = c.sb(st, "kT", [P, 2, TOK])
        v = c.sb(st, "v", [P, NT, HID])
        relu = c.sb(st, "relu", [P, NT, HID])
        mix = c.sb(st, "mix", [P, 2, P])
        (qk_ready, qk_stored, v_ready, v_stored, s_ready, mix_zero, chain_s, mix_ready, o_ready, o_stored) = (
            c.sem(st, n) for n in ("qk_ready", "qk_stored", "v_ready", "v_stored", "s_ready", "mix_zero", "chain",
                                   "mix_ready", "o_ready", "o_stored"))
        out = c.norm
        with nc.Block() as block:
            @block.tensor
            def _(pe):
                for n, (src, h, half) in enumerate((s, h, f) for s in (c.ctxT, c.xT) for h in range(2)
                                                   for f in range(2)):
                    nc.tensor.matmul(c.psum[:, n, :], wh[:, h, :], src[:, h, half * HALF:(half + 1) * HALF],
                                     start=True, stop=True).then_inc(qk_ready, 1)
                for t in range(NT):
                    pe.wait_ge(qk_stored, 6 if t < 4 else 8)
                    for h in range(2):
                        nc.tensor.matmul(c.psum[:, t // 2, t % 2 * HID + h * HD:t % 2 * HID + (h + 1) * HD],
                                         c.ctxT[:, h, t * P:(t + 1) * P], wh[:, h, :], start=True, stop=True)
                    for k in range(KC):
                        last = nc.tensor.matmul(c.psum[:, 4 + t // 2, t % 2 * HID:(t % 2 + 1) * HID],
                                                c.xT[:, k, t * P:(t + 1) * P], wg[:, k, :], start=k == 0,
                                                stop=k == KC - 1)
                    if t % 2:
                        last.then_inc(v_ready, 1)
                pe.wait_ge(v_stored, 8)
                for h in range(2):
                    for r in range(2):
                        for b in range(BATCH):
                            last = nc.tensor.matmul(c.psum[64 * r:64 * r + 64, 2 * h + r, 0:SEQ],
                                                    kT[:, h, b * SEQ:(b + 1) * SEQ], qT[:, h, b * SEQ:(b + 1) * SEQ],
                                                    start=b == 0, stop=b == BATCH - 1)
                        last.then_inc(s_ready, 1)
                pe.wait_ge(mix_ready, 4)
                for t in range(NT):
                    for h in range(2):
                        last = nc.tensor.matmul(c.psum[:, 4 + t // 2, t % 2 * HID + h * HD:t % 2 * HID + (h + 1) * HD],
                                                mix[:, h, :], v[:, t, h * HD:(h + 1) * HD], start=True, stop=True)
                    if t % 2:
                        last.then_inc(o_ready, 1)

            @block.scalar
            def _(act):
                for n in range(0, 8, 2):
                    act.wait_ge(qk_ready, n + 2)
                    nc.scalar.activation((kT if n < 4 else qT)[:, n // 2 % 2, :],
                                         c.psum[:, n:n + 2, :].rearrange("p b n -> p (b n)"),
                                         ACT.Copy).then_inc(qk_stored, 2)
                for g in range(4):
                    act.wait_ge(v_ready, g + 1)
                    nc.scalar.activation(v[:, 2 * g:2 * g + 2, :],
                                         c.psum[:, g, :].rearrange("p (t n) -> p t n", t=2), ACT.Copy).then_inc(v_stored, 1)
                    nc.scalar.activation(relu[:, 2 * g:2 * g + 2, :],
                                         c.psum[:, 4 + g, :].rearrange("p (t n) -> p t n", t=2),
                                         ACT.Relu).then_inc(v_stored, 1)
                for g in range(4):
                    act.wait_ge(o_ready, g + 1)
                    nc.scalar.activation(out[:, 2 * g:2 * g + 2, :],
                                         c.psum[:, 4 + g, :].rearrange("p (t n) -> p t n", t=2), ACT.Copy).then_inc(o_stored, 1)

            @block.vector
            def _(dve):
                chain = Chain(dve, chain_s)
                chain.after(nc.vector.memset(mix[:], 0.0))
                for h in range(2):
                    for r in range(2):
                        dve.wait_ge(s_ready, 2 * h + r + 1)
                        rows = slice(64 * r, 64 * r + 64)
                        part = mix[rows, h, 64 * r:64 * r + 64]
                        chain.after(nc.vector.scalar_tensor_tensor(
                            out=part, in0=c.psum[rows, 2 * h + r, 0:SEQ], scalar=HD ** -0.5, in1=decay[rows, h, :],
                            op0=ALU.mult, op1=ALU.mult))
                        chain.after(nc.vector.scalar_tensor_tensor(out=part, in0=part, scalar=-1.0, in1=part,
                                                                   op0=ALU.mult, op1=ALU.max))
                        nc.vector.tensor_scalar(part, part, 1.0, None, ALU.max).then_inc(mix_ready, 1)
        normed = v
        layernorm(c, out, normed, None, eps=1e-3)
        yT = qT
        (chain2, y_ready, turned, stored, p_ready, added) = (
            c.sem(st, n) for n in ("chain2", "y_ready", "turned", "y_stored", "p_ready", "added"))
        with nc.Block() as block:
            @block.vector
            def _(dve):
                chain = Chain(dve, chain2)
                for t in range(NT):
                    chain.after(nc.vector.tensor_tensor(normed[:, t, :], normed[:, t, :], gamma[:], ALU.mult))
                    chain.after(nc.vector.tensor_tensor(normed[:, t, :], normed[:, t, :], beta[:], ALU.add))
                    nc.vector.tensor_tensor(normed[:, t, :], normed[:, t, :], relu[:, t, :], ALU.mult).then_inc(y_ready, 1)
                for g in range(4):
                    dve.wait_ge(p_ready, g + 1)
                    nc.vector.scalar_tensor_tensor(
                        out=c.resid[:, 2 * g:2 * g + 2, :], in0=c.psum[:, 4 + g, :].rearrange("p (t n) -> p t n", t=2),
                        scalar=c.gate[:, 1:2], in1=c.resid[:, 2 * g:2 * g + 2, :], op0=ALU.mult,
                        op1=ALU.add).then_inc(added, 1)

            @block.tensor
            def _(pe):
                pe_transpose_tokens(c, pe, normed, y_ready, turned)
                for t in range(NT):
                    if t % 2 == 0:
                        pe.wait_ge(stored, t // 2 + 1)
                    for k in range(KC):
                        last = nc.tensor.matmul(c.psum[:, 4 + t // 2, t % 2 * HID:(t % 2 + 1) * HID],
                                                yT[:, k, t * P:(t + 1) * P], wo[:, k, :], start=k == 0, stop=k == KC - 1)
                    if t % 2:
                        last.then_inc(p_ready, 1)

            @block.scalar
            def _(act):
                act_store_transposed(c, act, yT, turned, stored)



def attn2(c):
    nc = c.nc
    layernorm(c, c.resid, c.norm, c.xT)
    H, D = NH, 16
    LN255 = float(np.log(255.0))
    with ExitStack() as st:
        w = []
        wq = load(c, st, w, "L2_wq", [P, KC, HID])
        wkv = load(c, st, w, "L2_wkv", [P, KC, 2 * HID])
        wp = load(c, st, w, "L2_wp", [P, KC, HID])
        bias = c.sb(st, "bias", [P, 2, HID])
        w.append((bias[:, 0], c.dram["L2_xattn_bq"].partition_broadcast(P)))
        w.append((bias[:, 1], c.dram["L2_bk"].partition_broadcast(P)))
        bv = load(c, st, w, "L2_bv", [P, KC])
        bp = c.sb(st, "bp", [P, HID])
        w.append((bp, c.dram["L2_xattn_bp"].partition_broadcast(P)))
        load_all(c, w)
        qT = c.sb(st, "qT", [P, H // 2, TOK], BF16)
        kT = c.sb(st, "kT", [P, H // 2, TOK], BF16)
        v = c.sb(st, "v", [P, NT, HID], BF16)
        sq = c.sb(st, "sq", [P, NT, 2, H])
        sv = c.sb(st, "sv", [P, 2, KC])
        with ExitStack() as inner:
            qk = c.sb(inner, "qk", [P, NT, 2, HID])
            parts = c.sb(inner, "parts", [P, 2, NT, H, 4, D], BF16)
            inv = c.sb(inner, "inv", [P, NT, 2, H])
            vT = c.sb(inner, "vT", [P, KC, TOK])
            vb = c.sb(inner, "vb", [P, KC, TOK], BF16)
            (chain_s, pool_s, qk_ready, qk_read, v_ready, vT_ready, vb_ready, parts_ready, turned, stored, v_turned,
             v_stored) = (c.sem(inner, n) for n in (
                 "chain", "pool_chain", "qk_ready", "qk_read", "v_ready", "vT_ready", "vb_ready", "parts_ready",
                 "turned", "stored", "v_turned", "v_stored"))
            with nc.Block() as block:
                @block.tensor
                def _(pe):
                    for t in range(NT):
                        for s, (src, w_) in enumerate(((c.xT, wq[:, :, :]), (c.ctxT, wkv[:, :, 0:HID]))):
                            for k in range(KC):
                                last = nc.tensor.matmul(c.psum[:, t, s * HID:(s + 1) * HID],
                                                        src[:, k, t * P:(t + 1) * P], w_[:, k, :], start=k == 0,
                                                        stop=k == KC - 1)
                        last.then_inc(qk_ready, 1)
                    for n, (m, half) in enumerate((m, f) for m in range(KC) for f in range(2)):
                        pe.wait_ge(qk_read, n + 1)
                        for k in range(KC):
                            last = nc.tensor.matmul(c.psum[:, n, :], wkv[:, k, HID + m * P:HID + (m + 1) * P],
                                                    c.ctxT[:, k, half * HALF:(half + 1) * HALF], start=k == 0,
                                                    stop=k == KC - 1)
                        last.then_inc(v_ready, 1)
                    pe.wait_ge(vb_ready, KC)
                    pe.wait_ge(qk_read, NT)
                    pb = c.psum[:, 4:6, :].bitcast(BF16)
                    for t in range(NT):
                        for m in range(KC):
                            last = nc.tensor.transpose(pb[:, t // 4, t % 4 * HID + m * P:t % 4 * HID + (m + 1) * P],
                                                       vb[:, m, t * P:(t + 1) * P], c.identb[:])
                        if t % 4 == 3:
                            last.then_inc(v_turned, 1)
                    for s in range(2):
                        pe.wait_ge(parts_ready, s + 1)
                        for t in range(NT):
                            n = s * NT + t
                            b = 6 + n % 2
                            if n >= 2:
                                pe.wait_ge(stored, n - 1)
                            dst = c.psum[:, b, :].bitcast(BF16)
                            for g in range(H // 2):
                                last = nc.tensor.transpose(
                                    dst[:, g * P:(g + 1) * P],
                                    parts[:, s, t, 2 * g:2 * g + 2, :, :].rearrange("p h f d -> p (h f d)"), c.identb[:])
                            last.then_inc(turned, 1)

                @block.scalar
                def _(act):
                    for m in range(KC):
                        act.wait_ge(v_ready, 2 * m + 2)
                        nc.scalar.activation(vT[:, m, :], c.psum[:, 2 * m:2 * m + 2, :].rearrange("p b n -> p (b n)"),
                                             ACT.Identity, bias=bv[:, m:m + 1]).then_inc(vT_ready, 1)
                    pb = c.psum[:, 4:6, :].bitcast(BF16)
                    for g in range(2):
                        act.wait_ge(v_turned, g + 1)
                        nc.scalar.activation(v[:, 4 * g:4 * g + 4, :], pb[:, g, :].rearrange("p (t n) -> p t n", t=4),
                                             ACT.Copy).then_inc(v_stored, 1)
                    for n in range(2 * NT):
                        s, t = n // NT, n % NT
                        act.wait_ge(turned, n + 1)
                        nc.scalar.activation((qT if s else kT)[:, :, t * P:(t + 1) * P],
                                             c.psum[:, 6 + n % 2, :].bitcast(BF16).rearrange("p (g n) -> p g n", g=8),
                                             ACT.Copy).then_inc(stored, 1)

                @block.vector
                def _(dve):
                    g, chain = nc.vector, Chain(dve, chain_s)
                    for t in range(NT):
                        dve.wait_ge(qk_ready, t + 1)
                        g.tensor_tensor(qk[:, t], c.psum[:, t, :].rearrange("p (s n) -> p s n", s=2), bias[:],
                                        ALU.add).then_inc(qk_read, 1)
                    dve.wait_ge(qk_read, NT)
                    chain.after(g.tensor_scalar(qk[:, :, 0, :], qk[:, :, 0, :], D ** -0.5, None, ALU.mult))
                    flat = qk[:].rearrange("p t s (h d) -> p (t s h) d", d=D)
                    steps, inverse = sq[:].rearrange("p t s h -> p (t s h)"), inv[:].rearrange("p t s h -> p (t s h)")
                    chain.after(g.tensor_reduce(steps, flat, X, ALU.max, apply_absolute_value=True))
                    chain.after(g.tensor_scalar(steps, steps, 1 / 127.0, 1e-8, ALU.mult, ALU.max))
                    chain.after(g.reciprocal(inverse, steps))
                    chain.after(g.tensor_tensor(flat, flat, bc(inverse, [P, NT * 2 * H, D]), ALU.mult))
                    chain.after(g.tensor_scalar(qk[:], qk[:], ROUND, ROUND, ALU.add, ALU.subtract))
                    keys = qk[:, :, 1, :].rearrange("p t (h d) -> p t h d", d=D)
                    chain.after(g.tensor_tensor(keys, keys, bc(sq[:, :, 1, :], [P, NT, H, D]), ALU.mult))
                    for f in range(3):
                        dst = parts[:, 0, :, :, f, :]
                        chain.after(g.tensor_copy(dst, keys))
                        if f < 2:
                            chain.after(g.tensor_tensor(keys, keys, dst, ALU.subtract))
                    g.memset(parts[:, 0, :, :, 3, :], 0.0).then_inc(parts_ready, 1)
                    queries = qk[:, :, 0, :].rearrange("p t (h d) -> p t h d", d=D)
                    for f in range(3):
                        chain.add(g.tensor_copy(parts[:, 1, :, :, f, :], queries))
                    chain.join()
                    g.memset(parts[:, 1, :, :, 3, :], 0.0).then_inc(parts_ready, 1)
                    for m in range(KC):
                        dve.wait_ge(vT_ready, m + 1)
                        chain.after(g.tensor_reduce(sv[:, 0, m:m + 1], vT[:, m, :], X, ALU.max,
                                                    apply_absolute_value=True))
                        chain.after(g.tensor_scalar(sv[:, 0, m:m + 1], sv[:, 0, m:m + 1], 1 / 127.0, 1e-8, ALU.mult,
                                                    ALU.max))
                        chain.after(g.reciprocal(sv[:, 1, m:m + 1], sv[:, 0, m:m + 1]))
                        chain.after(g.tensor_scalar(vT[:, m, :], vT[:, m, :], sv[:, 1, m:m + 1], ROUND, ALU.mult,
                                                    ALU.add))
                        g.tensor_scalar(vb[:, m, :], vT[:, m, :], ROUND, None, ALU.subtract).then_inc(vb_ready, 1)
                    chain.after(g.tensor_scalar(bp[:], bp[:], c.gate[:, 2:3], None, ALU.mult))

        (chain_s, tile_ready, s_ready, m_ready, exp_done, rounded, turned, even_stored, odd_stored, o_ready, o_scaled,
         ot_ready, ot_stored, y_ready, y_added, small_done) = (c.sem(st, n) for n in (
             "chain", "tile_ready", "s_ready", "m_ready", "exp_done", "rounded", "turned", "even_stored",
             "odd_stored", "o_ready", "o_scaled", "ot_ready", "ot_stored", "y_ready", "y_added", "small_done"))
        qt = c.sb(st, "qt", [P, H // 2, P], BF16)
        sqt = c.sb(st, "sqt", [P, H])
        m = c.sb(st, "m", [P, H])
        nb = c.sb(st, "nb", [P, H])
        e = c.sb(st, "e", [P, 2, TOK])
        esum = c.sb(st, "esum", [P, 2, H])
        pi = c.sb(st, "pi", [P, 2, TOK], BF16)
        pT = c.sb(st, "pT", [P, 2, TOK], BF16)
        o = c.sb(st, "o", [P, HID])
        oT = c.sb(st, "oT", [P, KC, P])
        small = c.sb(st, "small", [P, 1])
        with nc.Block() as block:
            @block.tensor
            def _(pe):
                def scores(i, h):
                    rows = slice(64 * (h % 2), 64 * (h % 2) + 64)
                    if h == 0:
                        pe.wait_ge(tile_ready, i + 1)
                    for f in range(2):
                        last = nc.tensor.matmul(c.psum[:, 2 * (h % 2) + f, :], qt[rows, h // 2, :],
                                                kT[rows, h // 2, f * HALF:(f + 1) * HALF], start=True, stop=True)
                    last.then_inc(s_ready, 1)

                def turn(i, h):
                    pe.wait_ge(rounded, i * H + h + 1)
                    dst = c.psum[:, 4 + h % 2, :].bitcast(BF16)
                    for k in range(NT):
                        last = nc.tensor.transpose(dst[:, k * P:(k + 1) * P], pi[:, h % 2, k * P:(k + 1) * P],
                                                   c.identb[:])
                    last.then_inc(turned, 1)

                def values(i, h):
                    pe.wait_ge(odd_stored if h % 2 else even_stored, i * (H // 2) + h // 2 + 1)
                    if h == 0:
                        pe.wait_ge(o_scaled, i)
                    for k in range(NT):
                        last = nc.tensor.matmul(c.psum[:, 6, h * D:(h + 1) * D], pT[:, h % 2, k * P:(k + 1) * P],
                                                v[:, k, h * D:(h + 1) * D], start=k == 0, stop=k == NT - 1)
                    if h == H - 1:
                        last.then_inc(o_ready, 1)

                with pe.Fori(0, NT) as i:
                    scores(i, 0)
                    for h in range(H):
                        if h + 1 < H:
                            scores(i, h + 1)
                        turn(i, h)
                        if h:
                            values(i, h - 1)
                    values(i, H - 1)
                    pe.wait_ge(o_scaled, i + 1)
                    pe.wait_ge(y_added, i)
                    for k in range(KC):
                        last = nc.tensor.transpose(c.psum[:, 7, k * P:(k + 1) * P], o[:, k * P:(k + 1) * P], c.ident[:])
                    last.then_inc(ot_ready, 1)
                    pe.wait_ge(ot_stored, i + 1)
                    for k in range(KC):
                        last = nc.tensor.matmul(c.psum[:, 7, HID:2 * HID], oT[:, k, :], wp[:, k, :], start=k == 0,
                                                stop=k == KC - 1)
                    last.then_inc(y_ready, 1)

            @block.scalar
            def _(act):
                with act.Fori(0, NT) as i:
                    for h in range(H):
                        act.wait_ge(m_ready, i * H + h + 1)
                        nc.scalar.activation(e[:, h % 2, :],
                                             c.psum[:, 2 * (h % 2):2 * (h % 2) + 2, :].rearrange("p b n -> p (b n)"),
                                             ACT.Exp, scale=sqt[:, h:h + 1], bias=nb[:, h:h + 1],
                                             accum_out=esum[:, 0, h:h + 1]).then_inc(exp_done, 1)
                        if h and h % 2 == 0:
                            act.wait_ge(turned, i * H + h)
                            nc.scalar.activation(pT[:, 1, :], c.psum[:, 5, :].bitcast(BF16), ACT.Copy
                                                 ).then_inc(odd_stored, 1)
                    act.wait_ge(turned, i * H + H)
                    nc.scalar.activation(pT[:, 1, :], c.psum[:, 5, :].bitcast(BF16), ACT.Copy).then_inc(odd_stored, 1)
                    act.wait_ge(ot_ready, i + 1)
                    for k in range(KC):
                        last = nc.scalar.activation(oT[:, k, :], c.psum[:, 7, k * P:(k + 1) * P], ACT.Copy,
                                                    scale=sv[:, 0, k:k + 1])
                    last.then_inc(ot_stored, 1)

            @block.vector
            def _(dve):
                g = nc.vector
                per = H * 2 + 2 + 1 + 1
                with dve.Fori(0, NT) as i:
                    chain = Chain(dve, chain_s, i * per)

                    def biggest(h):
                        dve.wait_ge(s_ready, i * H + h + 1)
                        chain.after(g.tensor_reduce(m[:, h:h + 1], c.psum[:, 2 * (h % 2):2 * (h % 2) + 2, :], XY, ALU.max))
                        chain.after(g.tensor_tensor(m[:, h:h + 1], m[:, h:h + 1], sqt[:, h:h + 1], ALU.mult))
                        g.tensor_scalar(nb[:, h:h + 1], m[:, h:h + 1], -1.0, LN255, ALU.mult, ALU.add
                                        ).then_inc(m_ready, 1)

                    dve.wait_ge(y_ready, i)
                    chain.add(g.tensor_copy(sqt[:], sq[:, bass.ds(i, 1), 0, :].rearrange("p o h -> p (o h)")))
                    g.tensor_copy(qt[:], qT[:, :, bass.ds(i * P, P)]).then_inc(tile_ready, 1)
                    chain.join()
                    biggest(0)
                    for h in range(H):
                        if h + 1 < H:
                            biggest(h + 1)
                        if h % 2 == 0:
                            dve.wait_ge(turned, i * H + h + 1)
                            g.tensor_copy(pT[:, 0, :], c.psum[:, 4, :].bitcast(BF16)).then_inc(even_stored, 1)
                    dve.wait_ge(exp_done, i * H + H)
                    chain.after(g.reciprocal(esum[:, 1, :], esum[:, 0, :]))
                    dve.wait_ge(o_ready, i + 1)
                    g.tensor_tensor(o[:].rearrange("p (h d) -> p h d", d=D),
                                    c.psum[:, 6, 0:HID].rearrange("p (h d) -> p h d", d=D),
                                    bc(esum[:, 1, :], [P, H, D]), ALU.mult).then_inc(o_scaled, 1)
                    dve.wait_ge(y_ready, i + 1)
                    chain.after(g.scalar_tensor_tensor(out=c.resid[:, i, :], in0=c.psum[:, 7, HID:2 * HID],
                                                       scalar=c.gate[:, 2:3], in1=c.resid[:, i, :], op0=ALU.mult,
                                                       op1=ALU.add))
                    chain.after(g.tensor_tensor(c.resid[:, i, :], c.resid[:, i, :], bp[:], ALU.add))
                    dve.sem_inc(y_added, 1)
                    assert chain.n == per, (chain.n, per)

            @block.gpsimd
            def _(pool):
                with pool.Fori(0, NT) as i:
                    for h in range(H):
                        pool.wait_ge(exp_done, i * H + h + 1)
                        pool.wait_ge(small_done, i * H + h)
                        nc.gpsimd.tensor_tensor(small[:], c.mhalf[:, 0:1], c.mhalf[:, 0:1], ALU.add
                                                ).then_inc(small_done, 1)
                        nc.gpsimd.tensor_scalar(pi[:, h % 2, :], e[:, h % 2, :], ROUND, ROUND, ALU.add, ALU.subtract
                                                ).then_inc(rounded, 1)


STAGES = tuple(range(8))


def build(nc, dram, out):
    stages = (attn0, ffn0, attn1, ffn1, attn2, ffn2, attn3, ffn3)
    with ExitStack() as ctx:
        c = Core(nc, ctx, dram)
        with c.new_stage():
            start(c)
        for s in STAGES:
            with c.new_stage():
                stages[s](c)
        with c.new_stage():
            finish(c, out)



def laid_out(i):
    c = np.ascontiguousarray
    a = {n: np.asarray(v) for n, v in i.items()}
    o = {}

    def rows(w):
        return c(w.reshape(KC, P, -1).transpose(1, 0, 2))

    def gu(g, u):
        w = np.concatenate([g, u], axis=2)
        return c(w.reshape(len(g), KC, P, -1).transpose(0, 2, 1, 3))

    def cols(w, f):
        return w.reshape(HID, -1, f).transpose(1, 0, 2)

    o["x"] = c(a["x"].reshape(TOK, HID))
    o["ctx_2048"] = c(a["ctx_2048"].reshape(TOK, HID))
    o["g_xattn"], o["g_ffn"] = a["g_xattn"], a["g_ffn"]
    o["L0_router"] = rows(a["L0_ffn_gate_weight"].T)
    o["L0_ffn_similarity"] = a["L0_ffn_similarity"]
    w = a["L0_ffn_gate_up_proj"].transpose(0, 2, 1)
    o["L0_gu"] = gu(w[:, :, :96], w[:, :, 96:])
    o["L0_dn"] = c(a["L0_ffn_down_proj"].transpose(0, 2, 1))
    o["L1_gu"] = gu(cols(a["L1_ffn_gate_w"].T, 88), cols(a["L1_ffn_up_w"].T, 88))
    o["L1_dn"] = c(np.concatenate([a["L1_ffn_down_w"].T, a["L1_ffn_gate_s"][:, None], a["L1_ffn_up_s"][:, None]],
                                  axis=1).reshape(8, 88, HID + 2))
    o["L1_ffn_down_s"] = a["L1_ffn_down_s"]
    o["L2_router"] = rows(a["L2_ffn_gate_w"].T)

    def halves(w, n):
        e, h, f = w.shape
        return w.reshape(e, h, n, f // n).transpose(0, 2, 1, 3).reshape(e * n, h, f // n)

    o["L2_gu"] = gu(halves(a["L2_ffn_w_gate"], 2), halves(a["L2_ffn_w_up"], 2))
    o["L2_dn"] = c(a["L2_ffn_w_down"].reshape(32, 88, HID))
    o["L2s_gu"] = gu(cols(a["L2_ffn_sw_gate"], 88), cols(a["L2_ffn_sw_up"], 88))
    o["L2s_dn"] = c(a["L2_ffn_sw_down"].reshape(4, 88, HID))
    o["L3_router"] = rows(a["L3_ffn_router_w"].T)
    w = a["L3_ffn_gate_up_proj"]
    o["L3_gu"] = gu(halves(w[:, :, :512], 4), halves(w[:, :, 512:], 4))
    o["L3_dn"] = c(a["L3_ffn_down_proj"].reshape(32, 128, HID))
    o["L3s_gu"] = gu(cols(a["L3_ffn_shared_gate_w"], 128), cols(a["L3_ffn_shared_up_w"], 128))
    o["L3s_dn"] = c(a["L3_ffn_shared_down_w"].reshape(4, 128, HID))

    o["L0_wq"], o["L0_wk"], o["L0_wv"] = rows(a["L0_xattn_Wq"]), rows(a["L0_xattn_Wk"]), rows(a["L0_xattn_Wv"])
    o["L0_wo"] = c(a["L0_xattn_Wo"].reshape(NH, P, HID).transpose(1, 0, 2))
    for n in ("L0_xattn_bq", "L0_xattn_bk", "L0_xattn_bv", "L1_xattn_gn_gamma", "L1_xattn_gn_beta"):
        o[n] = a[n]
    o["L0_norms"] = c(np.stack([a["L0_xattn_qn_w"], a["L0_xattn_kn_w"]], axis=1))
    o["mask"] = c(a["mask_1xSxS2_ff0"][0])
    o["L1_wh"] = c(a["L1_xattn_Wh"].transpose(1, 0, 2))
    o["L1_wg"], o["L1_wo"] = rows(a["L1_xattn_wg_w"]), rows(a["L1_xattn_wo_w"])
    o["L1_decay"] = decay_by_key()
    for n in ("wq", "wqx", "wk", "wv"):
        o["L3_" + n] = rows(a["L3_xattn_" + n].T)
    o["L3_wkvx"] = rows(a["L3_xattn_w_kv_x"].T)
    o["L3_wproj"] = c(a["L3_xattn_wproj"].T.reshape(2 * NH, P, HID).transpose(1, 0, 2))
    o["L3_ln"] = c(np.stack([a["L3_xattn_ln_w"], a["L3_xattn_ln_b"]]).reshape(2, KC, P).transpose(2, 0, 1))
    o["L3_in_scale"] = c(np.stack([a["L3_xattn_" + n + "_in_scale"] for n in ("q", "k", "v", "qx")])
                         .reshape(4, KC, P).transpose(2, 0, 1))
    o["L3_norms"] = c(np.stack([np.stack([a[f"L3_xattn_{n}ln_w"], a[f"L3_xattn_{n}ln_b"]])
                                for n in ("q", "k", "qx", "kx")]).transpose(2, 0, 1))
    o["L3_smooth"] = c(a["L3_xattn_proj_smooth"].reshape(2 * NH, P).T)
    for n in ("wq_scale", "wk_scale", "wv_scale", "wqx_scale", "proj_w_scale", "proj_in_scale"):
        o["L3_xattn_" + n] = c(a["L3_xattn_" + n].reshape(1))
    o["L2_wq"], o["L2_wkv"], o["L2_wp"] = (rows(a["L2_xattn_" + n]) for n in ("Wq", "Wkv", "Wp"))
    o["L2_xattn_bq"], o["L2_xattn_bp"], o["L2_bk"] = a["L2_xattn_bq"], a["L2_xattn_bp"], a["L2_xattn_bkv"][:HID]
    o["L2_bv"] = c(a["L2_xattn_bkv"][HID:].reshape(KC, P).T)
    return o


def kernel(**inputs):
    import concourse.bacc as bacc
    from concourse.bass_utils import run_bass_kernel_spmd

    nc = bacc.Bacc("TRN2", target_bir_lowering=False, num_devices=1)
    arrays, dram = {}, {}
    for name, a in laid_out(inputs).items():
        a = np.ascontiguousarray(a)
        arrays[f"in_{name}"] = a
        dram[name] = nc.dram_tensor(f"in_{name}", a.shape, mybir.dt.from_np(a.dtype), kind="ExternalInput").ap()
    out = nc.dram_tensor("out", (TOK, HID), F32, kind="ExternalOutput").ap()
    build(nc, dram, out)
    r = run_bass_kernel_spmd(nc, [arrays], core_ids=[0])
    return r.results[0]["out"].reshape(BATCH, SEQ, HID)
```

```python
from contextlib import ExitStack, contextmanager

import numpy as np

import concourse.bass as bass
from concourse import mybir

F32 = mybir.dt.float32
BF16 = mybir.dt.bfloat16
U16 = mybir.dt.uint16
U32 = mybir.dt.uint32
ALU = mybir.AluOpType
ACT = mybir.ActivationFunctionType
X, XY = mybir.AxisListType.X, mybir.AxisListType.XY

P = 128
BATCH, SEQ, HID = 16, 64, 256
TOK = BATCH * SEQ
NT = TOK // P
KC = HID // P
HD = 128
NH = 16
HALF = TOK // 2
ROUND = 1.5 * 2.0 ** 23
FP8_LEAST = 1.5 * 2.0 ** -6
FP8_STEP = 2.0 ** 20


class Chain:

    def __init__(self, eng, sem, base=0):
        self.eng, self.sem, self.base, self.n, self.per = eng, sem, base, 0, 0

    def add(self, ins):
        self.n += 1
        ins.then_inc(self.sem, 1)

    def join(self):
        self.eng.wait_ge(self.sem, self.base + self.n)

    def after(self, ins):
        self.add(ins)
        self.join()


class Core:

    def __init__(self, nc, ctx, dram):
        self.nc, self.dram, self.count = nc, dram, 0
        self.live = ctx
        self.psum = ctx.enter_context(nc.psum_tensor("psum", [P, 8, 512], F32))
        self.resid = self.sb(ctx, "resid", [P, NT, HID])
        self.norm = self.sb(ctx, "norm", [P, NT, HID])
        self.xT = self.sb(ctx, "xT", [P, KC, TOK])
        self.ctxT = self.sb(ctx, "ctxT", [P, KC, TOK])
        self.ident = self.sb(ctx, "ident", [P, P])
        self.identb = self.sb(ctx, "identb", [P, P], BF16)
        self.gate = self.sb(ctx, "gate", [P, 8])
        self.stats = self.sb(ctx, "stats", [P, NT, 6])
        self.mv = self.sb(ctx, "mv", [P, NT, 2])
        self.ve = self.sb(ctx, "ve", [P, NT])
        self.rstd = self.sb(ctx, "rstd", [P, NT])
        self.mhalf = self.sb(ctx, "mhalf", [P, 64])

    def sb(self, ctx, name, shape, dt=F32):
        self.count += 1
        return ctx.enter_context(self.nc.sbuf_tensor(f"{name}_{self.count}", shape, dt))

    def sem(self, ctx, name):
        self.count += 1
        s = self.stage.enter_context(self.nc.semaphore(f"{name}_{self.count}"))
        self.used.append(s)
        return s

    @contextmanager
    def new_stage(self):
        with ExitStack() as self.stage:
            self.used = []
            yield
            with self.nc.Block() as block:
                @block.gpsimd
                def _(pool):
                    nums = [s.num for s in self.used]
                    pool.sem_clear(range(min(nums), max(nums) + 1))


def bc(ap, shape):
    return ap.unsqueeze(len(ap.shape)).to_broadcast(shape)



def start(c):
    nc, d = c.nc, c.dram
    with ExitStack() as st:
        x_in, ctx_in, gates_in, ident_set, ident_ready, gates_ready, consts = (c.sem(st, n) for n in (
            "x_in", "ctx_in", "gates_in", "ident_set", "ident_ready", "gates_ready", "consts"))
        raw = c.sb(st, "gate_raw", [P, 8])
        with nc.Block() as block:
            @block.sync
            def _(sp):
                sp.dma_start(c.norm[:], d["ctx_2048"].rearrange("(t p) d -> p t d", p=P)).then_inc(ctx_in, 16)
                sp.dma_start(c.resid[:], d["x"].rearrange("(t p) d -> p t d", p=P)).then_inc(x_in, 16)
                sp.wait_ge(x_in, 16)

            @block.scalar
            def _(act):
                act.dma_start(raw[:, 0:4], d["g_xattn"].partition_broadcast(P)).then_inc(gates_in, 16)
                act.dma_start(raw[:, 4:8], d["g_ffn"].partition_broadcast(P)).then_inc(gates_in, 16)
                act.wait_ge(gates_in, 32)
                nc.scalar.activation(c.gate[:], raw[:], ACT.Tanh).then_inc(gates_ready, 1)
                act.wait_ge(ctx_in, 16)

            @block.vector
            def _(dve):
                nc.vector.memset(c.mhalf[:], -0.5).then_inc(consts, 1)

            @block.gpsimd
            def _(pool):
                nc.gpsimd.memset(c.ident[:], 0.0).then_inc(ident_set, 1)
                pool.wait_ge(ident_set, 1)
                nc.gpsimd.affine_select(out=c.ident[:], in_=c.ident[:], compare_op=ALU.not_equal, fill=1.0, base=0,
                                        pattern=[[-1, P]], channel_multiplier=1).then_inc(ident_set, 1)
                pool.wait_ge(ident_set, 2)
                nc.gpsimd.tensor_copy(c.identb[:], c.ident[:]).then_inc(ident_ready, 1)
        transpose_tokens(c, c.norm, c.ctxT)


def finish(c, out):
    nc = c.nc
    with ExitStack() as st:
        stored = c.sem(st, "stored")
        with nc.Block() as block:
            @block.sync
            def _(sp):
                sp.dma_start(out.rearrange("(t p) d -> p t d", p=P), c.resid[:]).then_inc(stored, 16)
                sp.wait_ge(stored, 16)



def pe_transpose_tokens(c, pe, src, ready, transposed):
    for t in range(NT):
        if ready is not None:
            pe.wait_ge(ready, t + 1)
        for k in range(KC):
            last = c.nc.tensor.transpose(c.psum[:, t // 2, k * 256 + t % 2 * P:k * 256 + t % 2 * P + P],
                                         src[:, t, k * P:(k + 1) * P], c.ident[:])
        last.then_inc(transposed, 1)


def act_store_transposed(c, act, dst, transposed, stored):
    for g in range(NT // 2):
        act.wait_ge(transposed, 2 * g + 2)
        c.nc.scalar.activation(dst[:, :, g * 256:(g + 1) * 256],
                               c.psum[:, g, :].rearrange("p (k n) -> p k n", k=KC), ACT.Copy).then_inc(stored, 1)


def transpose_tokens(c, src, dst):
    nc = c.nc
    with ExitStack() as st:
        transposed, stored = c.sem(st, "transposed"), c.sem(st, "stored")
        with nc.Block() as block:
            @block.tensor
            def _(pe):
                pe_transpose_tokens(c, pe, src, None, transposed)

            @block.scalar
            def _(act):
                act_store_transposed(c, act, dst, transposed, stored)


def layernorm(c, src, dst, dstT, eps=1e-5):
    nc = c.nc
    with ExitStack() as st:
        chain_s, var_ready, rstd_ready, norm_ready, transposed, stored = (c.sem(st, n) for n in (
            "ln_chain", "var_ready", "rstd_ready", "norm_ready", "transposed", "stored"))
        with nc.Block() as block:
            @block.vector
            def _(dve):
                chain = Chain(dve, chain_s)
                for t in range(NT):
                    chain.add(nc.vector.bn_stats(c.stats[:, t, :], src[:, t, :]))
                chain.join()
                for t in range(NT):
                    chain.add(nc.vector.bn_aggr(c.mv[:, t, :], c.stats[:, t, :]))
                chain.join()
                nc.vector.tensor_scalar(c.ve[:], c.mv[:, :, 1], eps, None, ALU.add).then_inc(var_ready, 1)
                dve.wait_ge(rstd_ready, 1)
                for t in range(NT):
                    nc.vector.tensor_scalar(dst[:, t, :], src[:, t, :], c.mv[:, t, 0:1], c.rstd[:, t:t + 1],
                                            ALU.subtract, ALU.mult).then_inc(norm_ready, 1)

            @block.gpsimd
            def _(pool):
                pool.wait_ge(var_ready, 1)
                nc.gpsimd.tensor_tensor(c.rstd[:], c.ve[:], c.mhalf[:, 0:NT], ALU.pow).then_inc(rstd_ready, 1)

            if dstT is not None:
                @block.tensor
                def _(pe):
                    pe_transpose_tokens(c, pe, dst, norm_ready, transposed)

                @block.scalar
                def _(act):
                    act_store_transposed(c, act, dstT, transposed, stored)



def ffn(c, name, chunks, f, xT, acc, comb=None, per_expert=1, scaled=False):
    nc, d = c.nc, c.dram
    unroll = max(2, per_expert)
    wdn = HID + (2 if scaled else 0)
    with ExitStack() as st:
        gu_in = [c.sem(st, f"gu_in{b}") for b in range(2)]
        dn_in = [c.sem(st, f"dn_in{b}") for b in range(2)]
        gu_ready, act_ready, h_ready, dn_ready, acc_done = (c.sem(st, n) for n in (
            "gu_ready", "act_ready", "h_ready", "dn_ready", "acc_done"))
        wgu = c.sb(st, "wgu", [P, 2, KC, 2 * f])
        wd = c.sb(st, "wd", [f, 2, wdn])
        sg = c.sb(st, "silu", [f, 2, HALF])
        hT = c.sb(st, "hT", [f, 2, HALF])
        with nc.Block() as block:
            @block.sync
            def _(sp):
                sp.sem_inc(dn_ready, 4)
                with sp.Fori(0, chunks // unroll) as i:
                    for u in range(unroll):
                        j, b = unroll * i + u, u % 2
                        sp.wait_ge(dn_ready, 2 * j + 2)
                        sp.dma_start(wgu[:, b], d[name + "_gu"][bass.ds(j, 1)].rearrange("o p k f -> p (o k) f")
                                     ).then_inc(gu_in[b], 16)
                        sp.dma_start(wd[:, b], d[name + "_dn"][bass.ds(j, 1)].rearrange("o p k -> p (o k)")
                                     ).then_inc(dn_in[b], 16)

            @block.tensor
            def _(pe):
                with pe.Fori(0, chunks // unroll) as i:
                    for c_ in range(unroll):
                        j, b = unroll * i + c_, c_ % 2
                        landed = 16 * (unroll // 2 * i + c_ // 2 + 1)
                        pe.wait_ge(gu_in[b], landed)
                        for half in range(2):
                            pe.wait_ge(h_ready, 2 * j + half + 1)
                            for u in range(2):
                                for k in range(KC):
                                    last = nc.tensor.matmul(c.psum[0:f, 2 * half + u, :],
                                                            wgu[:, b, k, u * f:(u + 1) * f],
                                                            xT[:, k, half * HALF:(half + 1) * HALF],
                                                            start=k == 0, stop=k == KC - 1)
                            last.then_inc(gu_ready, 1)
                        pe.wait_ge(dn_in[b], landed)
                        for half in range(2):
                            pe.wait_ge(h_ready, 2 * j + half + 3)
                            pe.wait_ge(acc_done, 2 * j + half + 1)
                            for q in range(4):
                                last = nc.tensor.matmul(c.psum[:, 4 + 2 * half + q // 2,
                                                               q % 2 * HID:(q % 2 + 1) * HID],
                                                        hT[:, half, q * P:(q + 1) * P], wd[:, b, 0:HID],
                                                        start=True, stop=True)
                            last.then_inc(dn_ready, 1)

            @block.scalar
            def _(act):
                with act.Fori(0, chunks // unroll) as i:
                    for u in range(unroll):
                        j, b = unroll * i + u, u % 2
                        if scaled:
                            act.wait_ge(dn_in[b], 16 * (unroll // 2 * i + u // 2 + 1))
                        for half in range(2):
                            act.wait_ge(gu_ready, 2 * j + half + 1)
                            act.wait_ge(h_ready, 2 * j + half + 1)
                            scale = wd[:, b, HID:HID + 1] if scaled else 1.0
                            nc.scalar.activation(sg[:, half], c.psum[0:f, 2 * half, :], ACT.Silu,
                                                 scale=scale).then_inc(act_ready, 1)

            @block.vector
            def _(dve):
                dve.sem_inc(h_ready, 2)
                dve.sem_inc(acc_done, 2)
                with dve.Fori(0, chunks // unroll) as i:
                    for u in range(unroll):
                        j, b = unroll * i + u, u % 2
                        for half in range(2):
                            dve.wait_ge(act_ready, 2 * j + half + 1)
                            dve.wait_ge(dn_ready, 2 * j + 4)
                            if scaled:
                                ins = nc.vector.scalar_tensor_tensor(
                                    out=hT[:, half], in0=c.psum[0:f, 2 * half + 1, :],
                                    scalar=wd[:, b, HID + 1:HID + 2], in1=sg[:, half], op0=ALU.mult, op1=ALU.mult)
                            else:
                                ins = nc.vector.tensor_tensor(hT[:, half], c.psum[0:f, 2 * half + 1, :], sg[:, half],
                                                              ALU.mult)
                            ins.then_inc(h_ready, 1)
                        for half in range(2):
                            dve.wait_ge(dn_ready, 2 * j + half + 5)
                            dve.wait_ge(acc_done, 2 * j + half + 1)
                            for q in range(4):
                                t = 4 * half + q
                                dn = c.psum[:, 4 + 2 * half + q // 2, q % 2 * HID:(q % 2 + 1) * HID]
                                if comb is None:
                                    if q % 2:
                                        continue
                                    dn = c.psum[:, 4 + 2 * half + q // 2, :].rearrange("p (t n) -> p t n", t=2)
                                    last = nc.vector.tensor_tensor(acc[:, t:t + 2, :], dn, acc[:, t:t + 2, :], ALU.add)
                                else:
                                    e = j if per_expert == 1 else i
                                    last = nc.vector.scalar_tensor_tensor(
                                        out=acc[:, t, :], in0=dn, scalar=comb[:, t, bass.ds(e, 1)],
                                        in1=acc[:, t, :], op0=ALU.mult, op1=ALU.add)
                            last.then_inc(acc_done, 1)


def zero(c, *bufs):
    nc = c.nc
    with ExitStack() as st:
        cleared = c.sem(st, "cleared")
        with nc.Block() as block:
            @block.gpsimd
            def _(pool):
                for b in bufs:
                    nc.gpsimd.memset(b[:], 0.0).then_inc(cleared, 1)


def add_gated(c, acc, gate, col_scale=None):
    nc = c.nc
    with ExitStack() as st:
        scaled_s, added = c.sem(st, "scaled"), c.sem(st, "added")
        with nc.Block() as block:
            @block.vector
            def _(dve):
                if col_scale is not None:
                    nc.vector.tensor_tensor(acc[:], acc[:], col_scale[:].unsqueeze(1).to_broadcast([P, NT, HID]),
                                            ALU.mult).then_inc(scaled_s, 1)
                    dve.wait_ge(scaled_s, 1)
                nc.vector.scalar_tensor_tensor(out=c.resid[:], in0=acc[:], scalar=c.gate[:, gate:gate + 1],
                                               in1=c.resid[:], op0=ALU.mult, op1=ALU.add).then_inc(added, 1)



def softmax_rows(c, dve, chain, logits, p, small, exp_go, exp_done, n, turn=1):
    v = c.nc.vector
    chain.after(v.tensor_reduce(small[:, 0, :], logits, X, ALU.max))
    v.tensor_tensor(p[:], logits, bc(small[:, 0, :], [P, NT, n]), ALU.subtract).then_inc(exp_go, 1)
    dve.wait_ge(exp_done, turn)
    chain.after(v.tensor_reduce(small[:, 0, :], p[:], X, ALU.add))
    chain.after(v.reciprocal(small[:, 1, :], small[:, 0, :]))
    chain.after(v.tensor_tensor(p[:], p[:], bc(small[:, 1, :], [P, NT, n]), ALU.mult))


def top_onehots(c, chain, values, top, idx, idxf, iota, onehot, k, n):
    v = c.nc.vector
    for t in range(NT):
        chain.add(v.max(top[:, t, :], values[:, t, :]))
    chain.join()
    for t in range(NT):
        chain.add(v.max_index(idx[:, t, :], top[:, t, :], values[:, t, :]))
    chain.join()
    chain.after(v.tensor_copy(idxf[:], idx[:]))
    for i in range(k):
        chain.add(v.tensor_tensor(onehot[:, :, i, :], iota[:].unsqueeze(1).to_broadcast([P, NT, n]),
                                  idxf[:, :, i:i + 1].to_broadcast([P, NT, n]), ALU.is_equal))
    chain.join()


def pe_logits(c, pe, wr, bank, n):
    for t in range(NT):
        for k in range(KC):
            last = c.nc.tensor.matmul(c.psum[:, bank, t * n:(t + 1) * n], c.xT[:, k, t * P:(t + 1) * P],
                                      wr[:, k, :], start=k == 0, stop=k == KC - 1)
    return last


def router0(c, comb):
    nc, d, E, K, S = c.nc, c.dram, 32, 8, 4
    with ExitStack() as st:
        wr_in, sim_in, consts, bd_ready, chain_s, logits_ready, exp_go, exp_done, oh_ready, oh_turned, oh_stored, \
            rows_ready = (c.sem(st, n) for n in (
                "wr_in", "sim_in", "consts", "bd_ready", "chain", "logits_ready", "exp_go", "exp_done", "oh_ready",
                "oh_turned", "oh_stored", "rows_ready"))
        wr = c.sb(st, "wr", [P, KC, E])
        simbd = c.sb(st, "simbd", [P, P])
        iota = c.sb(st, "iota", [P, E])
        p = c.sb(st, "p", [P, NT, E])
        small = c.sb(st, "small", [P, 2, NT])
        top = c.sb(st, "top", [P, NT, K])
        rw = c.sb(st, "rw", [P, NT, K])
        idx = c.sb(st, "idx", [P, NT, K], U32)
        idxf = c.sb(st, "idxf", [P, NT, K])
        oh = c.sb(st, "oh", [P, NT, K, E])
        secT = c.sb(st, "secT", [P, NT, P])
        cand4 = c.sb(st, "cand4", [P, NT, S, E])
        cand = c.sb(st, "cand", [P, NT * S, S])
        best = c.sb(st, "best", [P, NT * S])
        eq = c.sb(st, "eq", [P, NT * S, S])
        seen = c.sb(st, "seen", [P, NT * S])
        moved = c.sb(st, "moved", [P, NT, S])
        coef = c.sb(st, "coef", [P, NT, K])
        add = c.sb(st, "add", [P, NT, S])
        with nc.Block() as block:
            @block.sync
            def _(sp):
                sp.dma_start(wr[:], d["L0_router"]).then_inc(wr_in, 16)
                sp.wait_ge(bd_ready, 1)
                for j in range(S):
                    sp.dma_start(simbd[j * E:(j + 1) * E, j * E:(j + 1) * E],
                                 d["L0_ffn_similarity"]).then_inc(sim_in, 16)

            @block.gpsimd
            def _(pool):
                nc.gpsimd.iota(iota[:], pattern=[[1, E]], base=0, channel_multiplier=0,
                               allow_small_or_imprecise_dtypes=True).then_inc(consts, 1)

            @block.tensor
            def _(pe):
                pe.wait_ge(wr_in, 16)
                pe_logits(c, pe, wr, 0, E).then_inc(logits_ready, 1)
                pe.wait_ge(oh_ready, 1)
                for t in range(NT):
                    last = nc.tensor.transpose(c.psum[:, 1 + t // 4, t % 4 * P:(t % 4 + 1) * P],
                                               oh[:, t, S:K, :], c.ident[:])
                last.then_inc(oh_turned, 1)
                pe.wait_ge(oh_stored, 2)
                pe.wait_ge(sim_in, 16 * S)
                for t in range(NT):
                    last = nc.tensor.matmul(c.psum[:, 3 + t // 4, t % 4 * P:(t % 4 + 1) * P], secT[:, t, :],
                                            simbd[:], start=True, stop=True)
                last.then_inc(rows_ready, 1)

            @block.scalar
            def _(act):
                act.wait_ge(exp_go, 1)
                nc.scalar.activation(p[:], p[:], ACT.Exp).then_inc(exp_done, 1)
                act.wait_ge(oh_turned, 1)
                for h in range(2):
                    nc.scalar.activation(secT[:, 4 * h:4 * h + 4, :],
                                         c.psum[:, 1 + h, :].rearrange("p (t n) -> p t n", t=4),
                                         ACT.Copy).then_inc(oh_stored, 1)

            @block.vector
            def _(dve):
                v, chain = nc.vector, Chain(dve, chain_s)
                v.memset(simbd[:], 0.0).then_inc(bd_ready, 1)
                dve.wait_ge(logits_ready, 1)
                logits = c.psum[:, 0, 0:NT * E].rearrange("p (t e) -> p t e", t=NT)
                softmax_rows(c, dve, chain, logits, p, small, exp_go, exp_done, E)
                dve.wait_ge(consts, 1)
                top_onehots(c, chain, p, top, idx, idxf, iota, oh, K, E)
                v.tensor_reduce(small[:, 0, :], top[:], X, ALU.add).then_inc(oh_ready, 1)
                dve.wait_ge(oh_ready, 1)
                chain.after(v.tensor_scalar(small[:, 0, :], small[:, 0, :], 1e-12, None, ALU.max))
                chain.after(v.reciprocal(small[:, 1, :], small[:, 0, :]))
                chain.after(v.tensor_tensor(rw[:], top[:], bc(small[:, 1, :], [P, NT, K]), ALU.mult))
                dve.wait_ge(rows_ready, 1)
                for i in range(S):
                    for h in range(2):
                        rows = c.psum[:, 3 + h, :].rearrange("p (t j e) -> p t j e", t=4, j=S)
                        chain.add(v.tensor_tensor(
                            cand4[:, 4 * h:4 * h + 4], rows,
                            oh[:, 4 * h:4 * h + 4, i, :].unsqueeze(2).to_broadcast([P, 4, S, E]), ALU.mult))
                    chain.join()
                    chain.after(v.tensor_reduce(cand[:, :, i], cand4[:].rearrange("p t j e -> p (t j) e"), X, ALU.add))
                chain.after(v.tensor_reduce(best[:], cand[:], X, ALU.max))
                chain.after(v.tensor_tensor(eq[:], cand[:], bc(best[:], [P, NT * S, S]), ALU.is_equal))
                chain.after(v.tensor_copy(seen[:], eq[:, :, 0]))
                for i in range(1, S):
                    chain.after(v.scalar_tensor_tensor(out=eq[:, :, i], in0=seen[:], scalar=0.5, in1=eq[:, :, i],
                                                       op0=ALU.is_lt, op1=ALU.mult))
                    chain.after(v.tensor_tensor(seen[:], seen[:], eq[:, :, i], ALU.max))
                best3 = best[:].rearrange("p (t j) -> p t j", j=S)
                chain.after(v.scalar_tensor_tensor(out=coef[:, :, S:K], in0=best3, scalar=0.5, in1=rw[:, :, S:K],
                                                   op0=ALU.is_lt, op1=ALU.mult))
                chain.after(v.tensor_tensor(moved[:], rw[:, :, S:K], coef[:, :, S:K], ALU.subtract))
                eq4 = eq[:].rearrange("p (t j) i -> p t j i", j=S)
                chain.after(v.tensor_tensor(eq4, eq4, bc(moved[:], [P, NT, S, S]), ALU.mult))
                chain.after(v.tensor_reduce(add[:], eq[:].rearrange("p (t j) i -> p t i j", j=S), X, ALU.add))
                chain.after(v.tensor_tensor(coef[:, :, 0:S], rw[:, :, 0:S], add[:], ALU.add))
                for i in range(K):
                    chain.add(v.tensor_tensor(oh[:, :, i, :], oh[:, :, i, :],
                                              coef[:, :, i:i + 1].to_broadcast([P, NT, E]), ALU.mult))
                chain.join()
                chain.after(v.tensor_reduce(comb[:], oh[:].rearrange("p t k e -> p t e k"), X, ALU.add))


def router2(c, comb):
    nc, d, E, K, CAP = c.nc, c.dram, 16, 4, 128
    with ExitStack() as st:
        wr_in, consts, chain_s, logits_ready, exp_go, exp_done, mask_ready, rank_ready = (c.sem(st, n) for n in (
            "wr_in", "consts", "chain", "logits_ready", "exp_go", "exp_done", "mask_ready", "rank_ready"))
        wr = c.sb(st, "wr", [P, KC, E])
        iota = c.sb(st, "iota", [P, E])
        ones = c.sb(st, "ones", [P, P])
        before = c.sb(st, "before", [P, P])
        p = c.sb(st, "p", [P, NT, E])
        small = c.sb(st, "small", [P, 2, NT])
        top = c.sb(st, "top", [P, NT, 8])
        rw = c.sb(st, "rw", [P, NT, K])
        idx = c.sb(st, "idx", [P, NT, 8], U32)
        idxf = c.sb(st, "idxf", [P, NT, 8])
        oh = c.sb(st, "oh", [P, NT, K, E])
        mask = c.sb(st, "mask", [P, NT, E])
        with nc.Block() as block:
            @block.sync
            def _(sp):
                sp.dma_start(wr[:], d["L2_router"]).then_inc(wr_in, 16)

            @block.gpsimd
            def _(pool):
                nc.gpsimd.iota(iota[:], pattern=[[1, E]], base=0, channel_multiplier=0,
                               allow_small_or_imprecise_dtypes=True).then_inc(consts, 1)
                nc.gpsimd.memset(ones[:], 1.0).then_inc(consts, 1)
                nc.gpsimd.memset(before[:], 1.0).then_inc(consts, 1)
                pool.wait_ge(consts, 3)
                nc.gpsimd.affine_select(out=before[:], in_=before[:], compare_op=ALU.is_gt, fill=0.0, base=0,
                                        pattern=[[1, P]], channel_multiplier=-1).then_inc(consts, 1)

            @block.tensor
            def _(pe):
                pe.wait_ge(wr_in, 16)
                pe_logits(c, pe, wr, 0, E).then_inc(logits_ready, 1)
                pe.wait_ge(consts, 4)
                pe.wait_ge(mask_ready, 1)
                for t in range(NT):
                    for s in range(t + 1):
                        last = nc.tensor.matmul(c.psum[:, 1, t * E:(t + 1) * E], before[:] if s == t else ones[:],
                                                mask[:, s, :], start=s == 0, stop=s == t)
                last.then_inc(rank_ready, 1)

            @block.scalar
            def _(act):
                act.wait_ge(exp_go, 1)
                nc.scalar.activation(p[:], p[:], ACT.Exp).then_inc(exp_done, 1)

            @block.vector
            def _(dve):
                v, chain = nc.vector, Chain(dve, chain_s)
                dve.wait_ge(logits_ready, 1)
                logits = c.psum[:, 0, 0:NT * E].rearrange("p (t e) -> p t e", t=NT)
                softmax_rows(c, dve, chain, logits, p, small, exp_go, exp_done, E)
                dve.wait_ge(consts, 4)
                top_onehots(c, chain, p, top, idx, idxf, iota, oh, K, E)
                v.tensor_reduce(mask[:], oh[:].rearrange("p t k e -> p t e k"), X, ALU.add).then_inc(mask_ready, 1)
                chain.after(v.tensor_reduce(small[:, 0, :], top[:, :, 0:K], X, ALU.add))
                chain.after(v.tensor_scalar(small[:, 0, :], small[:, 0, :], 1e-20, None, ALU.add))
                chain.after(v.reciprocal(small[:, 1, :], small[:, 0, :]))
                chain.after(v.tensor_tensor(rw[:], top[:, :, 0:K], bc(small[:, 1, :], [P, NT, K]), ALU.mult))
                dve.wait_ge(mask_ready, 1)
                for i in range(K):
                    chain.add(v.tensor_tensor(oh[:, :, i, :], oh[:, :, i, :],
                                              rw[:, :, i:i + 1].to_broadcast([P, NT, E]), ALU.mult))
                chain.join()
                chain.after(v.tensor_reduce(comb[:], oh[:].rearrange("p t k e -> p t e k"), X, ALU.add))
                dve.wait_ge(rank_ready, 1)
                rank = c.psum[:, 1, 0:NT * E].rearrange("p (t e) -> p t e", t=NT)
                chain.after(v.scalar_tensor_tensor(out=comb[:], in0=rank, scalar=CAP - 0.5, in1=comb[:],
                                                   op0=ALU.is_lt, op1=ALU.mult))


def router3(c, comb, scaledT):
    nc, d, E = c.nc, c.dram, 8
    with ExitStack() as st:
        wr_in, consts, chain_s, logits_ready, top_ready, exp_done, scaled, turned, stored = (c.sem(st, n) for n in (
            "wr_in", "consts", "chain", "logits_ready", "top_ready", "exp_done", "scaled", "turned", "stored"))
        wr = c.sb(st, "wr", [P, KC, E])
        iota = c.sb(st, "iota", [P, E])
        logits = c.sb(st, "logits", [P, NT, E])
        top = c.sb(st, "top", [P, NT, 8])
        idx = c.sb(st, "idx", [P, NT, 8], U32)
        idxf = c.sb(st, "idxf", [P, NT, 8])
        sig = c.sb(st, "sig", [P, 2, NT])
        oh = c.sb(st, "oh", [P, NT, 1, E])
        with nc.Block() as block:
            @block.sync
            def _(sp):
                sp.dma_start(wr[:], d["L3_router"]).then_inc(wr_in, 16)

            @block.gpsimd
            def _(pool):
                nc.gpsimd.iota(iota[:], pattern=[[1, E]], base=0, channel_multiplier=0,
                               allow_small_or_imprecise_dtypes=True).then_inc(consts, 1)

            @block.tensor
            def _(pe):
                pe.wait_ge(wr_in, 16)
                pe_logits(c, pe, wr, 7, E).then_inc(logits_ready, 1)
                pe_transpose_tokens(c, pe, c.norm, scaled, turned)

            @block.scalar
            def _(act):
                act.wait_ge(top_ready, 1)
                nc.scalar.activation(sig[:, 0, :], top[:, :, 0], ACT.Exp, scale=-1.0).then_inc(exp_done, 1)
                act_store_transposed(c, act, scaledT, turned, stored)

            @block.vector
            def _(dve):
                v, chain = nc.vector, Chain(dve, chain_s)
                dve.wait_ge(logits_ready, 1)
                chain.after(v.tensor_copy(logits[:], c.psum[:, 7, 0:NT * E].rearrange("p (t e) -> p t e", t=NT)))
                dve.wait_ge(consts, 1)
                top_onehots(c, chain, logits, top, idx, idxf, iota, oh, 1, E)
                v.tensor_copy(comb[:], oh[:, :, 0, :]).then_inc(top_ready, 1)
                dve.wait_ge(exp_done, 1)
                chain.after(v.tensor_scalar(sig[:, 1, :], sig[:, 0, :], 1.0, None, ALU.add))
                chain.after(v.reciprocal(sig[:, 0, :], sig[:, 1, :]))
                for t in range(NT):
                    v.tensor_scalar(c.norm[:, t, :], c.norm[:, t, :], sig[:, 0, t:t + 1], None,
                                    ALU.mult).then_inc(scaled, 1)



def ffn0(c):
    layernorm(c, c.resid, c.norm, c.xT)
    with ExitStack() as st:
        comb, acc = c.sb(st, "comb", [P, NT, 32]), c.sb(st, "acc", [P, NT, HID])
        zero(c, acc)
        router0(c, comb)
        ffn(c, "L0", 32, 96, c.xT, acc, comb=comb)
        add_gated(c, acc, 4)


def ffn1(c):
    nc = c.nc
    layernorm(c, c.resid, c.norm, c.xT)
    with ExitStack() as st:
        acc, down_s = c.sb(st, "acc", [P, NT, HID]), c.sb(st, "down_s", [P, HID])
        s_in = c.sem(st, "down_s_in")
        with nc.Block() as block:
            @block.sync
            def _(sp):
                sp.dma_start(down_s[:], c.dram["L1_ffn_down_s"].partition_broadcast(P)).then_inc(s_in, 16)
                sp.wait_ge(s_in, 16)
        zero(c, acc)
        ffn(c, "L1", 8, 88, c.xT, acc, scaled=True)
        add_gated(c, acc, 5, down_s)


def ffn2(c):
    layernorm(c, c.resid, c.norm, c.xT)
    with ExitStack() as st:
        comb, acc = c.sb(st, "comb", [P, NT, 16]), c.sb(st, "acc", [P, NT, HID])
        zero(c, acc)
        router2(c, comb)
        ffn(c, "L2", 32, 88, c.xT, acc, comb=comb, per_expert=2)
        ffn(c, "L2s", 4, 88, c.xT, acc)
        add_gated(c, acc, 6)


def ffn3(c):
    layernorm(c, c.resid, c.norm, c.xT)
    with ExitStack() as st:
        comb, acc = c.sb(st, "comb", [P, NT, 8]), c.sb(st, "acc", [P, NT, HID])
        scaledT = c.sb(st, "scaledT", [P, KC, TOK])
        zero(c, acc)
        router3(c, comb, scaledT)
        ffn(c, "L3", 32, 128, scaledT, acc, comb=comb, per_expert=4)
        ffn(c, "L3s", 4, 128, c.xT, acc)
        add_gated(c, acc, 7)



def order(text):
    steps = []
    for s in text.split():
        name = s.rstrip("'")
        what = name.rstrip("0123456789")
        steps.append((what, int(name[len(what):] or 0), len(s) - len(name)))
    return steps


ORDER0 = {
    "pe": order("P0 R1' P1 P2 A1' P3 T0 P4 T1 T2 F' S0 T3 T4 P5 S1 R0 A0"),
    "act": order("R1' N0 O1' N1 T0 N2 T1 T2 N3 N4 T3 X0 T4 R0 X1 O0"),
    "dve": order("Q1' E0 V0 E1 V1 E2 V2 E3 E4 V3 V4 M0 Q0 E5 F' M1"),
    "pool": order("R1' R2' R3' R4' R0"),
}
ORDER3 = {
    "pe": order("T15' A1' P0 P1 R2' P2 P3 P4 S3' T0 P5 A2' P6 T1 P7 T4 P8 T5 P9 S0 R3' P10 A3' P11 T6 T7 P12 "
               "P13 S1 T8 P14 T9 F' P15 R0 T12 A0 T13 S2 T14 R1"),
    "act": order("T8' T9' N12' E14' N13' X1' E15' R0' T12' N14' T13' N15' T14' R1' X2' E0 E1 T15' E2 N0 R2' E3 "
                "E4 N1 T0 E5 X3' E6 N4 T1 E7 N5 E8 T4 T5 R3' E9 N6 E10 N7 E11 T6 T7 X0 N8 E12 E13 N9"),
    "dve": order("M2' Q2' V0 V1 O1' M3' V4 V5 Q3' O2' V6 V7 V8 V9 M0 O3' Z V12 V13 M1 Q0 V14 Q1 F' V15 O0"),
    "pool": order("R8' R9' R12' R13' R14' R15' R0 R1 R4 R5 R6 R7"),
}


def run_tiles(eng, steps, do, chain=None, before=None):
    def emit(i, now, back):
        if now and before is not None:
            before(i)
        for what, n, of_last in steps:
            if back if of_last else now:
                do[what](i - 1 if of_last else i, n)

    emit(0, True, False)
    first = chain.n if chain is not None else 0
    with eng.Fori(1, NT) as i:
        if chain is not None:
            per = chain.per
            chain.base, chain.n = first + (i - 1) * per, 0
        emit(i, True, True)
        if chain is not None:
            assert chain.n == per, (chain.n, per)
    if chain is not None:
        chain.base, chain.n = first + (NT - 1) * per, 0
    emit(NT, False, True)


def wait(eng, sem, value):
    if not isinstance(value, int) or value > 0:
        eng.wait_ge(sem, value)



def heads_attention(c, steps, sources, blocks, units, kv_heads, eps, w_out, out_scale, mask=None, quant=None):
    nc = c.nc
    ps, G, rms = c.psum, kv_heads, quant is None
    NB, NU = len(blocks), len(units)
    normed = [j for j, b in enumerate(blocks) if b["normed"]]
    NN = len(normed)
    NQ = 4 if NN % 4 == 0 else NN
    per_kv = NH // G
    scale = HD ** -0.5
    with ExitStack() as st:
        (x_ready, proj_ready, evacuated, ve_ready, rstd_ready, norm_ready, turned, stored, scores_ready, exp_go,
         exp_done, probs_ready, pt_turned, pt_stored, o_ready, o_read, a_ready, out_ready, resid_done, dve_chain,
         pool_chain, cleared) = (c.sem(st, n) for n in (
             "x_ready", "proj_ready", "evacuated", "ve_ready", "rstd_ready", "norm_ready", "turned", "stored",
             "scores_ready", "exp_go", "exp_done", "probs_ready", "pt_turned", "pt_stored", "o_ready", "o_read",
             "a_ready", "out_ready", "resid_done", "dve_chain", "pool_chain", "cleared"))
        src = {n: c.sb(st, "src", [P, KC, P]) for n in sources} if quant is None else {
            "ctx": c.sb(st, "src", [P, KC, P])}
        if quant is not None:
            xq = c.sb(st, "xq", [P, 4, KC, P])
            xq_next = c.sb(st, "xq_next", [P, 4, KC, P])
            xb = c.sb(st, "xb", [P, 4, KC, P], BF16)
            xbig = c.sb(st, "xbig", [P, 4, KC, P], BF16)
            yo = c.sb(st, "yo", [P, 1024])
            yb = c.sb(st, "yb", [P, 1024], BF16)
            ybig = c.sb(st, "ybig", [P, 1024], BF16)
            src.update({n: xq[:, s] for s, n in enumerate(("q", "k", "v", "qx"))})
        qs = c.sb(st, "qs", [P, NQ, 512])
        st6 = c.sb(st, "st6", [P, NQ, 4, 6])
        tmp = c.sb(st, "tmph", [P, NQ, 4, 3])
        neg_mean = c.sb(st, "neg_mean", [P, NQ, 4])
        shift = c.sb(st, "shift", [P, NQ, 4])
        ve = c.sb(st, "veh", [P, NQ, 4])
        rstd = c.sb(st, "rstdh", [P, NQ, 4])
        probs = c.sb(st, "probs", [P, 2, 512])
        diagonal = per_kv == 2
        probsT = c.sb(st, "probsT", [P, 2, 4, 2, P] if diagonal else [P, 2, 512])
        mx = c.sb(st, "mx", [P, 2, 2, 8])
        attnT = c.sb(st, "attnT", [P, NH * NU // 2, P])

        with nc.Block() as block:
            @block.tensor
            def _(pe):
                def project(i, j):
                    b = blocks[j]
                    if j == 0:
                        pe.wait_ge(x_ready, i + 1)
                    wait(pe, evacuated, i * NB + j - 1)
                    for k in range(KC):
                        last = nc.tensor.matmul(ps[:, j % 2, :], src[b["src"]][:, k, :], b["w"][:, k, :],
                                                start=k == 0, stop=k == KC - 1)
                    last.then_inc(proj_ready, 1)

                def turn(i, j):
                    n = normed.index(j)
                    pe.wait_ge(norm_ready, i * NN + n + 1)
                    wait(pe, stored, i * NN + n - 1 + (n == 0 and NN % 2))
                    for h in range(4):
                        last = nc.tensor.transpose(ps[:, 2 + n % 2, h * P:(h + 1) * P],
                                                   qs[:, n % NQ, h * HD:(h + 1) * HD], c.ident[:])
                    last.then_inc(turned, 1)

                def scores(i, u):
                    qT, kT = units[u]["qT"], units[u]["kT"]
                    pe.wait_ge(stored, i * NN + 1 + max(normed.index(j) for j in units[u]["needs"]))
                    wait(pe, exp_go, i * NU + u)
                    for pair in range(4):
                        head = 8 * (u % 2) + 2 * pair
                        for r in range(2):
                            last = nc.tensor.matmul(
                                ps[:, 4, (pair * 2 + r) * 64:(pair * 2 + r + 1) * 64],
                                qT[:, r, head:head + 2, :],
                                kT[:, head // per_kv, r * 64:(r + 1) * 64], start=True, stop=True)
                    last.then_inc(scores_ready, 1)

                def turn_probs(i, u):
                    pe.wait_ge(probs_ready, i * NU + u + 1)
                    wait(pe, pt_stored, i * NU + u)
                    if u == 0:
                        wait(pe, resid_done, i)
                    for pair in range(4):
                        last = nc.tensor.transpose(ps[:, 5, pair * P:(pair + 1) * P],
                                                   probs[:, u % 2, pair * P:(pair + 1) * P], c.ident[:])
                    last.then_inc(pt_turned, 1)

                def values(i, u):
                    v = units[u]["v"]
                    pe.wait_ge(pt_stored, i * NU + u + 1)
                    if diagonal and isinstance(i, int):
                        pe.wait_ge(cleared, 1)
                    pe.wait_ge(evacuated, i * NB + 1 + units[u]["v_block"])
                    wait(pe, o_read, i * NU + u)
                    if diagonal:
                        for pair in range(4):
                            g = 4 * (u % 2) + pair
                            last = nc.tensor.matmul(ps[:, 6 + pair // 2, pair % 2 * 256:(pair % 2 + 1) * 256],
                                                    v[:, g * HD:(g + 1) * HD], probsT[:, u % 2, pair], start=True,
                                                    stop=True)
                        last.then_inc(o_ready, 1)
                        return
                    span = per_kv // 2
                    for r in range(2):
                        for pair in range(0, 4, span):
                            g = (8 * (u % 2) + 2 * pair) // per_kv
                            last = nc.tensor.matmul(
                                ps[:, 6 + r, pair * P:(pair + span) * P],
                                v[r * 64:(r + 1) * 64, g * HD:(g + 1) * HD],
                                probsT[r * 64:(r + 1) * 64, u % 2, pair * P:(pair + span) * P],
                                start=True, stop=True)
                    last.then_inc(o_ready, 1)

                def output(i, _):
                    pe.wait_ge(a_ready, (i + 1) * NU)
                    if quant is None:
                        pe.wait_ge(o_read, (i + 1) * NU)
                    pe.wait_ge(pt_stored, (i + 1) * NU)
                    n = NH * NU // 2
                    for h in range(n):
                        last = nc.tensor.matmul(ps[:, 5, 0:HID], attnT[:, h, :], w_out[:, h, :],
                                                start=h == 0, stop=h == n - 1)
                    last.then_inc(out_ready, 1)

                run_tiles(pe, steps["pe"],
                          {"P": project, "T": turn, "S": scores, "R": turn_probs, "A": values, "F": output})

            @block.scalar
            def _(act):
                def evacuate(i, j):
                    b = blocks[j]
                    act.wait_ge(proj_ready, i * NB + j + 1)
                    dst = qs[:, normed.index(j) % NQ, :] if b["normed"] else b["dst"]
                    nc.scalar.activation(dst, ps[:, j % 2, :], ACT.Copy,
                                         scale=1.0 if b["scale"] is None else b["scale"]).then_inc(evacuated, 1)

                def normalise(i, j):
                    n = normed.index(j)
                    act.wait_ge(rstd_ready, i * NN + n + 1)
                    act.wait_ge(evacuated, i * NB + j + 1)
                    for h in range(4):
                        part, s = qs[:, n % NQ, h * HD:(h + 1) * HD], rstd[:, n % NQ, h:h + 1]
                        if rms:
                            last = nc.scalar.activation(part, part, ACT.Copy, scale=s)
                        else:
                            last = nc.scalar.activation(part, part, ACT.Identity, scale=s, bias=shift[:, n % NQ, h:h + 1])
                    last.then_inc(norm_ready, 1)

                def store(i, j):
                    n, b = normed.index(j), blocks[j]
                    act.wait_ge(turned, i * NN + n + 1)
                    nc.scalar.activation(b["dst"], ps[:, 2 + n % 2, :].rearrange("p (h r n) -> p h r n", h=4, r=2),
                                         ACT.Identity, scale=b["wT"],
                                         bias=0.0 if b["bT"] is None else b["bT"]).then_inc(stored, 1)

                def exps(i, u):
                    act.wait_ge(exp_go, i * NU + u + 1)
                    nc.scalar.activation(probs[:, u % 2, :], probs[:, u % 2, :], ACT.Exp,
                                         scale=scale if mask is None else 1.0).then_inc(exp_done, 1)

                def store_probs(i, u):
                    act.wait_ge(pt_turned, i * NU + u + 1)
                    if diagonal:
                        for r in range(2):
                            rows = slice(64 * r, 64 * r + 64)
                            last = nc.scalar.activation(probsT[rows, u % 2, :, r, :],
                                                        ps[rows, 5, :].rearrange("p (h n) -> p h n", h=4), ACT.Copy)
                        last.then_inc(pt_stored, 1)
                    else:
                        nc.scalar.activation(probsT[:, u % 2, :], ps[:, 5, :], ACT.Copy).then_inc(pt_stored, 1)

                def store_out(i, u):
                    act.wait_ge(o_ready, i * NU + u + 1)
                    for r in range(2):
                        nc.scalar.activation(attnT[:, 8 * u:8 * u + 8, r * 64:(r + 1) * 64],
                                             ps[:, 6 + r, :].rearrange("p (h n) -> p h n", h=8),
                                             ACT.Copy).then_inc(o_read if r else a_ready, 1)

                run_tiles(act, steps["act"], {"E": evacuate, "N": normalise, "T": store, "X": exps, "R": store_probs,
                                              "O": store_out})

            @block.vector
            def _(dve):
                v = nc.vector

                def evacuate(i, j):
                    b = blocks[j]
                    dve.wait_ge(proj_ready, i * NB + j + 1)
                    dst = qs[:, normed.index(j) % NQ, :] if b["normed"] else b["dst"]
                    v.tensor_tensor(dst, ps[:, j % 2, :], b["bias"], ALU.add).then_inc(evacuated, 1)

                def variance(i, j):
                    b = normed.index(j) % NQ
                    dve.wait_ge(evacuated, i * NB + j + 1)
                    for h in range(4):
                        chain.add(v.bn_stats(st6[:, b, h, :], qs[:, b, h * HD:(h + 1) * HD]))
                    chain.join()
                    even, odd, t = st6[:, b, :, 1:3], st6[:, b, :, 4:6], tmp[:, b]
                    chain.add(v.tensor_tensor(t[:, :, 0:2], even, odd, ALU.add))
                    chain.after(v.tensor_tensor(t[:, :, 2], even[:, :, 0], odd[:, :, 0], ALU.subtract))
                    chain.add(v.scalar_tensor_tensor(out=t[:, :, 2], in0=t[:, :, 2], scalar=0.25, in1=t[:, :, 2],
                                                     op0=ALU.mult, op1=ALU.mult))
                    if rms:
                        chain.add(v.scalar_tensor_tensor(out=t[:, :, 0], in0=t[:, :, 0], scalar=0.25,
                                                         in1=t[:, :, 0], op0=ALU.mult, op1=ALU.mult))
                    else:
                        chain.add(v.tensor_scalar(neg_mean[:, b, :], t[:, :, 0], -0.5, None, ALU.mult))
                    chain.after(v.tensor_scalar(t[:, :, 1], t[:, :, 1], 1.0 / HD, eps, ALU.mult, ALU.add))
                    if rms:
                        chain.after(v.tensor_tensor(t[:, :, 2], t[:, :, 2], t[:, :, 0], ALU.add))
                    v.tensor_tensor(ve[:, b, :], t[:, :, 1], t[:, :, 2], ALU.add).then_inc(ve_ready, 1)

                def less_max(i, u):
                    dve.wait_ge(scores_ready, i * NU + u + 1)
                    s = ps[:, 4, :].rearrange("p (g k) -> p g k", k=64)
                    p, top = probs[:, u % 2, :].rearrange("p (g k) -> p g k", k=64), mx[:, u % 2, 0, :]
                    if mask is not None:
                        chain.after(v.scalar_tensor_tensor(out=p, in0=s, scalar=scale,
                                                           in1=mask[:].unsqueeze(1).to_broadcast([P, 8, 64]),
                                                           op0=ALU.mult, op1=ALU.add))
                        s = p
                    chain.after(v.tensor_reduce(top, s, X, ALU.max))
                    v.tensor_tensor(p, s, bc(top, [P, 8, 64]), ALU.subtract).then_inc(exp_go, 1)

                def normalise_probs(i, u):
                    dve.wait_ge(exp_done, i * NU + u + 1)
                    p = probs[:, u % 2, :].rearrange("p (g k) -> p g k", k=64)
                    chain.after(v.tensor_reduce(mx[:, u % 2, 0, :], p, X, ALU.add))
                    chain.after(v.reciprocal(mx[:, u % 2, 1, :], mx[:, u % 2, 0, :]))
                    v.tensor_tensor(p, p, bc(mx[:, u % 2, 1, :], [P, 8, 64]), ALU.mult).then_inc(probs_ready, 1)

                def quantise_out(i, u):
                    dve.wait_ge(o_ready, i * NU + u + 1)
                    wait(dve, a_ready, i * NU + u)
                    rows = ps[:, 6:8, :].rearrange("p b (q r m) -> p (b q) r m", q=2, r=2)
                    for r in range(2):
                        v.tensor_tensor(yo[:, r * 512:(r + 1) * 512].rearrange("p (q h n) -> p q h n", q=4, h=2),
                                        rows[:, :, r, :].rearrange("p q (h n) -> p q h n", h=2),
                                        bc(quant["smooth"][:, 8 * u:8 * u + 8].rearrange("p (q h) -> p q h", h=2),
                                           [P, 4, 2, 64]), ALU.mult).then_inc(o_read if r else dve_chain, 1)
                    chain.n += 1
                    chain.join()
                    dve.wait_ge(o_read, i * NU + u + 1)
                    chain.after(v.tensor_scalar(yb[:], yo[:], -448.0, 448.0, ALU.max, ALU.min))
                    chain.after(v.tensor_scalar(ybig[:].bitcast(U16), yb[:].bitcast(U16), 0x7FFF, None,
                                                ALU.bitwise_and))
                    chain.after(v.tensor_scalar(ybig[:], ybig[:], FP8_LEAST, FP8_STEP, ALU.max, ALU.mult))
                    chain.after(v.tensor_tensor(yo[:], yb[:], ybig[:], ALU.add))
                    v.tensor_tensor(attnT[:, 8 * u:8 * u + 8, :].rearrange("p h (r n) -> p r h n", r=2),
                                    yo[:].rearrange("p (r h n) -> p r h n", r=2, h=8),
                                    ybig[:].rearrange("p (r h n) -> p r h n", r=2, h=8),
                                    ALU.subtract).then_inc(a_ready, 1)

                def next_inputs(tile):
                    chain.after(v.tensor_tensor(xq_next[:], sources["x"][:, :, tile].unsqueeze(1).to_broadcast(
                        [P, 4, KC, P]), bc(quant["in_inv"][:], [P, 4, KC, P]), ALU.mult))
                    chain.after(v.tensor_scalar(xb[:], xq_next[:], -448.0, 448.0, ALU.max, ALU.min))
                    chain.after(v.tensor_scalar(xbig[:].bitcast(U16), xb[:].bitcast(U16), 0x7FFF, None,
                                                ALU.bitwise_and))
                    chain.after(v.tensor_scalar(xbig[:], xbig[:], FP8_LEAST, FP8_STEP, ALU.max, ALU.mult))
                    chain.after(v.tensor_tensor(xq_next[:], xb[:], xbig[:], ALU.add))
                    chain.after(v.tensor_tensor(xq_next[:], xq_next[:], xbig[:], ALU.subtract))
                    chain.after(v.tensor_tensor(xq_next[:], xq_next[:], bc(quant["in_scale"][:], [P, 4, KC, P]),
                                                ALU.mult))

                def after_next(i, _):
                    next_inputs(bass.ds((i + 1) % NT * P, P))

                def add_out(i, _):
                    dve.wait_ge(out_ready, i + 1)
                    at = c.resid[:, i, :]
                    v.scalar_tensor_tensor(out=at, in0=ps[:, 5, 0:HID], scalar=out_scale, in1=at, op0=ALU.mult,
                                           op1=ALU.add).then_inc(resid_done, 1)

                def take_inputs(i):
                    wait(dve, proj_ready, i * NB)
                    if quant is None:
                        chain.after(v.tensor_copy(src["x"][:], sources["x"][:, :, bass.ds(i * P, P)]))
                    else:
                        chain.after(v.tensor_copy(xq[:], xq_next[:]))
                    v.tensor_copy(src["ctx"][:], sources["ctx"][:, :, bass.ds(i * P, P)]).then_inc(x_ready, 1)

                chain = Chain(dve, dve_chain)
                if quant is not None:
                    next_inputs(slice(0, P))
                cost = {"V": 9 + rms, "M": 1 + (mask is not None), "Q": 2, "O": 5, "Z": 7}
                chain.per = 1 + sum(cost.get(what, 0) for what, _, _ in steps["dve"])
                run_tiles(dve, steps["dve"], {"E": evacuate, "V": variance, "M": less_max, "Q": normalise_probs,
                                              "O": quantise_out, "F": add_out, "Z": after_next}, chain, take_inputs)

            @block.gpsimd
            def _(pool):
                g = nc.gpsimd

                def rstds(i, j):
                    n = normed.index(j)
                    b = n % NQ
                    pool.wait_ge(ve_ready, i * NN + n + 1)
                    one = g.tensor_tensor(rstd[:, b, :], ve[:, b, :], c.mhalf[:, 0:4], ALU.pow)
                    if rms:
                        one.then_inc(rstd_ready, 1)
                    else:
                        chain.after(one)
                        g.tensor_tensor(shift[:, b, :], rstd[:, b, :], neg_mean[:, b, :], ALU.mult
                                        ).then_inc(rstd_ready, 1)

                if diagonal:
                    g.memset(probsT[:], 0.0).then_inc(cleared, 1)
                chain = Chain(pool, pool_chain)
                chain.per = 0 if rms else NN
                run_tiles(pool, steps["pool"], {"R": rstds}, chain)


def load(c, st, waits, name, shape, src=None):
    buf = c.sb(st, name, shape)
    waits.append((buf, c.dram[name] if src is None else src))
    return buf


class Loads:

    def __init__(self, c, waits):
        self.c, self.waits = c, waits
        self.sp_in, self.act_in = c.sem(None, "sp_in"), c.sem(None, "act_in")
        with c.nc.Block() as block:
            @block.sync
            def _(sp):
                for buf, src in waits[0::2]:
                    sp.dma_start(buf[:], src).then_inc(self.sp_in, 16)

            @block.scalar
            def _(act):
                for buf, src in waits[1::2]:
                    act.dma_start(buf[:], src).then_inc(self.act_in, 16)

    def finish(self):
        with self.c.nc.Block() as block:
            @block.sync
            def _(sp):
                sp.wait_ge(self.sp_in, 16 * len(self.waits[0::2]))

            @block.scalar
            def _(act):
                act.wait_ge(self.act_in, 16 * len(self.waits[1::2]))


def by_head(qT, b):
    return qT[:, :, 4 * b:4 * b + 4, :].rearrange("p r h n -> p h r n")


def by_row(kT, b):
    return kT[:, 4 * b:4 * b + 4, :].rearrange("p h (r n) -> p h r n", r=2)


def attn0(c, before):
    with ExitStack() as st:
        w = []
        wq = load(c, st, w, "L0_wq", [P, KC, NH * HD])
        wk = load(c, st, w, "L0_wk", [P, KC, 4 * HD])
        wv = load(c, st, w, "L0_wv", [P, KC, 4 * HD])
        wo = load(c, st, w, "L0_wo", [P, NH, HID])
        bias = c.sb(st, "bias", [P, 6, 512])
        w.append((bias[:, 0:4].rearrange("p b n -> p (b n)"), c.dram["L0_xattn_bq"].partition_broadcast(P)))
        w.append((bias[:, 4], c.dram["L0_xattn_bk"].partition_broadcast(P)))
        w.append((bias[:, 5], c.dram["L0_xattn_bv"].partition_broadcast(P)))
        norms = load(c, st, w, "L0_norms", [P, 2])
        mask = c.sb(st, "mask", [P, SEQ])
        w.append((mask[0:64], c.dram["mask"]))
        w.append((mask[64:128], c.dram["mask"]))
        loads = Loads(c, w)
        before(c)
        layernorm(c, c.resid, c.norm, c.xT)
        loads.finish()
        qT = c.sb(st, "qT", [P, 2, NH, SEQ])
        kT = c.sb(st, "kT", [P, 4, P])
        v = c.sb(st, "v", [P, 4 * HD])
        blocks = [dict(src="ctx", w=wk, normed=True, bias=bias[:, 4], dst=by_row(kT, 0), wT=norms[:, 1:2], bT=None),
                  ]
        blocks += [dict(src="x", w=wq[:, :, 512 * b:512 * b + 512], normed=True, bias=bias[:, b],
                        dst=by_head(qT, b), wT=norms[:, 0:1], bT=None) for b in range(4)]
        blocks += [dict(src="ctx", w=wv, normed=False, bias=bias[:, 5], dst=v[:])]
        units = [dict(qT=qT, kT=kT, v=v, needs=[0, 1 + 2 * u, 2 + 2 * u], v_block=5) for u in range(2)]
        heads_attention(c, ORDER0, {"x": c.xT, "ctx": c.ctxT}, blocks, units, 4, 1e-6, wo, c.gate[:, 0:1], mask=mask)


def attn3(c, before):
    nc = c.nc
    with ExitStack() as st:
        w = []
        wq = load(c, st, w, "L3_wq", [P, KC, NH * HD])
        wqx = load(c, st, w, "L3_wqx", [P, KC, NH * HD])
        wk = load(c, st, w, "L3_wk", [P, KC, 8 * HD])
        wv = load(c, st, w, "L3_wv", [P, KC, 8 * HD])
        wkvx = load(c, st, w, "L3_wkvx", [P, KC, 16 * HD])
        wproj = load(c, st, w, "L3_wproj", [P, 2 * NH, HID])
        ln = load(c, st, w, "L3_ln", [P, 2, KC])
        in_scale = load(c, st, w, "L3_in_scale", [P, 4, KC])
        norms = load(c, st, w, "L3_norms", [P, 4, 2])
        smooth = load(c, st, w, "L3_smooth", [P, 2 * NH])
        scales = c.sb(st, "scales", [P, 6])
        for n, s in enumerate(("wq_scale", "wk_scale", "wv_scale", "wqx_scale", "proj_w_scale", "proj_in_scale")):
            w.append((scales[:, n:n + 1], c.dram["L3_xattn_" + s].partition_broadcast(P)))
        loads = Loads(c, w)
        before(c)
        layernorm(c, c.resid, c.norm, None)
        layernorm(c, c.norm, c.norm, c.xT)
        loads.finish()
        in_inv = c.sb(st, "in_inv", [P, 4, KC])
        smooth_inv = c.sb(st, "smooth_inv", [P, 2 * NH])
        out_scale = c.sb(st, "out_scale", [P, 1])
        consts, affine = c.sem(st, "consts"), c.sem(st, "affine")
        with nc.Block() as block:
            @block.vector
            def _(dve):
                nc.vector.reciprocal(in_inv[:], in_scale[:]).then_inc(consts, 1)
                nc.vector.reciprocal(smooth_inv[:], smooth[:]).then_inc(consts, 1)
                nc.vector.tensor_tensor(out_scale[:], scales[:, 4:5], scales[:, 5:6], ALU.mult).then_inc(consts, 1)
                dve.wait_ge(consts, 3)
                nc.vector.tensor_tensor(out_scale[:], out_scale[:], c.gate[:, 3:4], ALU.mult).then_inc(consts, 1)

            @block.scalar
            def _(act):
                for k in range(KC):
                    nc.scalar.activation(c.xT[:, k, :], c.xT[:, k, :], ACT.Identity, scale=ln[:, 0, k:k + 1],
                                         bias=ln[:, 1, k:k + 1]).then_inc(affine, 1)
        qT = c.sb(st, "qT", [P, 2, NH, SEQ])
        kT = c.sb(st, "kT", [P, 8, P])
        v = c.sb(st, "v", [P, 8 * HD])
        vx = c.sb(st, "vx", [P, 8 * HD])

        def turned(src, w_, dst, n, scale):
            return [dict(src=src, w=w_[:, :, 512 * b:512 * b + 512], normed=True, scale=scale,
                         dst=dst(b), wT=norms[:, n, 0:1], bT=norms[:, n, 1:2])
                    for b in range(w_.shape[2] // 512 if src != "ctx" else 2)]

        def plain(src, w_, dst, scale, off=0):
            return [dict(src=src, w=w_[:, :, off + 512 * b:off + 512 * b + 512], normed=False, scale=scale,
                         dst=dst[:, 512 * b:512 * b + 512]) for b in range(2)]

        blocks = (turned("k", wk, lambda b: by_row(kT, b), 1, scales[:, 1:2]) + plain("v", wv, v, scales[:, 2:3])
                  + turned("q", wq, lambda b: by_head(qT, b), 0, scales[:, 0:1]) + turned("ctx", wkvx, lambda b: by_row(kT, b), 3, None)
                  + plain("ctx", wkvx, vx, None, 8 * HD) + turned("qx", wqx, lambda b: by_head(qT, b), 2, scales[:, 3:4]))
        units = [dict(qT=qT, kT=kT, v=v if u < 2 else vx, needs=[(5, 7, 13, 15)[u]], v_block=(2, 3, 10, 11)[u])
                 for u in range(4)]
        heads_attention(c, ORDER3, {"x": c.xT, "ctx": c.ctxT}, blocks, units, 8, 1e-5, wproj, out_scale[:, 0:1],
                        quant={"in_inv": in_inv, "in_scale": in_scale, "smooth": smooth_inv})



def decay_by_key():
    gam = (1.0 - 2.0 ** (-5.0 - np.arange(2, dtype=np.float32))).astype(np.float32)
    at = np.arange(SEQ, dtype=np.float32)
    expo = at[None, :] - at[:, None]
    m = np.where(expo[None] <= 0, gam[:, None, None] ** expo[None], 0.0).astype(np.float32)
    m = m / np.sqrt(m.sum(axis=-1, dtype=np.float32))[:, None, :]
    m = m.astype(np.float32).transpose(2, 0, 1)
    return np.ascontiguousarray(np.concatenate([m, m]))


def attn1(c, before):
    nc = c.nc
    with ExitStack() as st:
        w = []
        wh = load(c, st, w, "L1_wh", [P, 2, HD])
        wg = load(c, st, w, "L1_wg", [P, KC, HID])
        wo = load(c, st, w, "L1_wo", [P, KC, HID])
        decay = load(c, st, w, "L1_decay", [P, 2, SEQ])
        gamma = c.sb(st, "gamma", [P, HID])
        beta = c.sb(st, "beta", [P, HID])
        w.append((gamma, c.dram["L1_xattn_gn_gamma"].partition_broadcast(P)))
        w.append((beta, c.dram["L1_xattn_gn_beta"].partition_broadcast(P)))
        loads = Loads(c, w)
        before(c)
        layernorm(c, c.resid, c.norm, c.xT)
        loads.finish()
        qT = c.sb(st, "qT", [P, 2, TOK])
        kT = c.sb(st, "kT", [P, 2, TOK])
        v = c.sb(st, "v", [P, NT, HID])
        relu = c.sb(st, "relu", [P, NT, HID])
        mix = c.sb(st, "mix", [P, 2, P])
        (qk_ready, qk_stored, v_ready, v_stored, s_ready, mix_zero, chain_s, mix_ready, o_ready, o_stored) = (
            c.sem(st, n) for n in ("qk_ready", "qk_stored", "v_ready", "v_stored", "s_ready", "mix_zero", "chain",
                                   "mix_ready", "o_ready", "o_stored"))
        out = c.norm
        with nc.Block() as block:
            @block.tensor
            def _(pe):
                for n, (src, h, half) in enumerate((s, h, f) for s in (c.ctxT, c.xT) for h in range(2)
                                                   for f in range(2)):
                    nc.tensor.matmul(c.psum[:, n, :], wh[:, h, :], src[:, h, half * HALF:(half + 1) * HALF],
                                     start=True, stop=True).then_inc(qk_ready, 1)
                for t in range(NT):
                    pe.wait_ge(qk_stored, 6 if t < 4 else 8)
                    for h in range(2):
                        nc.tensor.matmul(c.psum[:, t // 2, t % 2 * HID + h * HD:t % 2 * HID + (h + 1) * HD],
                                         c.ctxT[:, h, t * P:(t + 1) * P], wh[:, h, :], start=True, stop=True)
                    for k in range(KC):
                        last = nc.tensor.matmul(c.psum[:, 4 + t // 2, t % 2 * HID:(t % 2 + 1) * HID],
                                                c.xT[:, k, t * P:(t + 1) * P], wg[:, k, :], start=k == 0,
                                                stop=k == KC - 1)
                    if t % 2:
                        last.then_inc(v_ready, 1)
                pe.wait_ge(v_stored, 8)
                for h in range(2):
                    for r in range(2):
                        for b in range(BATCH):
                            last = nc.tensor.matmul(c.psum[64 * r:64 * r + 64, 2 * h + r, 0:SEQ],
                                                    kT[:, h, b * SEQ:(b + 1) * SEQ], qT[:, h, b * SEQ:(b + 1) * SEQ],
                                                    start=b == 0, stop=b == BATCH - 1)
                        last.then_inc(s_ready, 1)
                pe.wait_ge(mix_ready, 4)
                for t in range(NT):
                    for h in range(2):
                        last = nc.tensor.matmul(c.psum[:, 4 + t // 2, t % 2 * HID + h * HD:t % 2 * HID + (h + 1) * HD],
                                                mix[:, h, :], v[:, t, h * HD:(h + 1) * HD], start=True, stop=True)
                    if t % 2:
                        last.then_inc(o_ready, 1)

            @block.scalar
            def _(act):
                for n in range(0, 8, 2):
                    act.wait_ge(qk_ready, n + 2)
                    nc.scalar.activation((kT if n < 4 else qT)[:, n // 2 % 2, :],
                                         c.psum[:, n:n + 2, :].rearrange("p b n -> p (b n)"),
                                         ACT.Copy).then_inc(qk_stored, 2)
                for g in range(4):
                    act.wait_ge(v_ready, g + 1)
                    nc.scalar.activation(v[:, 2 * g:2 * g + 2, :],
                                         c.psum[:, g, :].rearrange("p (t n) -> p t n", t=2), ACT.Copy).then_inc(v_stored, 1)
                    nc.scalar.activation(relu[:, 2 * g:2 * g + 2, :],
                                         c.psum[:, 4 + g, :].rearrange("p (t n) -> p t n", t=2),
                                         ACT.Relu).then_inc(v_stored, 1)
                for g in range(4):
                    act.wait_ge(o_ready, g + 1)
                    nc.scalar.activation(out[:, 2 * g:2 * g + 2, :],
                                         c.psum[:, 4 + g, :].rearrange("p (t n) -> p t n", t=2), ACT.Copy).then_inc(o_stored, 1)

            @block.vector
            def _(dve):
                chain = Chain(dve, chain_s)
                chain.after(nc.vector.memset(mix[:], 0.0))
                for h in range(2):
                    for r in range(2):
                        dve.wait_ge(s_ready, 2 * h + r + 1)
                        rows = slice(64 * r, 64 * r + 64)
                        part = mix[rows, h, 64 * r:64 * r + 64]
                        chain.after(nc.vector.scalar_tensor_tensor(
                            out=part, in0=c.psum[rows, 2 * h + r, 0:SEQ], scalar=HD ** -0.5, in1=decay[rows, h, :],
                            op0=ALU.mult, op1=ALU.mult))
                        chain.after(nc.vector.scalar_tensor_tensor(out=part, in0=part, scalar=-1.0, in1=part,
                                                                   op0=ALU.mult, op1=ALU.max))
                        nc.vector.tensor_scalar(part, part, 1.0, None, ALU.max).then_inc(mix_ready, 1)
        normed = v
        layernorm(c, out, normed, None, eps=1e-3)
        yT = qT
        (chain2, y_ready, turned, stored, p_ready, added) = (
            c.sem(st, n) for n in ("chain2", "y_ready", "turned", "y_stored", "p_ready", "added"))
        with nc.Block() as block:
            @block.vector
            def _(dve):
                chain = Chain(dve, chain2)
                for t in range(NT):
                    chain.after(nc.vector.tensor_tensor(normed[:, t, :], normed[:, t, :], gamma[:], ALU.mult))
                    chain.after(nc.vector.tensor_tensor(normed[:, t, :], normed[:, t, :], beta[:], ALU.add))
                    nc.vector.tensor_tensor(normed[:, t, :], normed[:, t, :], relu[:, t, :], ALU.mult).then_inc(y_ready, 1)
                for g in range(4):
                    dve.wait_ge(p_ready, g + 1)
                    nc.vector.scalar_tensor_tensor(
                        out=c.resid[:, 2 * g:2 * g + 2, :], in0=c.psum[:, 4 + g, :].rearrange("p (t n) -> p t n", t=2),
                        scalar=c.gate[:, 1:2], in1=c.resid[:, 2 * g:2 * g + 2, :], op0=ALU.mult,
                        op1=ALU.add).then_inc(added, 1)

            @block.tensor
            def _(pe):
                pe_transpose_tokens(c, pe, normed, y_ready, turned)
                for t in range(NT):
                    if t % 2 == 0:
                        pe.wait_ge(stored, t // 2 + 1)
                    for k in range(KC):
                        last = nc.tensor.matmul(c.psum[:, 4 + t // 2, t % 2 * HID:(t % 2 + 1) * HID],
                                                yT[:, k, t * P:(t + 1) * P], wo[:, k, :], start=k == 0, stop=k == KC - 1)
                    if t % 2:
                        last.then_inc(p_ready, 1)

            @block.scalar
            def _(act):
                act_store_transposed(c, act, yT, turned, stored)



ORDER2 = {
    "pe": order("S0 T14' A13' S1 T15' A14' S2 T0 A15' S3 T1 A0 W' S4 T2 A1 Y' S5 T3 A2 S6 T4 A3 S7 T5 A4 S8 T6 "
               "A5 S9 T7 A6 S10 T8 A7 S11 T9 A8 S12 T10 A9 S13 T11 A10 S14 T12 A11 S15 T13 A12"),
    "act": order("X0 E15' X1 E0 X2 E1 X3 Z' E2 X4 E3 X5 E4 X6 E5 X7 E6 X8 E7 X9 E8 X10 E9 X11 E10 X12 E11 X13 E12 "
                "X14 E13 X15 E14"),
    "dve": order("R14' M0 R15' J' L M1 R0 M2 O' R1 M3 R2 M4 R3 F' M5 R4 M6 R5 M7 R6 M8 R7 M9 R8 I M10 R9 M11 R10 "
                "M12 R11 M13 R12 M14 R13 M15"),
}


def attn2(c, before):
    nc = c.nc
    H, D = NH, 16
    LN255 = float(np.log(255.0))
    with ExitStack() as st:
        w = []
        wq = load(c, st, w, "L2_wq", [P, KC, HID])
        wkv = load(c, st, w, "L2_wkv", [P, KC, 2 * HID])
        wp = load(c, st, w, "L2_wp", [P, KC, HID])
        bias = c.sb(st, "bias", [P, 2, HID])
        w.append((bias[:, 0], c.dram["L2_xattn_bq"].partition_broadcast(P)))
        w.append((bias[:, 1], c.dram["L2_bk"].partition_broadcast(P)))
        bv = load(c, st, w, "L2_bv", [P, KC])
        bp = c.sb(st, "bp", [P, HID])
        w.append((bp, c.dram["L2_xattn_bp"].partition_broadcast(P)))
        loads = Loads(c, w)
        before(c)
        layernorm(c, c.resid, c.norm, c.xT)
        loads.finish()
        qT = c.sb(st, "qT", [P, H // 2, TOK], BF16)
        kT = c.sb(st, "kT", [P, H // 2, TOK], BF16)
        v = c.sb(st, "v", [P, NT, HID], BF16)
        sq = c.sb(st, "sq", [P, NT, 2, H])
        sv = c.sb(st, "sv", [P, 2, KC])
        with ExitStack() as inner:
            qk = c.sb(inner, "qk", [P, NT, 2, HID])
            parts = c.sb(inner, "parts", [P, 2, NT, H, 4, D], BF16)
            inv = c.sb(inner, "inv", [P, NT, 2, H])
            vT = c.sb(inner, "vT", [P, KC, TOK])
            vb = c.sb(inner, "vb", [P, KC, TOK], BF16)
            (chain_s, pool_s, qk_ready, qk_read, v_ready, vT_ready, vb_ready, parts_ready, turned, stored, v_turned,
             v_stored) = (c.sem(inner, n) for n in (
                 "chain", "pool_chain", "qk_ready", "qk_read", "v_ready", "vT_ready", "vb_ready", "parts_ready",
                 "turned", "stored", "v_turned", "v_stored"))
            with nc.Block() as block:
                @block.tensor
                def _(pe):
                    for t in range(NT):
                        for s, (src, w_) in enumerate(((c.xT, wq[:, :, :]), (c.ctxT, wkv[:, :, 0:HID]))):
                            for k in range(KC):
                                last = nc.tensor.matmul(c.psum[:, t, s * HID:(s + 1) * HID],
                                                        src[:, k, t * P:(t + 1) * P], w_[:, k, :], start=k == 0,
                                                        stop=k == KC - 1)
                        last.then_inc(qk_ready, 1)
                    for n, (m, half) in enumerate((m, f) for m in range(KC) for f in range(2)):
                        pe.wait_ge(qk_read, n + 1)
                        for k in range(KC):
                            last = nc.tensor.matmul(c.psum[:, n, :], wkv[:, k, HID + m * P:HID + (m + 1) * P],
                                                    c.ctxT[:, k, half * HALF:(half + 1) * HALF], start=k == 0,
                                                    stop=k == KC - 1)
                        last.then_inc(v_ready, 1)
                    pe.wait_ge(vb_ready, KC)
                    pe.wait_ge(qk_read, NT)
                    pb = c.psum[:, 4:6, :].bitcast(BF16)
                    for t in range(NT):
                        for m in range(KC):
                            last = nc.tensor.transpose(pb[:, t // 4, t % 4 * HID + m * P:t % 4 * HID + (m + 1) * P],
                                                       vb[:, m, t * P:(t + 1) * P], c.identb[:])
                        if t % 4 == 3:
                            last.then_inc(v_turned, 1)
                    for s in range(2):
                        pe.wait_ge(parts_ready, s + 1)
                        for t in range(NT):
                            n = s * NT + t
                            b = 6 + n % 2
                            if n >= 2:
                                pe.wait_ge(stored, n - 1)
                            dst = c.psum[:, b, :].bitcast(BF16)
                            for g in range(H // 2):
                                last = nc.tensor.transpose(
                                    dst[:, g * P:(g + 1) * P],
                                    parts[:, s, t, 2 * g:2 * g + 2, :, :].rearrange("p h f d -> p (h f d)"), c.identb[:])
                            last.then_inc(turned, 1)

                @block.scalar
                def _(act):
                    for m in range(KC):
                        act.wait_ge(v_ready, 2 * m + 2)
                        nc.scalar.activation(vT[:, m, :], c.psum[:, 2 * m:2 * m + 2, :].rearrange("p b n -> p (b n)"),
                                             ACT.Identity, bias=bv[:, m:m + 1]).then_inc(vT_ready, 1)
                    pb = c.psum[:, 4:6, :].bitcast(BF16)
                    for g in range(2):
                        act.wait_ge(v_turned, g + 1)
                        nc.scalar.activation(v[:, 4 * g:4 * g + 4, :], pb[:, g, :].rearrange("p (t n) -> p t n", t=4),
                                             ACT.Copy).then_inc(v_stored, 1)
                    for n in range(2 * NT):
                        s, t = n // NT, n % NT
                        act.wait_ge(turned, n + 1)
                        nc.scalar.activation((qT if s else kT)[:, :, t * P:(t + 1) * P],
                                             c.psum[:, 6 + n % 2, :].bitcast(BF16).rearrange("p (g n) -> p g n", g=8),
                                             ACT.Copy).then_inc(stored, 1)

                @block.vector
                def _(dve):
                    g, chain = nc.vector, Chain(dve, chain_s)
                    for t in range(NT):
                        dve.wait_ge(qk_ready, t + 1)
                        g.tensor_tensor(qk[:, t], c.psum[:, t, :].rearrange("p (s n) -> p s n", s=2), bias[:],
                                        ALU.add).then_inc(qk_read, 1)
                    dve.wait_ge(qk_read, NT)
                    chain.after(g.tensor_scalar(qk[:, :, 0, :], qk[:, :, 0, :], D ** -0.5, None, ALU.mult))
                    flat = qk[:].rearrange("p t s (h d) -> p (t s h) d", d=D)
                    steps, inverse = sq[:].rearrange("p t s h -> p (t s h)"), inv[:].rearrange("p t s h -> p (t s h)")
                    chain.after(g.tensor_reduce(steps, flat, X, ALU.max, apply_absolute_value=True))
                    chain.after(g.tensor_scalar(steps, steps, 1 / 127.0, 1e-8, ALU.mult, ALU.max))
                    chain.after(g.reciprocal(inverse, steps))
                    chain.after(g.tensor_tensor(flat, flat, bc(inverse, [P, NT * 2 * H, D]), ALU.mult))
                    chain.after(g.tensor_scalar(qk[:], qk[:], ROUND, ROUND, ALU.add, ALU.subtract))
                    keys = qk[:, :, 1, :].rearrange("p t (h d) -> p t h d", d=D)
                    chain.after(g.tensor_tensor(keys, keys, bc(sq[:, :, 1, :], [P, NT, H, D]), ALU.mult))
                    for f in range(3):
                        dst = parts[:, 0, :, :, f, :]
                        chain.after(g.tensor_copy(dst, keys))
                        if f < 2:
                            chain.after(g.tensor_tensor(keys, keys, dst, ALU.subtract))
                    g.memset(parts[:, 0, :, :, 3, :], 0.0).then_inc(parts_ready, 1)
                    queries = qk[:, :, 0, :].rearrange("p t (h d) -> p t h d", d=D)
                    for f in range(3):
                        chain.add(g.tensor_copy(parts[:, 1, :, :, f, :], queries))
                    chain.join()
                    g.memset(parts[:, 1, :, :, 3, :], 0.0).then_inc(parts_ready, 1)
                    for m in range(KC):
                        dve.wait_ge(vT_ready, m + 1)
                        chain.after(g.tensor_reduce(sv[:, 0, m:m + 1], vT[:, m, :], X, ALU.max,
                                                    apply_absolute_value=True))
                        chain.after(g.tensor_scalar(sv[:, 0, m:m + 1], sv[:, 0, m:m + 1], 1 / 127.0, 1e-8, ALU.mult,
                                                    ALU.max))
                        chain.after(g.reciprocal(sv[:, 1, m:m + 1], sv[:, 0, m:m + 1]))
                        chain.after(g.tensor_scalar(vT[:, m, :], vT[:, m, :], sv[:, 1, m:m + 1], ROUND, ALU.mult,
                                                    ALU.add))
                        g.tensor_scalar(vb[:, m, :], vT[:, m, :], ROUND, None, ALU.subtract).then_inc(vb_ready, 1)
                    chain.after(g.tensor_scalar(bp[:], bp[:], c.gate[:, 2:3], None, ALU.mult))

        (chain_s, tile_ready, s_ready, m_ready, exp_done, rounded, turned, pt_stored, o_ready, o_scaled,
         ot_ready, ot_stored, y_ready, y_added) = (c.sem(st, n) for n in (
             "chain", "tile_ready", "s_ready", "m_ready", "exp_done", "rounded", "turned", "pt_stored",
             "o_ready", "o_scaled", "ot_ready", "ot_stored", "y_ready", "y_added"))
        qt = c.sb(st, "qt", [P, H // 2, P], BF16)
        sqt = c.sb(st, "sqt", [P, 2, H])
        m = c.sb(st, "m", [P, H])
        nb = c.sb(st, "nb", [P, H])
        e = c.sb(st, "e", [P, 2, TOK])
        esum = c.sb(st, "esum", [P, 2, H])
        pi = c.sb(st, "pi", [P, 2, TOK], BF16)
        pT = c.sb(st, "pT", [P, 2, TOK], BF16)
        o = c.sb(st, "o", [P, HID])
        oT = c.sb(st, "oT", [P, KC, P])
        with nc.Block() as block:
            @block.tensor
            def _(pe):
                def scores(i, h):
                    rows = slice(64 * (h % 2), 64 * (h % 2) + 64)
                    if h == 0:
                        pe.wait_ge(tile_ready, i + 1)
                    wait(pe, exp_done, i * H + h - 1)
                    for f in range(2):
                        last = nc.tensor.matmul(c.psum[:, 2 * (h % 2) + f, :], qt[rows, h // 2, :],
                                                kT[rows, h // 2, f * HALF:(f + 1) * HALF], start=True, stop=True)
                    last.then_inc(s_ready, 1)

                def turn(i, h):
                    pe.wait_ge(rounded, i * H + h + 1)
                    dst = c.psum[:, 4 + h % 2, :].bitcast(BF16)
                    for k in range(NT):
                        last = nc.tensor.transpose(dst[:, k * P:(k + 1) * P], pi[:, h % 2, k * P:(k + 1) * P],
                                                   c.identb[:])
                    last.then_inc(turned, 1)

                def values(i, h):
                    pe.wait_ge(pt_stored, i * H + h + 1)
                    if h == 0:
                        wait(pe, o_scaled, i)
                    for k in range(NT):
                        last = nc.tensor.matmul(c.psum[:, 6, h * D:(h + 1) * D], pT[:, h % 2, k * P:(k + 1) * P],
                                                v[:, k, h * D:(h + 1) * D], start=k == 0, stop=k == NT - 1)
                    if h == H - 1:
                        last.then_inc(o_ready, 1)

                def turn_out(i, _):
                    pe.wait_ge(o_scaled, i + 1)
                    wait(pe, y_added, i)
                    for k in range(KC):
                        last = nc.tensor.transpose(c.psum[:, 7, k * P:(k + 1) * P], o[:, k * P:(k + 1) * P], c.ident[:])
                    last.then_inc(ot_ready, 1)

                def project(i, _):
                    pe.wait_ge(ot_stored, i + 1)
                    for k in range(KC):
                        last = nc.tensor.matmul(c.psum[:, 7, HID:2 * HID], oT[:, k, :], wp[:, k, :], start=k == 0,
                                                stop=k == KC - 1)
                    last.then_inc(y_ready, 1)

                run_tiles(pe, ORDER2["pe"], {"S": scores, "T": turn, "A": values, "W": turn_out, "Y": project})

            @block.scalar
            def _(act):
                def exps(i, h):
                    act.wait_ge(m_ready, i * H + h + 1)
                    nc.scalar.activation(e[:, h % 2, :],
                                         c.psum[:, 2 * (h % 2):2 * (h % 2) + 2, :].rearrange("p b n -> p (b n)"),
                                         ACT.Exp, scale=sqt[:, 0, h:h + 1], bias=nb[:, h:h + 1],
                                         accum_out=esum[:, 0, h:h + 1]).then_inc(exp_done, 1)

                def store(i, h):
                    act.wait_ge(turned, i * H + h + 1)
                    nc.scalar.activation(pT[:, h % 2, :], c.psum[:, 4 + h % 2, :].bitcast(BF16), ACT.Copy
                                         ).then_inc(pt_stored, 1)

                def store_out(i, _):
                    act.wait_ge(ot_ready, i + 1)
                    for k in range(KC):
                        last = nc.scalar.activation(oT[:, k, :], c.psum[:, 7, k * P:(k + 1) * P], ACT.Copy,
                                                    scale=sv[:, 0, k:k + 1])
                    last.then_inc(ot_stored, 1)

                run_tiles(act, ORDER2["act"], {"X": exps, "E": store, "Z": store_out})

            @block.vector
            def _(dve):
                g = nc.vector

                def take_steps(i, heads):
                    now = sq[:, bass.ds(i, 1), 0, heads].rearrange("p o h -> p (o h)")
                    chain.add(g.tensor_copy(sqt[:, 0, heads], now))
                    chain.add(g.tensor_scalar(sqt[:, 1, heads], now, -1.0, None, ALU.mult))
                    chain.join()

                def take_queries(i):
                    take_steps(i, slice(0, 8))
                    g.tensor_copy(qt[:], qT[:, :, bass.ds(i * P, P)]).then_inc(tile_ready, 1)

                def late_steps(i, _):
                    take_steps(i, slice(8, 16))

                def biggest(i, h):
                    dve.wait_ge(s_ready, i * H + h + 1)
                    chain.after(g.tensor_reduce(m[:, h:h + 1], c.psum[:, 2 * (h % 2):2 * (h % 2) + 2, :], XY, ALU.max))
                    g.tensor_scalar(nb[:, h:h + 1], m[:, h:h + 1], sqt[:, 1, h:h + 1], LN255, ALU.mult, ALU.add
                                    ).then_inc(m_ready, 1)

                def round_probs(i, h):
                    dve.wait_ge(exp_done, i * H + h + 1)
                    g.tensor_scalar(pi[:, h % 2, :], e[:, h % 2, :], ROUND, ROUND, ALU.add, ALU.subtract
                                    ).then_inc(rounded, 1)

                def invert_first(i, _):
                    chain.after(g.reciprocal(esum[:, 1, 0:8], esum[:, 0, 0:8]))

                def invert_last(i, _):
                    chain.after(g.reciprocal(esum[:, 1, 8:16], esum[:, 0, 8:16]))

                def scale_out(i, _):
                    dve.wait_ge(o_ready, i + 1)
                    g.tensor_tensor(o[:].rearrange("p (h d) -> p h d", d=D),
                                    c.psum[:, 6, 0:HID].rearrange("p (h d) -> p h d", d=D),
                                    bc(esum[:, 1, :], [P, H, D]), ALU.mult).then_inc(o_scaled, 1)

                def add_out(i, _):
                    dve.wait_ge(y_ready, i + 1)
                    at = c.resid[:, i, :]
                    chain.after(g.scalar_tensor_tensor(out=at, in0=c.psum[:, 7, HID:2 * HID], scalar=c.gate[:, 2:3],
                                                       in1=at, op0=ALU.mult, op1=ALU.add))
                    g.tensor_tensor(at, at, bp[:], ALU.add).then_inc(y_added, 1)

                chain = Chain(dve, chain_s)
                cost = {"M": 1, "I": 1, "J": 1, "L": 2, "F": 1}
                chain.per = 2 + sum(cost.get(what, 0) for what, _, _ in ORDER2["dve"])
                run_tiles(dve, ORDER2["dve"], {"M": biggest, "R": round_probs, "I": invert_first, "J": invert_last,
                                               "L": late_steps, "O": scale_out, "F": add_out}, chain, take_queries)


STAGES = tuple(range(8))


def build(nc, dram, out):
    attention, feed_forward = (attn0, attn1, attn2, attn3), (ffn0, ffn1, ffn2, ffn3)
    with ExitStack() as ctx:
        c = Core(nc, ctx, dram)
        before = start
        for s in range(4):
            if 2 * s in STAGES:
                with c.new_stage():
                    attention[s](c, before)
                before = nothing
            if 2 * s + 1 in STAGES:
                if before is not nothing:
                    with c.new_stage():
                        before(c)
                before = feed_forward[s]
        with c.new_stage():
            before(c)
            finish(c, out)


def nothing(c):
    pass



def laid_out(i):
    c = np.ascontiguousarray
    a = {n: np.asarray(v) for n, v in i.items()}
    o = {}

    def rows(w):
        return c(w.reshape(KC, P, -1).transpose(1, 0, 2))

    def gu(g, u):
        w = np.concatenate([g, u], axis=2)
        return c(w.reshape(len(g), KC, P, -1).transpose(0, 2, 1, 3))

    def cols(w, f):
        return w.reshape(HID, -1, f).transpose(1, 0, 2)

    o["x"] = c(a["x"].reshape(TOK, HID))
    o["ctx_2048"] = c(a["ctx_2048"].reshape(TOK, HID))
    o["g_xattn"], o["g_ffn"] = a["g_xattn"], a["g_ffn"]
    o["L0_router"] = rows(a["L0_ffn_gate_weight"].T)
    o["L0_ffn_similarity"] = a["L0_ffn_similarity"]
    w = a["L0_ffn_gate_up_proj"].transpose(0, 2, 1)
    o["L0_gu"] = gu(w[:, :, :96], w[:, :, 96:])
    o["L0_dn"] = c(a["L0_ffn_down_proj"].transpose(0, 2, 1))
    o["L1_gu"] = gu(cols(a["L1_ffn_gate_w"].T, 88), cols(a["L1_ffn_up_w"].T, 88))
    o["L1_dn"] = c(np.concatenate([a["L1_ffn_down_w"].T, a["L1_ffn_gate_s"][:, None], a["L1_ffn_up_s"][:, None]],
                                  axis=1).reshape(8, 88, HID + 2))
    o["L1_ffn_down_s"] = a["L1_ffn_down_s"]
    o["L2_router"] = rows(a["L2_ffn_gate_w"].T)

    def halves(w, n):
        e, h, f = w.shape
        return w.reshape(e, h, n, f // n).transpose(0, 2, 1, 3).reshape(e * n, h, f // n)

    o["L2_gu"] = gu(halves(a["L2_ffn_w_gate"], 2), halves(a["L2_ffn_w_up"], 2))
    o["L2_dn"] = c(a["L2_ffn_w_down"].reshape(32, 88, HID))
    o["L2s_gu"] = gu(cols(a["L2_ffn_sw_gate"], 88), cols(a["L2_ffn_sw_up"], 88))
    o["L2s_dn"] = c(a["L2_ffn_sw_down"].reshape(4, 88, HID))
    o["L3_router"] = rows(a["L3_ffn_router_w"].T)
    w = a["L3_ffn_gate_up_proj"]
    o["L3_gu"] = gu(halves(w[:, :, :512], 4), halves(w[:, :, 512:], 4))
    o["L3_dn"] = c(a["L3_ffn_down_proj"].reshape(32, 128, HID))
    o["L3s_gu"] = gu(cols(a["L3_ffn_shared_gate_w"], 128), cols(a["L3_ffn_shared_up_w"], 128))
    o["L3s_dn"] = c(a["L3_ffn_shared_down_w"].reshape(4, 128, HID))

    o["L0_wq"], o["L0_wk"], o["L0_wv"] = rows(a["L0_xattn_Wq"]), rows(a["L0_xattn_Wk"]), rows(a["L0_xattn_Wv"])
    o["L0_wo"] = c(a["L0_xattn_Wo"].reshape(NH, P, HID).transpose(1, 0, 2))
    for n in ("L0_xattn_bq", "L0_xattn_bk", "L0_xattn_bv", "L1_xattn_gn_gamma", "L1_xattn_gn_beta"):
        o[n] = a[n]
    o["L0_norms"] = c(np.stack([a["L0_xattn_qn_w"], a["L0_xattn_kn_w"]], axis=1))
    o["mask"] = c(a["mask_1xSxS2_ff0"][0])
    o["L1_wh"] = c(a["L1_xattn_Wh"].transpose(1, 0, 2))
    o["L1_wg"], o["L1_wo"] = rows(a["L1_xattn_wg_w"]), rows(a["L1_xattn_wo_w"])
    o["L1_decay"] = decay_by_key()
    for n in ("wq", "wqx", "wk", "wv"):
        o["L3_" + n] = rows(a["L3_xattn_" + n].T)
    o["L3_wkvx"] = rows(a["L3_xattn_w_kv_x"].T)
    o["L3_wproj"] = c(a["L3_xattn_wproj"].T.reshape(2 * NH, P, HID).transpose(1, 0, 2))
    o["L3_ln"] = c(np.stack([a["L3_xattn_ln_w"], a["L3_xattn_ln_b"]]).reshape(2, KC, P).transpose(2, 0, 1))
    o["L3_in_scale"] = c(np.stack([a["L3_xattn_" + n + "_in_scale"] for n in ("q", "k", "v", "qx")])
                         .reshape(4, KC, P).transpose(2, 0, 1))
    o["L3_norms"] = c(np.stack([np.stack([a[f"L3_xattn_{n}ln_w"], a[f"L3_xattn_{n}ln_b"]])
                                for n in ("q", "k", "qx", "kx")]).transpose(2, 0, 1))
    o["L3_smooth"] = c(a["L3_xattn_proj_smooth"].reshape(2 * NH, P).T)
    for n in ("wq_scale", "wk_scale", "wv_scale", "wqx_scale", "proj_w_scale", "proj_in_scale"):
        o["L3_xattn_" + n] = c(a["L3_xattn_" + n].reshape(1))
    o["L2_wq"], o["L2_wkv"], o["L2_wp"] = (rows(a["L2_xattn_" + n]) for n in ("Wq", "Wkv", "Wp"))
    o["L2_xattn_bq"], o["L2_xattn_bp"], o["L2_bk"] = a["L2_xattn_bq"], a["L2_xattn_bp"], a["L2_xattn_bkv"][:HID]
    o["L2_bv"] = c(a["L2_xattn_bkv"][HID:].reshape(KC, P).T)
    return o


def kernel(**inputs):
    import concourse.bacc as bacc
    from concourse.bass_utils import run_bass_kernel_spmd

    nc = bacc.Bacc("TRN2", target_bir_lowering=False, num_devices=1)
    arrays, dram = {}, {}
    for name, a in laid_out(inputs).items():
        a = np.ascontiguousarray(a)
        arrays[f"in_{name}"] = a
        dram[name] = nc.dram_tensor(f"in_{name}", a.shape, mybir.dt.from_np(a.dtype), kind="ExternalInput").ap()
    out = nc.dram_tensor("out", (TOK, HID), F32, kind="ExternalOutput").ap()
    build(nc, dram, out)
    r = run_bass_kernel_spmd(nc, [arrays], core_ids=[0])
    return r.results[0]["out"].reshape(BATCH, SEQ, HID)
```

```python
from contextlib import ExitStack, contextmanager

import numpy as np

import concourse.bass as bass
from concourse import mybir

F32 = mybir.dt.float32
BF16 = mybir.dt.bfloat16
U16 = mybir.dt.uint16
U32 = mybir.dt.uint32
ALU = mybir.AluOpType
ACT = mybir.ActivationFunctionType
X, XY = mybir.AxisListType.X, mybir.AxisListType.XY

P = 128
BATCH, SEQ, HID = 16, 64, 256
TOK = BATCH * SEQ
NT = TOK // P
KC = HID // P
HD = 128
NH = 16
HALF = TOK // 2
ROUND = 1.5 * 2.0 ** 23
FP8_LEAST = 1.5 * 2.0 ** -6
FP8_STEP = 2.0 ** 20


class Chain:

    def __init__(self, eng, sem, base=0):
        self.eng, self.sem, self.base, self.n, self.per = eng, sem, base, 0, 0

    def add(self, ins):
        self.n += 1
        ins.then_inc(self.sem, 1)

    def join(self):
        self.eng.wait_ge(self.sem, self.base + self.n)

    def after(self, ins):
        self.add(ins)
        self.join()


class Core:

    def __init__(self, nc, ctx, dram):
        self.nc, self.dram, self.count = nc, dram, 0
        self.live = ctx
        self.psum = ctx.enter_context(nc.psum_tensor("psum", [P, 8, 512], F32))
        self.resid = self.sb(ctx, "resid", [P, NT, HID])
        self.norm = self.sb(ctx, "norm", [P, NT, HID])
        self.xT = self.sb(ctx, "xT", [P, KC, TOK])
        self.ctxT = self.sb(ctx, "ctxT", [P, KC, TOK])
        self.ident = self.sb(ctx, "ident", [P, P])
        self.identb = self.sb(ctx, "identb", [P, P], BF16)
        self.gate = self.sb(ctx, "gate", [P, 8])
        self.gate_raw = self.sb(ctx, "gate_raw", [P, 8])
        self.stats = self.sb(ctx, "stats", [P, NT, 6])
        self.mv = self.sb(ctx, "mv", [P, NT, 2])
        self.ve = self.sb(ctx, "ve", [P, NT])
        self.rstd = self.sb(ctx, "rstd", [P, NT])
        self.mhalf = self.sb(ctx, "mhalf", [P, 64])

    def sb(self, ctx, name, shape, dt=F32):
        self.count += 1
        return ctx.enter_context(self.nc.sbuf_tensor(f"{name}_{self.count}", shape, dt))

    def sem(self, ctx, name):
        self.count += 1
        s = self.stage.enter_context(self.nc.semaphore(f"{name}_{self.count}"))
        self.used.append(s)
        return s

    @contextmanager
    def new_stage(self):
        with ExitStack() as self.stage:
            self.used = []
            yield
            with self.nc.Block() as block:
                @block.gpsimd
                def _(pool):
                    nums = [s.num for s in self.used]
                    pool.sem_clear(range(min(nums), max(nums) + 1))


def bc(ap, shape):
    return ap.unsqueeze(len(ap.shape)).to_broadcast(shape)



def start_loads(c):
    d = c.dram
    c.x_in, c.ctx_in, c.gates_in = (c.sem(None, n) for n in ("x_in", "ctx_in", "gates_in"))
    with c.nc.Block() as block:
        @block.sync
        def _(sp):
            sp.dma_start(c.norm[:], d["ctx_2048"].rearrange("(t p) d -> p t d", p=P)).then_inc(c.ctx_in, 16)
            sp.dma_start(c.resid[:], d["x"].rearrange("(t p) d -> p t d", p=P)).then_inc(c.x_in, 16)

        @block.scalar
        def _(act):
            act.dma_start(c.gate_raw[:, 0:4], d["g_xattn"].partition_broadcast(P)).then_inc(c.gates_in, 16)
            act.dma_start(c.gate_raw[:, 4:8], d["g_ffn"].partition_broadcast(P)).then_inc(c.gates_in, 16)


def start(c):
    nc = c.nc
    with ExitStack() as st:
        ident_set, ident_ready, gates_ready, consts = (c.sem(st, n) for n in (
            "ident_set", "ident_ready", "gates_ready", "consts"))
        with nc.Block() as block:
            @block.sync
            def _(sp):
                sp.wait_ge(c.x_in, 16)

            @block.scalar
            def _(act):
                act.wait_ge(c.gates_in, 32)
                nc.scalar.activation(c.gate[:], c.gate_raw[:], ACT.Tanh).then_inc(gates_ready, 1)
                act.wait_ge(c.ctx_in, 16)

            @block.vector
            def _(dve):
                nc.vector.memset(c.mhalf[:], -0.5).then_inc(consts, 1)

            @block.gpsimd
            def _(pool):
                nc.gpsimd.memset(c.ident[:], 0.0).then_inc(ident_set, 1)
                pool.wait_ge(ident_set, 1)
                nc.gpsimd.affine_select(out=c.ident[:], in_=c.ident[:], compare_op=ALU.not_equal, fill=1.0, base=0,
                                        pattern=[[-1, P]], channel_multiplier=1).then_inc(ident_set, 1)
                pool.wait_ge(ident_set, 2)
                nc.gpsimd.tensor_copy(c.identb[:], c.ident[:]).then_inc(ident_ready, 1)
        transpose_tokens(c, c.norm, c.ctxT)


def finish(c, out):
    nc = c.nc
    with ExitStack() as st:
        stored = c.sem(st, "stored")
        with nc.Block() as block:
            @block.sync
            def _(sp):
                sp.dma_start(out.rearrange("(t p) d -> p t d", p=P), c.resid[:]).then_inc(stored, 16)
                sp.wait_ge(stored, 16)



def pe_transpose_tokens(c, pe, src, ready, transposed):
    for t in range(NT):
        if ready is not None:
            pe.wait_ge(ready, t + 1)
        for k in range(KC):
            last = c.nc.tensor.transpose(c.psum[:, t // 2, k * 256 + t % 2 * P:k * 256 + t % 2 * P + P],
                                         src[:, t, k * P:(k + 1) * P], c.ident[:])
        last.then_inc(transposed, 1)


def act_store_transposed(c, act, dst, transposed, stored):
    for g in range(NT // 2):
        act.wait_ge(transposed, 2 * g + 2)
        c.nc.scalar.activation(dst[:, :, g * 256:(g + 1) * 256],
                               c.psum[:, g, :].rearrange("p (k n) -> p k n", k=KC), ACT.Copy).then_inc(stored, 1)


def transpose_tokens(c, src, dst):
    nc = c.nc
    with ExitStack() as st:
        transposed, stored = c.sem(st, "transposed"), c.sem(st, "stored")
        with nc.Block() as block:
            @block.tensor
            def _(pe):
                pe_transpose_tokens(c, pe, src, None, transposed)

            @block.scalar
            def _(act):
                act_store_transposed(c, act, dst, transposed, stored)


def layernorm(c, src, dst, dstT, eps=1e-5, clear=None):
    nc, halves = c.nc, (range(0, NT // 2), range(NT // 2, NT))
    with ExitStack() as st:
        chain_s, var_ready, rstd_ready, norm_ready, transposed, stored, ln_cleared = (c.sem(st, n) for n in (
            "ln_chain", "var_ready", "rstd_ready", "norm_ready", "transposed", "stored", "ln_cleared"))
        with nc.Block() as block:
            @block.vector
            def _(dve):
                chain, v = Chain(dve, chain_s), nc.vector
                for half in halves:
                    for t in half:
                        chain.add(v.bn_stats(c.stats[:, t, :], src[:, t, :]))
                    chain.join()
                    for t in half:
                        chain.add(v.bn_aggr(c.mv[:, t, :], c.stats[:, t, :]))
                    chain.join()
                    part = slice(half[0], half[-1] + 1)
                    v.tensor_scalar(c.ve[:, part], c.mv[:, part, 1], eps, None, ALU.add).then_inc(var_ready, 1)
                for n, half in enumerate(halves):
                    dve.wait_ge(rstd_ready, n + 1)
                    for t in half:
                        v.tensor_scalar(dst[:, t, :], src[:, t, :], c.mv[:, t, 0:1], c.rstd[:, t:t + 1],
                                        ALU.subtract, ALU.mult).then_inc(norm_ready, 1)

            @block.gpsimd
            def _(pool):
                for n, half in enumerate(halves):
                    part = slice(half[0], half[-1] + 1)
                    pool.wait_ge(var_ready, n + 1)
                    nc.gpsimd.tensor_tensor(c.rstd[:, part], c.ve[:, part], c.mhalf[:, 0:len(half)], ALU.pow
                                            ).then_inc(rstd_ready, 1)
                if clear is not None:
                    nc.gpsimd.memset(clear[:], 0.0).then_inc(ln_cleared, 1)

            if dstT is not None:
                @block.tensor
                def _(pe):
                    pe_transpose_tokens(c, pe, dst, norm_ready, transposed)

                @block.scalar
                def _(act):
                    act_store_transposed(c, act, dstT, transposed, stored)



def ffn(c, gu, dn, f, xT, acc, scaled=False, beside=None):
    nc, chunks = c.nc, gu.shape[0]
    unroll = 2
    wdn = HID + (2 if scaled else 0)
    with ExitStack() as st:
        gu_in = [c.sem(st, f"gu_in{b}") for b in range(2)]
        dn_in = [c.sem(st, f"dn_in{b}") for b in range(2)]
        gu_ready, act_ready, h_ready, dn_ready, acc_done = (c.sem(st, n) for n in (
            "gu_ready", "act_ready", "h_ready", "dn_ready", "acc_done"))
        wgu = c.sb(st, "wgu", [P, 2, KC, 2 * f])
        wd = c.sb(st, "wd", [f, 2, wdn])
        sg = c.sb(st, "silu", [f, 2, HALF])
        hT = c.sb(st, "hT", [f, 2, HALF])
        with nc.Block() as block:
            if beside is not None:
                block.gpsimd(beside)

            @block.sync
            def _(sp):
                sp.sem_inc(dn_ready, 4)
                with sp.Fori(0, chunks // unroll) as i:
                    for u in range(unroll):
                        j, b = unroll * i + u, u % 2
                        sp.wait_ge(dn_ready, 2 * j + 2)
                        sp.dma_start(wgu[:, b], gu[bass.ds(j, 1)].rearrange("o p k f -> p (o k) f")
                                     ).then_inc(gu_in[b], 16)
                        sp.dma_start(wd[:, b], dn[bass.ds(j, 1)].rearrange("o p k -> p (o k)")
                                     ).then_inc(dn_in[b], 16)

            @block.tensor
            def _(pe):
                with pe.Fori(0, chunks // unroll) as i:
                    for c_ in range(unroll):
                        j, b = unroll * i + c_, c_ % 2
                        landed = 16 * (unroll // 2 * i + c_ // 2 + 1)
                        pe.wait_ge(gu_in[b], landed)
                        for half in range(2):
                            pe.wait_ge(h_ready, 2 * j + half + 1)
                            for u in range(2):
                                for k in range(KC):
                                    last = nc.tensor.matmul(c.psum[0:f, 2 * half + u, :],
                                                            wgu[:, b, k, u * f:(u + 1) * f],
                                                            xT[:, k, half * HALF:(half + 1) * HALF],
                                                            start=k == 0, stop=k == KC - 1)
                            last.then_inc(gu_ready, 1)
                        pe.wait_ge(dn_in[b], landed)
                        for half in range(2):
                            pe.wait_ge(h_ready, 2 * j + half + 3)
                            pe.wait_ge(acc_done, 2 * j + half + 1)
                            for q in range(4):
                                last = nc.tensor.matmul(c.psum[:, 4 + 2 * half + q // 2,
                                                               q % 2 * HID:(q % 2 + 1) * HID],
                                                        hT[:, half, q * P:(q + 1) * P], wd[:, b, 0:HID],
                                                        start=True, stop=True)
                            last.then_inc(dn_ready, 1)

            @block.scalar
            def _(act):
                with act.Fori(0, chunks // unroll) as i:
                    for u in range(unroll):
                        j, b = unroll * i + u, u % 2
                        if scaled:
                            act.wait_ge(dn_in[b], 16 * (unroll // 2 * i + u // 2 + 1))
                        for half in range(2):
                            act.wait_ge(gu_ready, 2 * j + half + 1)
                            act.wait_ge(h_ready, 2 * j + half + 1)
                            scale = wd[:, b, HID:HID + 1] if scaled else 1.0
                            nc.scalar.activation(sg[:, half], c.psum[0:f, 2 * half, :], ACT.Silu,
                                                 scale=scale).then_inc(act_ready, 1)

            @block.vector
            def _(dve):
                dve.sem_inc(h_ready, 2)
                dve.sem_inc(acc_done, 2)
                with dve.Fori(0, chunks // unroll) as i:
                    for u in range(unroll):
                        j, b = unroll * i + u, u % 2
                        for half in range(2):
                            dve.wait_ge(act_ready, 2 * j + half + 1)
                            dve.wait_ge(dn_ready, 2 * j + 4)
                            if scaled:
                                ins = nc.vector.scalar_tensor_tensor(
                                    out=hT[:, half], in0=c.psum[0:f, 2 * half + 1, :],
                                    scalar=wd[:, b, HID + 1:HID + 2], in1=sg[:, half], op0=ALU.mult, op1=ALU.mult)
                            else:
                                ins = nc.vector.tensor_tensor(hT[:, half], c.psum[0:f, 2 * half + 1, :], sg[:, half],
                                                              ALU.mult)
                            ins.then_inc(h_ready, 1)
                        for half in range(2):
                            dve.wait_ge(dn_ready, 2 * j + half + 5)
                            dve.wait_ge(acc_done, 2 * j + half + 1)
                            for q in range(0, 4, 2):
                                t = 4 * half + q
                                last = nc.vector.tensor_tensor(
                                    acc[:, t:t + 2, :],
                                    c.psum[:, 4 + 2 * half + q // 2, :].rearrange("p (t n) -> p t n", t=2),
                                    acc[:, t:t + 2, :], ALU.add)
                            last.then_inc(acc_done, 1)


def add_gated(c, acc, gate, col_scale=None):
    nc = c.nc
    with ExitStack() as st:
        scaled_s, added = c.sem(st, "scaled"), c.sem(st, "added")
        with nc.Block() as block:
            @block.vector
            def _(dve):
                if col_scale is not None:
                    nc.vector.tensor_tensor(acc[:], acc[:], col_scale[:].unsqueeze(1).to_broadcast([P, NT, HID]),
                                            ALU.mult).then_inc(scaled_s, 1)
                    dve.wait_ge(scaled_s, 1)
                nc.vector.scalar_tensor_tensor(out=c.resid[:], in0=acc[:], scalar=c.gate[:, gate:gate + 1],
                                               in1=c.resid[:], op0=ALU.mult, op1=ALU.add).then_inc(added, 1)



def softmax_rows(c, dve, chain, logits, p, small, exp_go, exp_done, n, turn=1):
    v = c.nc.vector
    chain.after(v.tensor_reduce(small[:, 0, :], logits, X, ALU.max))
    v.tensor_tensor(p[:], logits, bc(small[:, 0, :], [P, NT, n]), ALU.subtract).then_inc(exp_go, 1)
    dve.wait_ge(exp_done, turn)
    chain.after(v.tensor_reduce(small[:, 0, :], p[:], X, ALU.add))
    chain.after(v.reciprocal(small[:, 1, :], small[:, 0, :]))
    chain.after(v.tensor_tensor(p[:], p[:], bc(small[:, 1, :], [P, NT, n]), ALU.mult))


def top_onehots(c, chain, values, top, idx, idxf, iota, onehot, k, n):
    v = c.nc.vector
    for t in range(NT):
        chain.add(v.max(top[:, t, :], values[:, t, :]))
    chain.join()
    for t in range(NT):
        chain.add(v.max_index(idx[:, t, :], top[:, t, :], values[:, t, :]))
    chain.join()
    chain.after(v.tensor_copy(idxf[:], idx[:]))
    for i in range(k):
        chain.add(v.tensor_tensor(onehot[:, :, i, :], iota[:].unsqueeze(1).to_broadcast([P, NT, n]),
                                  idxf[:, :, i:i + 1].to_broadcast([P, NT, n]), ALU.is_equal))
    chain.join()


def pe_logits(c, pe, wr, bank, n):
    for t in range(NT):
        for k in range(KC):
            last = c.nc.tensor.matmul(c.psum[:, bank, t * n:(t + 1) * n], c.xT[:, k, t * P:(t + 1) * P],
                                      wr[:, k, :], start=k == 0, stop=k == KC - 1)
    return last


def router0(c, comb):
    nc, d, E, K, S = c.nc, c.dram, 32, 8, 4
    with ExitStack() as st:
        wr_in, sim_in, consts, bd_ready, chain_s, logits_ready, exp_go, exp_done, oh_ready, oh_turned, oh_stored, \
            rows_ready = (c.sem(st, n) for n in (
                "wr_in", "sim_in", "consts", "bd_ready", "chain", "logits_ready", "exp_go", "exp_done", "oh_ready",
                "oh_turned", "oh_stored", "rows_ready"))
        wr = c.sb(st, "wr", [P, KC, E])
        simbd = c.sb(st, "simbd", [P, P])
        iota = c.sb(st, "iota", [P, E])
        p = c.sb(st, "p", [P, NT, E])
        small = c.sb(st, "small", [P, 2, NT])
        top = c.sb(st, "top", [P, NT, K])
        rw = c.sb(st, "rw", [P, NT, K])
        idx = c.sb(st, "idx", [P, NT, K], U32)
        idxf = c.sb(st, "idxf", [P, NT, K])
        oh = c.sb(st, "oh", [P, NT, K, E])
        secT = c.sb(st, "secT", [P, NT, P])
        cand4 = c.sb(st, "cand4", [P, NT, S, E])
        cand = c.sb(st, "cand", [P, NT * S, S])
        best = c.sb(st, "best", [P, NT * S])
        eq = c.sb(st, "eq", [P, NT * S, S])
        seen = c.sb(st, "seen", [P, NT * S])
        moved = c.sb(st, "moved", [P, NT, S])
        coef = c.sb(st, "coef", [P, NT, K])
        add = c.sb(st, "add", [P, NT, S])
        with nc.Block() as block:
            @block.sync
            def _(sp):
                sp.dma_start(wr[:], d["L0_router"]).then_inc(wr_in, 16)
                sp.wait_ge(bd_ready, 1)
                for j in range(S):
                    sp.dma_start(simbd[j * E:(j + 1) * E, j * E:(j + 1) * E],
                                 d["L0_ffn_similarity"]).then_inc(sim_in, 16)

            @block.gpsimd
            def _(pool):
                nc.gpsimd.iota(iota[:], pattern=[[1, E]], base=0, channel_multiplier=0,
                               allow_small_or_imprecise_dtypes=True).then_inc(consts, 1)

            @block.tensor
            def _(pe):
                pe.wait_ge(wr_in, 16)
                pe_logits(c, pe, wr, 0, E).then_inc(logits_ready, 1)
                pe.wait_ge(oh_ready, 1)
                for t in range(NT):
                    last = nc.tensor.transpose(c.psum[:, 1 + t // 4, t % 4 * P:(t % 4 + 1) * P],
                                               oh[:, t, S:K, :], c.ident[:])
                last.then_inc(oh_turned, 1)
                pe.wait_ge(oh_stored, 2)
                pe.wait_ge(sim_in, 16 * S)
                for t in range(NT):
                    last = nc.tensor.matmul(c.psum[:, 3 + t // 4, t % 4 * P:(t % 4 + 1) * P], secT[:, t, :],
                                            simbd[:], start=True, stop=True)
                last.then_inc(rows_ready, 1)

            @block.scalar
            def _(act):
                act.wait_ge(exp_go, 1)
                nc.scalar.activation(p[:], p[:], ACT.Exp).then_inc(exp_done, 1)
                act.wait_ge(oh_turned, 1)
                for h in range(2):
                    nc.scalar.activation(secT[:, 4 * h:4 * h + 4, :],
                                         c.psum[:, 1 + h, :].rearrange("p (t n) -> p t n", t=4),
                                         ACT.Copy).then_inc(oh_stored, 1)

            @block.vector
            def _(dve):
                v, chain = nc.vector, Chain(dve, chain_s)
                v.memset(simbd[:], 0.0).then_inc(bd_ready, 1)
                dve.wait_ge(logits_ready, 1)
                logits = c.psum[:, 0, 0:NT * E].rearrange("p (t e) -> p t e", t=NT)
                softmax_rows(c, dve, chain, logits, p, small, exp_go, exp_done, E)
                dve.wait_ge(consts, 1)
                top_onehots(c, chain, p, top, idx, idxf, iota, oh, K, E)
                v.tensor_reduce(small[:, 0, :], top[:], X, ALU.add).then_inc(oh_ready, 1)
                dve.wait_ge(oh_ready, 1)
                chain.after(v.tensor_scalar(small[:, 0, :], small[:, 0, :], 1e-12, None, ALU.max))
                chain.after(v.reciprocal(small[:, 1, :], small[:, 0, :]))
                chain.after(v.tensor_tensor(rw[:], top[:], bc(small[:, 1, :], [P, NT, K]), ALU.mult))
                dve.wait_ge(rows_ready, 1)
                for i in range(S):
                    for h in range(2):
                        rows = c.psum[:, 3 + h, :].rearrange("p (t j e) -> p t j e", t=4, j=S)
                        chain.add(v.tensor_tensor(
                            cand4[:, 4 * h:4 * h + 4], rows,
                            oh[:, 4 * h:4 * h + 4, i, :].unsqueeze(2).to_broadcast([P, 4, S, E]), ALU.mult))
                    chain.join()
                    chain.after(v.tensor_reduce(cand[:, :, i], cand4[:].rearrange("p t j e -> p (t j) e"), X, ALU.add))
                chain.after(v.tensor_reduce(best[:], cand[:], X, ALU.max))
                chain.after(v.tensor_tensor(eq[:], cand[:], bc(best[:], [P, NT * S, S]), ALU.is_equal))
                chain.after(v.tensor_copy(seen[:], eq[:, :, 0]))
                for i in range(1, S):
                    chain.after(v.scalar_tensor_tensor(out=eq[:, :, i], in0=seen[:], scalar=0.5, in1=eq[:, :, i],
                                                       op0=ALU.is_lt, op1=ALU.mult))
                    chain.after(v.tensor_tensor(seen[:], seen[:], eq[:, :, i], ALU.max))
                best3 = best[:].rearrange("p (t j) -> p t j", j=S)
                chain.after(v.scalar_tensor_tensor(out=coef[:, :, S:K], in0=best3, scalar=0.5, in1=rw[:, :, S:K],
                                                   op0=ALU.is_lt, op1=ALU.mult))
                chain.after(v.tensor_tensor(moved[:], rw[:, :, S:K], coef[:, :, S:K], ALU.subtract))
                eq4 = eq[:].rearrange("p (t j) i -> p t j i", j=S)
                chain.after(v.tensor_tensor(eq4, eq4, bc(moved[:], [P, NT, S, S]), ALU.mult))
                chain.after(v.tensor_reduce(add[:], eq[:].rearrange("p (t j) i -> p t i j", j=S), X, ALU.add))
                chain.after(v.tensor_tensor(coef[:, :, 0:S], rw[:, :, 0:S], add[:], ALU.add))
                for i in range(K):
                    chain.add(v.tensor_tensor(oh[:, :, i, :], oh[:, :, i, :],
                                              coef[:, :, i:i + 1].to_broadcast([P, NT, E]), ALU.mult))
                chain.join()
                chain.after(v.tensor_reduce(comb[:], oh[:].rearrange("p t k e -> p t e k"), X, ALU.add))


def slots_before(c, pe, bank, before, ones, mask, n):
    for t in range(NT):
        for s in range(t + 1):
            last = c.nc.tensor.matmul(c.psum[:, bank, t * n:(t + 1) * n], before[:] if s == t else ones[:],
                                      mask[:, s, :], start=s == 0, stop=s == t)
    return last


def router2(c, weight, put, get, widx):
    nc, d, E, K, CAP = c.nc, c.dram, 16, 4, 128
    with ExitStack() as st:
        wr_in, consts, chain_s, logits_ready, exp_go, exp_done, mask_ready, rank_ready = (c.sem(st, n) for n in (
            "wr_in", "consts", "chain", "logits_ready", "exp_go", "exp_done", "mask_ready", "rank_ready"))
        wr = c.sb(st, "wr", [P, KC, E])
        iota = c.sb(st, "iota", [P, E])
        ones = c.sb(st, "ones", [P, P])
        before = c.sb(st, "before", [P, P])
        p = c.sb(st, "p", [P, NT, E])
        small = c.sb(st, "small", [P, 2, NT])
        top = c.sb(st, "top", [P, NT, 8])
        rw = c.sb(st, "rw", [P, NT, K])
        idx = c.sb(st, "idx", [P, NT, 8], U32)
        idxf = c.sb(st, "idxf", [P, NT, 8])
        oh = c.sb(st, "oh", [P, NT, K, E])
        mask = c.sb(st, "mask", [P, NT, E])
        first = c.sb(st, "first", [P, E])
        spare = c.sb(st, "spare", [P, NT, K])
        tile_row = c.sb(st, "tile_row", [P, E])
        slot = c.sb(st, "slot", [P, NT, E])
        chosen = c.sb(st, "chosen", [P, NT, K, E])
        rank_of, slot_of, keep = (c.sb(st, n, [P, NT, K]) for n in ("rank_of", "slot_of", "keep"))
        with nc.Block() as block:
            @block.sync
            def _(sp):
                sp.dma_start(wr[:], d["L2_router"]).then_inc(wr_in, 16)

            @block.gpsimd
            def _(pool):
                nc.gpsimd.iota(iota[:], pattern=[[1, E]], base=0, channel_multiplier=0,
                               allow_small_or_imprecise_dtypes=True).then_inc(consts, 1)
                nc.gpsimd.memset(ones[:], 1.0).then_inc(consts, 1)
                for dst, pattern, base, per_row in ((first, [[CAP, E]], 0, 0), (tile_row, [[P, E]], 0, 1),
                                                    (spare, [[P, NT], [TOK, K]], E * CAP, 1)):
                    nc.gpsimd.iota(dst[:], pattern=pattern, base=base, channel_multiplier=per_row,
                                   allow_small_or_imprecise_dtypes=True).then_inc(consts, 1)
                nc.gpsimd.memset(before[:], 1.0).then_inc(consts, 1)
                pool.wait_ge(consts, 6)
                nc.gpsimd.affine_select(out=before[:], in_=before[:], compare_op=ALU.is_gt, fill=0.0, base=0,
                                        pattern=[[1, P]], channel_multiplier=-1).then_inc(consts, 1)

            @block.tensor
            def _(pe):
                pe.wait_ge(wr_in, 16)
                pe_logits(c, pe, wr, 0, E).then_inc(logits_ready, 1)
                pe.wait_ge(consts, 7)
                pe.wait_ge(mask_ready, 1)
                slots_before(c, pe, 1, before, ones, mask, E).then_inc(rank_ready, 1)

            @block.scalar
            def _(act):
                act.wait_ge(exp_go, 1)
                nc.scalar.activation(p[:], p[:], ACT.Exp).then_inc(exp_done, 1)

            @block.vector
            def _(dve):
                v, chain = nc.vector, Chain(dve, chain_s)
                dve.wait_ge(logits_ready, 1)
                logits = c.psum[:, 0, 0:NT * E].rearrange("p (t e) -> p t e", t=NT)
                softmax_rows(c, dve, chain, logits, p, small, exp_go, exp_done, E)
                dve.wait_ge(consts, 7)
                top_onehots(c, chain, p, top, idx, idxf, iota, oh, K, E)
                v.tensor_reduce(mask[:], oh[:].rearrange("p t k e -> p t e k"), X, ALU.add).then_inc(mask_ready, 1)
                chain.after(v.tensor_reduce(small[:, 0, :], top[:, :, 0:K], X, ALU.add))
                chain.after(v.tensor_scalar(small[:, 0, :], small[:, 0, :], 1e-20, None, ALU.add))
                chain.after(v.reciprocal(small[:, 1, :], small[:, 0, :]))
                chain.after(v.tensor_tensor(rw[:], top[:, :, 0:K], bc(small[:, 1, :], [P, NT, K]), ALU.mult))
                chain.after(v.tensor_copy(widx[:], tile_row[:]))
                dve.wait_ge(rank_ready, 1)
                rank = c.psum[:, 1, 0:NT * E].rearrange("p (t e) -> p t e", t=NT)
                chain.after(v.tensor_tensor(slot[:], rank, first[:].unsqueeze(1).to_broadcast([P, NT, E]), ALU.add))
                for values, of in ((rank, rank_of), (slot[:], slot_of)):
                    for i in range(K):
                        chain.add(v.tensor_tensor(chosen[:, :, i, :], oh[:, :, i, :], values, ALU.mult))
                    chain.join()
                    chain.after(v.tensor_reduce(of[:], chosen[:], X, ALU.add))
                chain.after(v.tensor_scalar(keep[:], rank_of[:], CAP - 0.5, None, ALU.is_lt))
                chain.after(v.tensor_tensor(weight[:], rw[:], keep[:], ALU.mult))
                chain.after(v.tensor_scalar(get[:], slot_of[:], E * CAP - 1.0, None, ALU.min))
                chain.after(v.tensor_tensor(slot_of[:], slot_of[:], spare[:], ALU.subtract))
                chain.after(v.tensor_tensor(slot_of[:], slot_of[:], keep[:], ALU.mult))
                chain.after(v.tensor_tensor(put[:], slot_of[:], spare[:], ALU.add))


def router3(c, put, widx, tiles):
    nc, d, E = c.nc, c.dram, 8
    with ExitStack() as st:
        wr_in, consts, chain_s, logits_ready, top_ready, exp_done, scaled, rank_ready, mask_ready = (c.sem(st, n) for n in (
            "wr_in", "consts", "chain", "logits_ready", "top_ready", "exp_done", "scaled", "rank_ready", "mask_ready"))
        wr = c.sb(st, "wr", [P, KC, E])
        iota = c.sb(st, "iota", [P, E])
        logits = c.sb(st, "logits", [P, NT, E])
        top = c.sb(st, "top", [P, NT, 8])
        idx = c.sb(st, "idx", [P, NT, 8], U32)
        idxf = c.sb(st, "idxf", [P, NT, 8])
        sig = c.sb(st, "sig", [P, 2, NT])
        oh = c.sb(st, "oh", [P, NT, 1, E])
        ones = c.sb(st, "ones", [P, P])
        before = c.sb(st, "before", [P, P])
        numbers = c.sb(st, "numbers", [P, 16])
        row = c.sb(st, "row", [P, 1])
        mask = c.sb(st, "mask", [P, NT, E])
        count, first, last_, slot_of = (c.sb(st, n, [P, E]) for n in ("count", "first", "last", "slot_of"))
        earlier = c.sb(st, "earlier", [P, E, E])
        passed = c.sb(st, "passed", [P, tiles, E])
        slot = c.sb(st, "slot", [P, NT, E])
        wrow = c.sb(st, "wrow", [P, tiles])
        with nc.Block() as block:
            @block.sync
            def _(sp):
                sp.dma_start(wr[:], d["L3_router"]).then_inc(wr_in, 16)

            @block.gpsimd
            def _(pool):
                for dst, pattern, per_row in ((iota, [[1, E]], 0), (numbers, [[1, 16]], 0), (row, [[1, 1]], 1)):
                    nc.gpsimd.iota(dst[:], pattern=pattern, base=0, channel_multiplier=per_row,
                                   allow_small_or_imprecise_dtypes=True).then_inc(consts, 1)
                nc.gpsimd.memset(ones[:], 1.0).then_inc(consts, 1)
                nc.gpsimd.memset(before[:], 1.0).then_inc(consts, 1)
                pool.wait_ge(consts, 5)
                nc.gpsimd.affine_select(out=before[:], in_=before[:], compare_op=ALU.is_gt, fill=0.0, base=0,
                                        pattern=[[1, P]], channel_multiplier=-1).then_inc(consts, 1)

            @block.tensor
            def _(pe):
                pe.wait_ge(wr_in, 16)
                pe_logits(c, pe, wr, 7, E).then_inc(logits_ready, 1)
                pe.wait_ge(consts, 6)
                pe.wait_ge(mask_ready, 1)
                slots_before(c, pe, 1, before, ones, mask, E)
                for t in range(NT):
                    last = nc.tensor.matmul(c.psum[:, 2, 0:E], ones[:], mask[:, t, :], start=t == 0, stop=t == NT - 1)
                last.then_inc(rank_ready, 1)

            @block.scalar
            def _(act):
                act.wait_ge(top_ready, 1)
                nc.scalar.activation(sig[:, 0, :], top[:, :, 0], ACT.Exp, scale=-1.0).then_inc(exp_done, 1)

            @block.vector
            def _(dve):
                v, chain = nc.vector, Chain(dve, chain_s)
                dve.wait_ge(logits_ready, 1)
                chain.after(v.tensor_copy(logits[:], c.psum[:, 7, 0:NT * E].rearrange("p (t e) -> p t e", t=NT)))
                dve.wait_ge(consts, 6)
                top_onehots(c, chain, logits, top, idx, idxf, iota, oh, 1, E)
                v.tensor_copy(mask[:], oh[:, :, 0, :]).then_inc(mask_ready, 1)
                dve.sem_inc(top_ready, 1)
                dve.wait_ge(exp_done, 1)
                chain.after(v.tensor_scalar(sig[:, 1, :], sig[:, 0, :], 1.0, None, ALU.add))
                chain.after(v.reciprocal(sig[:, 0, :], sig[:, 1, :]))
                for t in range(NT):
                    v.tensor_scalar(c.norm[:, t, :], c.norm[:, t, :], sig[:, 0, t:t + 1], None,
                                    ALU.mult).then_inc(scaled, 1)
                dve.wait_ge(rank_ready, 1)
                chain.after(v.tensor_scalar(count[:], c.psum[:, 2, 0:E], 1.0 / P, 0.5 - 0.5 / P, ALU.mult, ALU.add))
                chain.after(v.tensor_scalar(count[:], count[:], ROUND, ROUND, ALU.add, ALU.subtract))
                iota_e, iota_j = (iota[:].unsqueeze(a).to_broadcast([P, E, E]) for a in (2, 1))
                chain.after(v.tensor_tensor(earlier[:], iota_j, iota_e, ALU.is_lt))
                chain.after(v.tensor_tensor(earlier[:], earlier[:], count[:].unsqueeze(1).to_broadcast([P, E, E]),
                                            ALU.mult))
                chain.after(v.tensor_reduce(first[:], earlier[:], X, ALU.add))
                chain.after(v.tensor_tensor(last_[:], first[:], count[:], ALU.add))
                chain.after(v.tensor_tensor(passed[:], last_[:].unsqueeze(1).to_broadcast([P, tiles, E]),
                                            bc(numbers[:, 0:tiles], [P, tiles, E]), ALU.is_le))
                chain.after(v.tensor_reduce(wrow[:], passed[:], X, ALU.add))
                chain.after(v.tensor_scalar(wrow[:], wrow[:], E - 1.0, float(P), ALU.min, ALU.mult))
                chain.after(v.tensor_scalar(widx[:], wrow[:], row[:, 0:1], None, ALU.add))
                chain.after(v.tensor_scalar(first[:], first[:], float(P), None, ALU.mult))
                rank = c.psum[:, 1, 0:NT * E].rearrange("p (t e) -> p t e", t=NT)
                chain.after(v.tensor_tensor(slot[:], rank, first[:].unsqueeze(1).to_broadcast([P, NT, E]), ALU.add))
                dve.wait_ge(mask_ready, 1)
                chain.after(v.tensor_tensor(slot[:], slot[:], mask[:], ALU.mult))
                chain.after(v.tensor_reduce(sig[:, 1, :], slot[:], X, ALU.add))
                chain.after(v.tensor_copy(put[:], sig[:, 1, :]))



def packed_ffn(c, comb, experts, f, gate):
    nc, d = c.nc, c.dram
    group = next(n for n in range(1, experts) if n * P % f == 0)
    whole = group * P // f
    with ExitStack() as st:
        turned, stored, comb_out, h_read, silu_done, products, h_done, outputs, added = (c.sem(st, n) for n in (
            "turned", "stored", "comb_out", "h_read", "silu_done", "products", "h_done", "outputs", "added"))
        w_in = [c.sem(st, f"w_in{u}") for u in range(group)]
        comb_in = [c.sem(st, f"comb_in{u}") for u in range(group)]
        combT = c.sb(st, "combT", [experts, TOK])
        wgu = c.sb(st, "wgu", [P, group, KC, 2 * P])
        wd = c.sb(st, "wd", [P, group, HID])
        by_row = c.sb(st, "by_row", [P, group, TOK])
        sg = c.sb(st, "silu", [P, 2, HALF])
        hT = c.sb(st, "hT", [P, 2, HALF])
        with nc.Block() as block:
            @block.tensor
            def _(pe):
                for t in range(NT):
                    last = nc.tensor.transpose(c.psum[0:experts, t // 4, t % 4 * P:(t % 4 + 1) * P], comb[:, t, :],
                                               c.ident[:])
                last.then_inc(turned, 1)

            @block.scalar
            def _(act):
                act.wait_ge(turned, 1)
                nc.scalar.activation(combT[:], c.psum[0:experts, 0:2, :].rearrange("p b n -> p (b n)"), ACT.Copy
                                     ).then_inc(stored, 1)

            @block.sync
            def _(sp):
                sp.wait_ge(stored, 1)
                sp.dma_start(d["L0_comb"], combT[:]).then_inc(comb_out, 16)

        units, steps = 2 * group, experts * f // P // group
        with nc.Block() as block:
            @block.sync
            def _(sp):
                def fetch(i, u):
                    m = group * i + u
                    wait(sp, outputs, 2 * (m - group) + 2)
                    sp.dma_start(wgu[:, u], d["L0_gu"][bass.ds(m, 1)].rearrange("o p k f -> p (o k) f")
                                 ).then_inc(w_in[u], 16)
                    sp.dma_start(wd[:, u], d["L0_dn"][bass.ds(m, 1)].rearrange("o p k -> p (o k)")).then_inc(w_in[u], 16)
                    if isinstance(i, int) and u == 0:
                        sp.wait_ge(comb_out, 16)
                    split = (u * P // f + 1) * f - u * P
                    for k, rows in enumerate((slice(0, split), slice(split, P))):
                        sp.dma_start(by_row[rows, u], d["L0_comb"][bass.ds(whole * i + u * P // f + k, 1)].to_broadcast(
                            [rows.stop - rows.start, TOK])).then_inc(comb_in[u], 16)

                run_tiles(sp, [("L", u, 0) for u in range(group)], {"L": fetch}, count=steps)

            @block.tensor
            def _(pe):
                def gate_up(i, v):
                    n, u, half = units * i + v, v // 2, v % 2
                    if half == 0:
                        pe.wait_ge(w_in[u], 32 * (i + 1))
                    wait(pe, h_read, n - 1)
                    for side in range(2):
                        for k in range(KC):
                            last = nc.tensor.matmul(c.psum[:, 2 * half + side, :], wgu[:, u, k, side * P:(side + 1) * P],
                                                    c.xT[:, k, half * HALF:(half + 1) * HALF], start=k == 0,
                                                    stop=k == KC - 1)
                    last.then_inc(products, 1)

                def down(i, v):
                    n, u, half = units * i + v, v // 2, v % 2
                    pe.wait_ge(h_done, n + 1)
                    first, final = (isinstance(i, int) and n // 2 == m for m in (0, group * steps - 1))
                    for q in range(4):
                        last = nc.tensor.matmul(c.psum[:, 4 + 2 * half + q // 2, q % 2 * HID:(q % 2 + 1) * HID],
                                                hT[:, half, q * P:(q + 1) * P], wd[:, u, :],
                                                start=first and q % 2 == 0, stop=final and q % 2 == 1)
                    last.then_inc(outputs, 1)

                run_tiles(pe, delayed("G", "D", units), {"G": gate_up, "D": down}, count=steps,
                          peel_last=True)

            @block.scalar
            def _(act):
                def silu(i, v):
                    act.wait_ge(products, units * i + v + 1)
                    nc.scalar.activation(sg[:, v % 2], c.psum[:, v % 2 * 2, :], ACT.Silu).then_inc(silu_done, 1)

                run_tiles(act, [("S", v, 0) for v in range(units)], {"S": silu}, count=steps)

            @block.vector
            def _(dve):
                def hidden(i, v):
                    n, u, half = units * i + v, v // 2, v % 2
                    dve.wait_ge(silu_done, n + 1)
                    wait(dve, outputs, n - 1)
                    nc.vector.tensor_tensor(hT[:, half], c.psum[:, 2 * half + 1, :], sg[:, half], ALU.mult
                                            ).then_inc(h_read, 1)
                    if half == 0:
                        dve.wait_ge(comb_in[u], 32 * (i + 1))
                    dve.wait_ge(h_read, n + 1)
                    nc.vector.tensor_tensor(hT[:, half], hT[:, half], by_row[:, u, half * HALF:(half + 1) * HALF],
                                            ALU.mult).then_inc(h_done, 1)

                run_tiles(dve, [("H", v, 0) for v in range(units)], {"H": hidden}, count=steps)
                dve.wait_ge(outputs, units * steps)
                for b in range(NT // 2):
                    at = c.resid[:, 2 * b:2 * b + 2, :]
                    nc.vector.scalar_tensor_tensor(out=at, in0=c.psum[:, 4 + b, :].rearrange("p (t n) -> p t n", t=2),
                                                   scalar=gate, in1=at, op0=ALU.mult, op1=ALU.add).then_inc(added, 1)


def ffn0(c):
    with ExitStack() as st:
        comb = c.sb(st, "comb", [P, NT, 32])
        layernorm(c, c.resid, c.norm, c.xT)
        router0(c, comb)
        packed_ffn(c, comb, 32, 96, c.gate[:, 4:5])


def ffn1(c):
    with ExitStack() as st:
        acc, down_s = c.sb(st, "acc", [P, NT, HID]), c.sb(st, "down_s", [P, HID])
        loads = Loads(c, [(down_s, c.dram["L1_ffn_down_s"].partition_broadcast(P))])
        layernorm(c, c.resid, c.norm, c.xT, clear=acc)
        loads.finish()
        ffn(c, c.dram["L1_gu"], c.dram["L1_dn"], P, c.xT, acc, scaled=True)
        add_gated(c, acc, 5, down_s)


def sparse_ffn(c, name, chunks, f, choices, tiles, unroll, put, get, widx, weight, shared, acc, slots_zeroed):
    nc, d = c.nc, c.dram
    rows = tiles * P
    xs, ys = d[name + "_slots"], d[name + "_outs"]
    wgu, wdn = chunks * KC * 2 * f, chunks * HID
    with ExitStack() as st:
        scattered, x_in, y_out = (c.sem(st, n) for n in ("scattered", "x_in", "y_out"))
        with ExitStack() as inner:
            xg = c.sb(inner, "xg", [P, tiles, HID])
            xgT = c.sb(inner, "xgT", [P, KC, rows])
            w = c.sb(inner, "w", [P, unroll, wgu + wdn])
            w_in = [c.sem(st, f"w_in{u}") for u in range(unroll)]

            def fetch(m):
                nc.gpsimd.indirect_dma_start(
                    w[:, m % unroll, :], None, d[name + "_w"][:, :],
                    bass.IndirectOffsetOnAxis(ap=widx[:, m:m + 1], axis=0)).then_inc(w_in[m % unroll], 16)

            def scatter(pool):
                pool.wait_ge(slots_zeroed, 16)
                for t in range(NT):
                    for k in range(choices):
                        nc.gpsimd.indirect_dma_start(
                            xs[:, :], bass.IndirectOffsetOnAxis(ap=put[:, t, k:k + 1], axis=0), c.norm[:, t, :],
                            None).then_inc(scattered, 16)
                pool.wait_ge(scattered, 16 * NT * choices)
                pool.dma_start(xg[:], xs[0:rows].rearrange("(t p) d -> p t d", p=P)).then_inc(x_in, 16)
                for m in range(unroll):
                    fetch(m)
                pool.wait_ge(x_in, 16)

            ffn(c, *shared, c.xT, acc, beside=scatter)
            turned, stored = c.sem(st, "turned"), c.sem(st, "stored")
            with nc.Block() as block:
                groups = [(g, min(g + 4, tiles)) for g in range(0, tiles, 4)]

                @block.tensor
                def _(pe):
                    for n, (lo, hi) in enumerate(groups):
                        for k in range(KC):
                            for t in range(lo, hi):
                                last = nc.tensor.transpose(c.psum[:, 2 * n + k, (t - lo) * P:(t - lo + 1) * P],
                                                           xg[:, t, k * P:(k + 1) * P], c.ident[:])
                            last.then_inc(turned, 1)

                @block.scalar
                def _(act):
                    for n, (lo, hi) in enumerate(groups):
                        act.wait_ge(turned, 2 * n + 1)
                        nc.scalar.activation(xgT[:, 0, lo * P:hi * P], c.psum[:, 2 * n, 0:(hi - lo) * P],
                                             ACT.Copy).then_inc(stored, 1)

                @block.vector
                def _(dve):
                    for n, (lo, hi) in enumerate(groups):
                        dve.wait_ge(turned, 2 * n + 2)
                        nc.vector.tensor_copy(xgT[:, 1, lo * P:hi * P], c.psum[:, 2 * n + 1, 0:(hi - lo) * P]
                                              ).then_inc(stored, 1)
            sg = c.sb(inner, "silu", [f, unroll, chunks, P])
            hT = c.sb(inner, "hT", [f, unroll, chunks, P])
            products, silu_done, h_done, outputs, y_stored = (c.sem(st, n) for n in (
                "products", "silu_done", "h_done", "outputs", "y_stored"))
            wide = 2 * chunks * P > 512

            def gates(u):
                return c.psum[0:f, u, 0:chunks * P]

            def ups(u):
                return c.psum[0:f, u + unroll, 0:chunks * P] if wide else c.psum[0:f, u, chunks * P:2 * chunks * P]

            with nc.Block() as block:
                @block.gpsimd
                def _(pool):
                    for m in range(unroll, tiles):
                        pool.wait_ge(outputs, m - unroll + 1)
                        fetch(m)

                @block.tensor
                def _(pe):
                    def products_of(i, u):
                        m = unroll * i + u
                        pe.wait_ge(w_in[u], 16 * (i + 1))
                        wait(pe, y_stored, m - unroll + 1)
                        for side in range(2):
                            for n in range(chunks):
                                for k in range(KC):
                                    at = (n * KC + k) * 2 * f + side * f
                                    last = nc.tensor.matmul((ups if side else gates)(u)[:, n * P:(n + 1) * P],
                                                            w[:, u, at:at + f], xgT[:, k, bass.ds(m * P, P)],
                                                            start=k == 0, stop=k == KC - 1)
                        last.then_inc(products, 1)

                    def output(i, u):
                        m = unroll * i + u
                        pe.wait_ge(h_done, m + 1)
                        for n in range(chunks):
                            last = nc.tensor.matmul(c.psum[:, u, 0:HID], hT[:, u, n, :],
                                                    w[0:f, u, wgu + n * HID:wgu + (n + 1) * HID], start=n == 0,
                                                    stop=n == chunks - 1)
                        last.then_inc(outputs, 1)

                    run_tiles(pe, delayed("G", "D", unroll), {"G": products_of, "D": output}, count=tiles // unroll)

                @block.scalar
                def _(act):
                    def silu(i, u):
                        m = unroll * i + u
                        act.wait_ge(products, m + 1)
                        nc.scalar.activation(sg[:, u].rearrange("p n t -> p (n t)"), gates(u), ACT.Silu
                                             ).then_inc(silu_done, 1)

                    run_tiles(act, [("S", u, 0) for u in range(unroll)], {"S": silu}, count=tiles // unroll)

                @block.vector
                def _(dve):
                    def hidden(i, u):
                        m = unroll * i + u
                        dve.wait_ge(silu_done, m + 1)
                        nc.vector.tensor_tensor(hT[:, u].rearrange("p n t -> p (n t)"), ups(u),
                                                sg[:, u].rearrange("p n t -> p (n t)"), ALU.mult).then_inc(h_done, 1)

                    def store(i, u):
                        m = unroll * i + u
                        dve.wait_ge(outputs, m + 1)
                        nc.vector.tensor_copy(xg[:, m, :], c.psum[:, u, 0:HID]).then_inc(y_stored, 1)

                    run_tiles(dve, delayed("H", "Y", unroll), {"H": hidden, "Y": store}, count=tiles // unroll)

                @block.sync
                def _(sp):
                    def send(i, u):
                        m = unroll * i + u
                        sp.wait_ge(y_stored, m + 1)
                        sp.dma_start(ys[bass.ds(m, 1)].rearrange("o p d -> p (o d)"), xg[:, m, :]
                                     ).then_inc(y_out, 16)

                    run_tiles(sp, [("O", u, 0) for u in range(unroll)], {"O": send}, count=tiles // unroll)
                    sp.wait_ge(y_out, 16 * tiles)
        with ExitStack() as inner:
            back = c.sb(inner, "back", [P, NT, choices, HID])
            chain_s = c.sem(st, "chain")
            gathered = [c.sem(st, f"gathered{t}") for t in range(NT)]
            with nc.Block() as block:
                @block.gpsimd
                def _(pool):
                    for t in range(NT):
                        for k in range(choices):
                            nc.gpsimd.indirect_dma_start(
                                back[:, t, k, :], None, ys.rearrange("t p d -> (t p) d"),
                                bass.IndirectOffsetOnAxis(ap=get[:, t, k:k + 1], axis=0)).then_inc(gathered[t], 16)

                @block.vector
                def _(dve):
                    chain = Chain(dve, chain_s)
                    for t in range(NT):
                        dve.wait_ge(gathered[t], 16 * choices)
                        for k in range(choices):
                            if weight is None:
                                chain.after(nc.vector.tensor_tensor(acc[:, t, :], back[:, t, k, :], acc[:, t, :],
                                                                    ALU.add))
                            else:
                                chain.after(nc.vector.scalar_tensor_tensor(
                                    out=acc[:, t, :], in0=back[:, t, k, :], scalar=weight[:, t, k:k + 1],
                                    in1=acc[:, t, :], op0=ALU.mult, op1=ALU.add))


def clear_slots(c, st, name, tiles):
    nc = c.nc
    zeros = c.sb(st, "zeros", [P, HID])
    cleared, slots_zeroed = c.sem(st, "cleared"), c.sem(st, "slots_zeroed")
    with nc.Block() as block:
        @block.gpsimd
        def _(pool):
            nc.gpsimd.memset(zeros[:], 0.0).then_inc(cleared, 1)

        @block.sync
        def _(sp):
            sp.wait_ge(cleared, 1)
            sp.dma_start(c.dram[name + "_slots"][0:tiles * P].rearrange("(t p) d -> p t d", p=P),
                         zeros[:].unsqueeze(1).to_broadcast([P, tiles, HID])).then_inc(slots_zeroed, 16)
    return slots_zeroed


def delayed(now, later, n):
    steps = []
    for u in range(n):
        steps += [(now, u, 0), (later, (u - 1) % n, 1 if u == 0 else 0)]
    return steps


def ffn2(c):
    d, K, tiles = c.dram, 4, 16
    with ExitStack() as st:
        slots_zeroed = clear_slots(c, st, "L2", tiles)
        acc, weight = c.sb(st, "acc", [P, NT, HID]), c.sb(st, "weight", [P, NT, K])
        layernorm(c, c.resid, c.norm, c.xT, clear=acc)
        put, get, widx = c.sb(st, "put", [P, NT, K], U32), c.sb(st, "get", [P, NT, K], U32), c.sb(st, "widx", [P, tiles], U32)
        router2(c, weight, put, get, widx)
        sparse_ffn(c, "L2", 2, 88, K, tiles, 4, put, get, widx, weight, (d["L2s_gu"], d["L2s_dn"], 88), acc,
                   slots_zeroed)
        add_gated(c, acc, 6)


def ffn3(c):
    d, tiles = c.dram, (TOK + 8 * (P - 1)) // P
    with ExitStack() as st:
        slots_zeroed = clear_slots(c, st, "L3", tiles)
        acc = c.sb(st, "acc", [P, NT, HID])
        layernorm(c, c.resid, c.norm, c.xT, clear=acc)
        put, widx = c.sb(st, "put", [P, NT, 1], U32), c.sb(st, "widx", [P, tiles], U32)
        router3(c, put[:, :, 0], widx, tiles)
        sparse_ffn(c, "L3", 4, 128, 1, tiles, 3, put, put, widx, None, (d["L3s_gu"], d["L3s_dn"], 128), acc,
                   slots_zeroed)
        add_gated(c, acc, 7)



def order(text):
    steps = []
    for s in text.split():
        name = s.rstrip("'")
        what = name.rstrip("0123456789")
        steps.append((what, int(name[len(what):] or 0), len(s) - len(name)))
    return steps


ORDER0 = {
    "pe": order("P0 P1 R1' P2 A1' P3 T0 P4 T1 P5 T2 S0 T3 F' T4 R0 S1 A0"),
    "act": order("R1' N0 O1' N1 T0 N2 T1 T2 N3 N4 X0 T3 T4 R0 X1 O0"),
    "dve": order("M1' Q1' E0 V0 E1 V1 E2 V2 E3 V3 E4 V4 E5 M0 Q0 F'"),
    "pool": order("R1' R2' R3' R4' R0"),
}
ORDER3 = {
    "pe": order("P0 P1 P2 P3 T14' R2' P4 T15' P5 S3' T0 P6 T1 P7 A2' T4 P8 R3' T5 P9 S0 A3' P10 P11 T6 T7 P12 "
               "F' S1 P13 T8 R0 P14 A0 T9 T12 R1 T13 P15 S2 A1"),
    "act": order("T5' E9' N6' E10' N7' X0' E11' T6' T7' N8' E12' N9' X1' E13' T8' R0' N12' N13' T9' T12' E14' "
                "T13' R1' E15' E0 X2' E1 N14' N15' E2 N0 T14' E3 T15' N1 R2' E4 E5 T0 X3' E6 N4 E7 T1 N5 E8 "
                "T4 R3'"),
    "dve": order("V14' M2' V15' V0 Q2' V1 O1' V4 M3' V5 Q3' O2' V6 V7 O3' Z M0 V8 V9 Q0 F' M1 V12 V13 Q1 O0"),
    "pool": order("R4' R5' R6' R7' R8' R9' R12' R13' R14' R15' R0 R1"),
}


def run_tiles(eng, steps, do, chain=None, before=None, count=NT, peel_last=False):
    def emit(i, now, back):
        if now and before is not None:
            before(i)
        for what, n, of_last in steps:
            if back if of_last else now:
                do[what](i - 1 if of_last else i, n)

    emit(0, True, False)
    first = chain.n if chain is not None else 0
    with eng.Fori(1, count - peel_last) as i:
        if chain is not None:
            per = chain.per
            chain.base, chain.n = first + (i - 1) * per, 0
        emit(i, True, True)
        if chain is not None:
            assert chain.n == per, (chain.n, per)
    if peel_last:
        emit(count - 1, True, True)
    if chain is not None:
        chain.base, chain.n = first + (count - 1) * per, 0
    emit(count, False, True)


def wait(eng, sem, value):
    if not isinstance(value, int) or value > 0:
        eng.wait_ge(sem, value)



def heads_attention(c, steps, sources, blocks, units, kv_heads, eps, w_out, out_scale, mask=None, quant=None):
    nc = c.nc
    ps, G, rms = c.psum, kv_heads, quant is None
    NB, NU = len(blocks), len(units)
    normed = [j for j, b in enumerate(blocks) if b["normed"]]
    NN = len(normed)
    NQ = 4 if NN % 4 == 0 else NN
    per_kv = NH // G
    scale = HD ** -0.5
    with ExitStack() as st:
        (x_ready, proj_ready, evacuated, ve_ready, rstd_ready, norm_ready, turned, stored, scores_ready, exp_go,
         exp_done, probs_ready, pt_turned, pt_stored, o_ready, o_read, a_ready, out_ready, resid_done, dve_chain,
         pool_chain, cleared) = (c.sem(st, n) for n in (
             "x_ready", "proj_ready", "evacuated", "ve_ready", "rstd_ready", "norm_ready", "turned", "stored",
             "scores_ready", "exp_go", "exp_done", "probs_ready", "pt_turned", "pt_stored", "o_ready", "o_read",
             "a_ready", "out_ready", "resid_done", "dve_chain", "pool_chain", "cleared"))
        src = {n: c.sb(st, "src", [P, KC, P]) for n in sources} if quant is None else {
            "ctx": c.sb(st, "src", [P, KC, P])}
        if quant is not None:
            xq = c.sb(st, "xq", [P, 4, KC, P])
            xq_next = c.sb(st, "xq_next", [P, 4, KC, P])
            xb = c.sb(st, "xb", [P, 4, KC, P], BF16)
            xbig = c.sb(st, "xbig", [P, 4, KC, P], BF16)
            yo = c.sb(st, "yo", [P, 1024])
            yb = c.sb(st, "yb", [P, 1024], BF16)
            ybig = c.sb(st, "ybig", [P, 1024], BF16)
            src.update({n: xq[:, s] for s, n in enumerate(("q", "k", "v", "qx"))})
        qs = c.sb(st, "qs", [P, NQ, 512])
        st6 = c.sb(st, "st6", [P, NQ, 4, 6])
        tmp = c.sb(st, "tmph", [P, NQ, 4, 3])
        neg_mean = c.sb(st, "neg_mean", [P, NQ, 4])
        shift = c.sb(st, "shift", [P, NQ, 4])
        ve = c.sb(st, "veh", [P, NQ, 4])
        rstd = c.sb(st, "rstdh", [P, NQ, 4])
        probs = c.sb(st, "probs", [P, 2, 512])
        diagonal = per_kv == 2
        probsT = c.sb(st, "probsT", [P, 2, 4, 2, P] if diagonal else [P, 2, 512])
        mx = c.sb(st, "mx", [P, 2, 2, 8])
        attnT = c.sb(st, "attnT", [P, NH * NU // 2, P])

        with nc.Block() as block:
            @block.tensor
            def _(pe):
                def project(i, j):
                    b = blocks[j]
                    if j == 0:
                        pe.wait_ge(x_ready, i + 1)
                    wait(pe, evacuated, i * NB + j - 1)
                    for k in range(KC):
                        last = nc.tensor.matmul(ps[:, j % 2, :], src[b["src"]][:, k, :], b["w"][:, k, :],
                                                start=k == 0, stop=k == KC - 1)
                    last.then_inc(proj_ready, 1)

                def turn(i, j):
                    n = normed.index(j)
                    pe.wait_ge(norm_ready, i * NN + n + 1)
                    wait(pe, stored, i * NN + n - 1 + (n == 0 and NN % 2))
                    for h in range(4):
                        last = nc.tensor.transpose(ps[:, 2 + n % 2, h * P:(h + 1) * P],
                                                   qs[:, n % NQ, h * HD:(h + 1) * HD], c.ident[:])
                    last.then_inc(turned, 1)

                def scores(i, u):
                    qT, kT = units[u]["qT"], units[u]["kT"]
                    pe.wait_ge(stored, i * NN + 1 + max(normed.index(j) for j in units[u]["needs"]))
                    wait(pe, exp_go, i * NU + u)
                    for pair in range(4):
                        head = 8 * (u % 2) + 2 * pair
                        for r in range(2):
                            last = nc.tensor.matmul(
                                ps[:, 4, (pair * 2 + r) * 64:(pair * 2 + r + 1) * 64],
                                qT[:, r, head:head + 2, :],
                                kT[:, head // per_kv, r * 64:(r + 1) * 64], start=True, stop=True)
                    last.then_inc(scores_ready, 1)

                def turn_probs(i, u):
                    pe.wait_ge(probs_ready, i * NU + u + 1)
                    wait(pe, pt_stored, i * NU + u)
                    if u == 0:
                        wait(pe, resid_done, i)
                    for pair in range(4):
                        last = nc.tensor.transpose(ps[:, 5, pair * P:(pair + 1) * P],
                                                   probs[:, u % 2, pair * P:(pair + 1) * P], c.ident[:])
                    last.then_inc(pt_turned, 1)

                def values(i, u):
                    v = units[u]["v"]
                    pe.wait_ge(pt_stored, i * NU + u + 1)
                    if diagonal and isinstance(i, int):
                        pe.wait_ge(cleared, 1)
                    pe.wait_ge(evacuated, i * NB + 1 + units[u]["v_block"])
                    wait(pe, o_read, i * NU + u)
                    if diagonal:
                        for pair in range(4):
                            g = 4 * (u % 2) + pair
                            last = nc.tensor.matmul(ps[:, 6 + pair // 2, pair % 2 * 256:(pair % 2 + 1) * 256],
                                                    v[:, g * HD:(g + 1) * HD], probsT[:, u % 2, pair], start=True,
                                                    stop=True)
                        last.then_inc(o_ready, 1)
                        return
                    span = per_kv // 2
                    for r in range(2):
                        for pair in range(0, 4, span):
                            g = (8 * (u % 2) + 2 * pair) // per_kv
                            last = nc.tensor.matmul(
                                ps[:, 6 + r, pair * P:(pair + span) * P],
                                v[r * 64:(r + 1) * 64, g * HD:(g + 1) * HD],
                                probsT[r * 64:(r + 1) * 64, u % 2, pair * P:(pair + span) * P],
                                start=True, stop=True)
                    last.then_inc(o_ready, 1)

                def output(i, _):
                    pe.wait_ge(a_ready, (i + 1) * NU)
                    if quant is None:
                        pe.wait_ge(o_read, (i + 1) * NU)
                    pe.wait_ge(pt_stored, (i + 1) * NU)
                    n = NH * NU // 2
                    for h in range(n):
                        last = nc.tensor.matmul(ps[:, 5, 0:HID], attnT[:, h, :], w_out[:, h, :],
                                                start=h == 0, stop=h == n - 1)
                    last.then_inc(out_ready, 1)

                run_tiles(pe, steps["pe"],
                          {"P": project, "T": turn, "S": scores, "R": turn_probs, "A": values, "F": output})

            @block.scalar
            def _(act):
                def evacuate(i, j):
                    b = blocks[j]
                    act.wait_ge(proj_ready, i * NB + j + 1)
                    dst = qs[:, normed.index(j) % NQ, :] if b["normed"] else b["dst"]
                    nc.scalar.activation(dst, ps[:, j % 2, :], ACT.Copy,
                                         scale=1.0 if b["scale"] is None else b["scale"]).then_inc(evacuated, 1)

                def normalise(i, j):
                    n = normed.index(j)
                    act.wait_ge(rstd_ready, i * NN + n + 1)
                    act.wait_ge(evacuated, i * NB + j + 1)
                    for h in range(4):
                        part, s = qs[:, n % NQ, h * HD:(h + 1) * HD], rstd[:, n % NQ, h:h + 1]
                        if rms:
                            last = nc.scalar.activation(part, part, ACT.Copy, scale=s)
                        else:
                            last = nc.scalar.activation(part, part, ACT.Identity, scale=s, bias=shift[:, n % NQ, h:h + 1])
                    last.then_inc(norm_ready, 1)

                def store(i, j):
                    n, b = normed.index(j), blocks[j]
                    act.wait_ge(turned, i * NN + n + 1)
                    nc.scalar.activation(b["dst"], ps[:, 2 + n % 2, :].rearrange("p (h r n) -> p h r n", h=4, r=2),
                                         ACT.Identity, scale=b["wT"],
                                         bias=0.0 if b["bT"] is None else b["bT"]).then_inc(stored, 1)

                def exps(i, u):
                    act.wait_ge(exp_go, i * NU + u + 1)
                    nc.scalar.activation(probs[:, u % 2, :], probs[:, u % 2, :], ACT.Exp,
                                         scale=scale if mask is None else 1.0).then_inc(exp_done, 1)

                def store_probs(i, u):
                    act.wait_ge(pt_turned, i * NU + u + 1)
                    if diagonal:
                        for r in range(2):
                            rows = slice(64 * r, 64 * r + 64)
                            last = nc.scalar.activation(probsT[rows, u % 2, :, r, :],
                                                        ps[rows, 5, :].rearrange("p (h n) -> p h n", h=4), ACT.Copy)
                        last.then_inc(pt_stored, 1)
                    else:
                        nc.scalar.activation(probsT[:, u % 2, :], ps[:, 5, :], ACT.Copy).then_inc(pt_stored, 1)

                def store_out(i, u):
                    act.wait_ge(o_ready, i * NU + u + 1)
                    for r in range(2):
                        nc.scalar.activation(attnT[:, 8 * u:8 * u + 8, r * 64:(r + 1) * 64],
                                             ps[:, 6 + r, :].rearrange("p (h n) -> p h n", h=8),
                                             ACT.Copy).then_inc(o_read if r else a_ready, 1)

                run_tiles(act, steps["act"], {"E": evacuate, "N": normalise, "T": store, "X": exps, "R": store_probs,
                                              "O": store_out})

            @block.vector
            def _(dve):
                v = nc.vector

                def evacuate(i, j):
                    b = blocks[j]
                    dve.wait_ge(proj_ready, i * NB + j + 1)
                    dst = qs[:, normed.index(j) % NQ, :] if b["normed"] else b["dst"]
                    v.tensor_tensor(dst, ps[:, j % 2, :], b["bias"], ALU.add).then_inc(evacuated, 1)

                def variance(i, j):
                    b = normed.index(j) % NQ
                    dve.wait_ge(evacuated, i * NB + j + 1)
                    for h in range(4):
                        chain.add(v.bn_stats(st6[:, b, h, :], qs[:, b, h * HD:(h + 1) * HD]))
                    chain.join()
                    even, odd, t = st6[:, b, :, 1:3], st6[:, b, :, 4:6], tmp[:, b]
                    chain.add(v.tensor_tensor(t[:, :, 0:2], even, odd, ALU.add))
                    chain.after(v.tensor_tensor(t[:, :, 2], even[:, :, 0], odd[:, :, 0], ALU.subtract))
                    chain.add(v.scalar_tensor_tensor(out=t[:, :, 2], in0=t[:, :, 2], scalar=0.25, in1=t[:, :, 2],
                                                     op0=ALU.mult, op1=ALU.mult))
                    if rms:
                        chain.add(v.scalar_tensor_tensor(out=t[:, :, 0], in0=t[:, :, 0], scalar=0.25,
                                                         in1=t[:, :, 0], op0=ALU.mult, op1=ALU.mult))
                    else:
                        chain.add(v.tensor_scalar(neg_mean[:, b, :], t[:, :, 0], -0.5, None, ALU.mult))
                    chain.after(v.tensor_scalar(t[:, :, 1], t[:, :, 1], 1.0 / HD, eps, ALU.mult, ALU.add))
                    if rms:
                        chain.after(v.tensor_tensor(t[:, :, 2], t[:, :, 2], t[:, :, 0], ALU.add))
                    v.tensor_tensor(ve[:, b, :], t[:, :, 1], t[:, :, 2], ALU.add).then_inc(ve_ready, 1)

                def less_max(i, u):
                    dve.wait_ge(scores_ready, i * NU + u + 1)
                    s = ps[:, 4, :].rearrange("p (g k) -> p g k", k=64)
                    p, top = probs[:, u % 2, :].rearrange("p (g k) -> p g k", k=64), mx[:, u % 2, 0, :]
                    if mask is not None:
                        chain.after(v.scalar_tensor_tensor(out=p, in0=s, scalar=scale,
                                                           in1=mask[:].unsqueeze(1).to_broadcast([P, 8, 64]),
                                                           op0=ALU.mult, op1=ALU.add))
                        s = p
                    chain.after(v.tensor_reduce(top, s, X, ALU.max))
                    v.tensor_tensor(p, s, bc(top, [P, 8, 64]), ALU.subtract).then_inc(exp_go, 1)

                def normalise_probs(i, u):
                    dve.wait_ge(exp_done, i * NU + u + 1)
                    p = probs[:, u % 2, :].rearrange("p (g k) -> p g k", k=64)
                    chain.after(v.tensor_reduce(mx[:, u % 2, 0, :], p, X, ALU.add))
                    chain.after(v.reciprocal(mx[:, u % 2, 1, :], mx[:, u % 2, 0, :]))
                    v.tensor_tensor(p, p, bc(mx[:, u % 2, 1, :], [P, 8, 64]), ALU.mult).then_inc(probs_ready, 1)

                def quantise_out(i, u):
                    dve.wait_ge(o_ready, i * NU + u + 1)
                    wait(dve, a_ready, i * NU + u)
                    rows = ps[:, 6:8, :].rearrange("p b (q r m) -> p (b q) r m", q=2, r=2)
                    for r in range(2):
                        v.tensor_tensor(yo[:, r * 512:(r + 1) * 512].rearrange("p (q h n) -> p q h n", q=4, h=2),
                                        rows[:, :, r, :].rearrange("p q (h n) -> p q h n", h=2),
                                        bc(quant["smooth"][:, 8 * u:8 * u + 8].rearrange("p (q h) -> p q h", h=2),
                                           [P, 4, 2, 64]), ALU.mult).then_inc(o_read if r else dve_chain, 1)
                    chain.n += 1
                    chain.join()
                    dve.wait_ge(o_read, i * NU + u + 1)
                    chain.after(v.tensor_scalar(yb[:], yo[:], -448.0, 448.0, ALU.max, ALU.min))
                    chain.after(v.tensor_scalar(ybig[:].bitcast(U16), yb[:].bitcast(U16), 0x7FFF, None,
                                                ALU.bitwise_and))
                    chain.after(v.tensor_scalar(ybig[:], ybig[:], FP8_LEAST, FP8_STEP, ALU.max, ALU.mult))
                    chain.after(v.tensor_tensor(yo[:], yb[:], ybig[:], ALU.add))
                    v.tensor_tensor(attnT[:, 8 * u:8 * u + 8, :].rearrange("p h (r n) -> p r h n", r=2),
                                    yo[:].rearrange("p (r h n) -> p r h n", r=2, h=8),
                                    ybig[:].rearrange("p (r h n) -> p r h n", r=2, h=8),
                                    ALU.subtract).then_inc(a_ready, 1)

                def next_inputs(tile):
                    chain.after(v.tensor_tensor(xq_next[:], sources["x"][:, :, tile].unsqueeze(1).to_broadcast(
                        [P, 4, KC, P]), bc(quant["in_inv"][:], [P, 4, KC, P]), ALU.mult))
                    chain.after(v.tensor_scalar(xb[:], xq_next[:], -448.0, 448.0, ALU.max, ALU.min))
                    chain.after(v.tensor_scalar(xbig[:].bitcast(U16), xb[:].bitcast(U16), 0x7FFF, None,
                                                ALU.bitwise_and))
                    chain.after(v.tensor_scalar(xbig[:], xbig[:], FP8_LEAST, FP8_STEP, ALU.max, ALU.mult))
                    chain.after(v.tensor_tensor(xq_next[:], xb[:], xbig[:], ALU.add))
                    chain.after(v.tensor_tensor(xq_next[:], xq_next[:], xbig[:], ALU.subtract))
                    chain.after(v.tensor_tensor(xq_next[:], xq_next[:], bc(quant["in_scale"][:], [P, 4, KC, P]),
                                                ALU.mult))

                def after_next(i, _):
                    next_inputs(bass.ds((i + 1) % NT * P, P))

                def add_out(i, _):
                    dve.wait_ge(out_ready, i + 1)
                    at = c.resid[:, i, :]
                    v.scalar_tensor_tensor(out=at, in0=ps[:, 5, 0:HID], scalar=out_scale, in1=at, op0=ALU.mult,
                                           op1=ALU.add).then_inc(resid_done, 1)

                def take_inputs(i):
                    wait(dve, proj_ready, i * NB)
                    if quant is None:
                        chain.after(v.tensor_copy(src["x"][:], sources["x"][:, :, bass.ds(i * P, P)]))
                    else:
                        chain.after(v.tensor_copy(xq[:], xq_next[:]))
                    v.tensor_copy(src["ctx"][:], sources["ctx"][:, :, bass.ds(i * P, P)]).then_inc(x_ready, 1)

                chain = Chain(dve, dve_chain)
                if quant is not None:
                    next_inputs(slice(0, P))
                cost = {"V": 9 + rms, "M": 1 + (mask is not None), "Q": 2, "O": 5, "Z": 7}
                chain.per = 1 + sum(cost.get(what, 0) for what, _, _ in steps["dve"])
                run_tiles(dve, steps["dve"], {"E": evacuate, "V": variance, "M": less_max, "Q": normalise_probs,
                                              "O": quantise_out, "F": add_out, "Z": after_next}, chain, take_inputs)

            @block.gpsimd
            def _(pool):
                g = nc.gpsimd

                def rstds(i, j):
                    n = normed.index(j)
                    b = n % NQ
                    pool.wait_ge(ve_ready, i * NN + n + 1)
                    one = g.tensor_tensor(rstd[:, b, :], ve[:, b, :], c.mhalf[:, 0:4], ALU.pow)
                    if rms:
                        one.then_inc(rstd_ready, 1)
                    else:
                        chain.after(one)
                        g.tensor_tensor(shift[:, b, :], rstd[:, b, :], neg_mean[:, b, :], ALU.mult
                                        ).then_inc(rstd_ready, 1)

                if diagonal:
                    g.memset(probsT[:], 0.0).then_inc(cleared, 1)
                chain = Chain(pool, pool_chain)
                chain.per = 0 if rms else NN
                run_tiles(pool, steps["pool"], {"R": rstds}, chain)


def load(c, st, waits, name, shape, src=None):
    buf = c.sb(st, name, shape)
    waits.append((buf, c.dram[name] if src is None else src))
    return buf


class Loads:

    def __init__(self, c, waits):
        self.c, self.waits = c, waits
        self.sp_in, self.act_in = c.sem(None, "sp_in"), c.sem(None, "act_in")
        with c.nc.Block() as block:
            @block.sync
            def _(sp):
                for buf, src in waits[0::2]:
                    sp.dma_start(buf[:], src).then_inc(self.sp_in, 16)

            @block.scalar
            def _(act):
                for buf, src in waits[1::2]:
                    act.dma_start(buf[:], src).then_inc(self.act_in, 16)

    def finish(self):
        with self.c.nc.Block() as block:
            @block.sync
            def _(sp):
                sp.wait_ge(self.sp_in, 16 * len(self.waits[0::2]))

            @block.scalar
            def _(act):
                act.wait_ge(self.act_in, 16 * len(self.waits[1::2]))


def by_head(qT, b):
    return qT[:, :, 4 * b:4 * b + 4, :].rearrange("p r h n -> p h r n")


def by_row(kT, b):
    return kT[:, 4 * b:4 * b + 4, :].rearrange("p h (r n) -> p h r n", r=2)


def attn0(c, before):
    with ExitStack() as st:
        w = []
        wq = load(c, st, w, "L0_wq", [P, KC, NH * HD])
        wk = load(c, st, w, "L0_wk", [P, KC, 4 * HD])
        wv = load(c, st, w, "L0_wv", [P, KC, 4 * HD])
        wo = load(c, st, w, "L0_wo", [P, NH, HID])
        bias = c.sb(st, "bias", [P, 6, 512])
        w.append((bias[:, 0:4].rearrange("p b n -> p (b n)"), c.dram["L0_xattn_bq"].partition_broadcast(P)))
        w.append((bias[:, 4], c.dram["L0_xattn_bk"].partition_broadcast(P)))
        w.append((bias[:, 5], c.dram["L0_xattn_bv"].partition_broadcast(P)))
        norms = load(c, st, w, "L0_norms", [P, 2])
        mask = c.sb(st, "mask", [P, SEQ])
        w.append((mask[0:64], c.dram["mask"]))
        w.append((mask[64:128], c.dram["mask"]))
        loads = Loads(c, w)
        if before is not None:
            before(c)
        layernorm(c, c.resid, c.norm, c.xT)
        loads.finish()
        qT = c.sb(st, "qT", [P, 2, NH, SEQ])
        kT = c.sb(st, "kT", [P, 4, P])
        v = c.sb(st, "v", [P, 4 * HD])
        blocks = [dict(src="ctx", w=wk, normed=True, bias=bias[:, 4], dst=by_row(kT, 0), wT=norms[:, 1:2], bT=None),
                  ]
        blocks += [dict(src="x", w=wq[:, :, 512 * b:512 * b + 512], normed=True, bias=bias[:, b],
                        dst=by_head(qT, b), wT=norms[:, 0:1], bT=None) for b in range(4)]
        blocks += [dict(src="ctx", w=wv, normed=False, bias=bias[:, 5], dst=v[:])]
        units = [dict(qT=qT, kT=kT, v=v, needs=[0, 1 + 2 * u, 2 + 2 * u], v_block=5) for u in range(2)]
        heads_attention(c, ORDER0, {"x": c.xT, "ctx": c.ctxT}, blocks, units, 4, 1e-6, wo, c.gate[:, 0:1], mask=mask)


def attn3(c, before):
    nc = c.nc
    with ExitStack() as st:
        w = []
        wq = load(c, st, w, "L3_wq", [P, KC, NH * HD])
        wqx = load(c, st, w, "L3_wqx", [P, KC, NH * HD])
        wk = load(c, st, w, "L3_wk", [P, KC, 8 * HD])
        wv = load(c, st, w, "L3_wv", [P, KC, 8 * HD])
        wkvx = load(c, st, w, "L3_wkvx", [P, KC, 16 * HD])
        wproj = load(c, st, w, "L3_wproj", [P, 2 * NH, HID])
        ln = load(c, st, w, "L3_ln", [P, 2, KC])
        in_scale = load(c, st, w, "L3_in_scale", [P, 4, KC])
        norms = load(c, st, w, "L3_norms", [P, 4, 2])
        smooth = load(c, st, w, "L3_smooth", [P, 2 * NH])
        scales = c.sb(st, "scales", [P, 6])
        for n, s in enumerate(("wq_scale", "wk_scale", "wv_scale", "wqx_scale", "proj_w_scale", "proj_in_scale")):
            w.append((scales[:, n:n + 1], c.dram["L3_xattn_" + s].partition_broadcast(P)))
        loads = Loads(c, w)
        if before is not None:
            before(c)
        layernorm(c, c.resid, c.norm, None)
        layernorm(c, c.norm, c.norm, c.xT)
        loads.finish()
        in_inv = c.sb(st, "in_inv", [P, 4, KC])
        smooth_inv = c.sb(st, "smooth_inv", [P, 2 * NH])
        out_scale = c.sb(st, "out_scale", [P, 1])
        consts, affine = c.sem(st, "consts"), c.sem(st, "affine")
        with nc.Block() as block:
            @block.vector
            def _(dve):
                nc.vector.reciprocal(in_inv[:], in_scale[:]).then_inc(consts, 1)
                nc.vector.reciprocal(smooth_inv[:], smooth[:]).then_inc(consts, 1)
                nc.vector.tensor_tensor(out_scale[:], scales[:, 4:5], scales[:, 5:6], ALU.mult).then_inc(consts, 1)
                dve.wait_ge(consts, 3)
                nc.vector.tensor_tensor(out_scale[:], out_scale[:], c.gate[:, 3:4], ALU.mult).then_inc(consts, 1)

            @block.scalar
            def _(act):
                for k in range(KC):
                    nc.scalar.activation(c.xT[:, k, :], c.xT[:, k, :], ACT.Identity, scale=ln[:, 0, k:k + 1],
                                         bias=ln[:, 1, k:k + 1]).then_inc(affine, 1)
        qT = c.sb(st, "qT", [P, 2, NH, SEQ])
        kT = c.sb(st, "kT", [P, 8, P])
        v = c.sb(st, "v", [P, 8 * HD])
        vx = c.sb(st, "vx", [P, 8 * HD])

        def turned(src, w_, dst, n, scale):
            return [dict(src=src, w=w_[:, :, 512 * b:512 * b + 512], normed=True, scale=scale,
                         dst=dst(b), wT=norms[:, n, 0:1], bT=norms[:, n, 1:2])
                    for b in range(w_.shape[2] // 512 if src != "ctx" else 2)]

        def plain(src, w_, dst, scale, off=0):
            return [dict(src=src, w=w_[:, :, off + 512 * b:off + 512 * b + 512], normed=False, scale=scale,
                         dst=dst[:, 512 * b:512 * b + 512]) for b in range(2)]

        blocks = (turned("k", wk, lambda b: by_row(kT, b), 1, scales[:, 1:2]) + plain("v", wv, v, scales[:, 2:3])
                  + turned("q", wq, lambda b: by_head(qT, b), 0, scales[:, 0:1]) + turned("ctx", wkvx, lambda b: by_row(kT, b), 3, None)
                  + plain("ctx", wkvx, vx, None, 8 * HD) + turned("qx", wqx, lambda b: by_head(qT, b), 2, scales[:, 3:4]))
        units = [dict(qT=qT, kT=kT, v=v if u < 2 else vx, needs=[(5, 7, 13, 15)[u]], v_block=(2, 3, 10, 11)[u])
                 for u in range(4)]
        heads_attention(c, ORDER3, {"x": c.xT, "ctx": c.ctxT}, blocks, units, 8, 1e-5, wproj, out_scale[:, 0:1],
                        quant={"in_inv": in_inv, "in_scale": in_scale, "smooth": smooth_inv})



def decay_by_key():
    gam = (1.0 - 2.0 ** (-5.0 - np.arange(2, dtype=np.float32))).astype(np.float32)
    at = np.arange(SEQ, dtype=np.float32)
    expo = at[None, :] - at[:, None]
    m = np.where(expo[None] <= 0, gam[:, None, None] ** expo[None], 0.0).astype(np.float32)
    m = m / np.sqrt(m.sum(axis=-1, dtype=np.float32))[:, None, :]
    m = m.astype(np.float32).transpose(2, 0, 1)
    return np.ascontiguousarray(np.concatenate([m, m]))


def attn1(c, before):
    nc = c.nc
    with ExitStack() as st:
        w = []
        wh = load(c, st, w, "L1_wh", [P, 2, HD])
        wg = load(c, st, w, "L1_wg", [P, KC, HID])
        wo = load(c, st, w, "L1_wo", [P, KC, HID])
        decay = load(c, st, w, "L1_decay", [P, 2, SEQ])
        gamma = c.sb(st, "gamma", [P, HID])
        beta = c.sb(st, "beta", [P, HID])
        w.append((gamma, c.dram["L1_xattn_gn_gamma"].partition_broadcast(P)))
        w.append((beta, c.dram["L1_xattn_gn_beta"].partition_broadcast(P)))
        loads = Loads(c, w)
        if before is not None:
            before(c)
        layernorm(c, c.resid, c.norm, c.xT)
        loads.finish()
        qT = c.sb(st, "qT", [P, 2, TOK])
        kT = c.sb(st, "kT", [P, 2, TOK])
        v = c.sb(st, "v", [P, NT, HID])
        relu = c.sb(st, "relu", [P, NT, HID])
        mix = c.sb(st, "mix", [P, 2, P])
        (qk_ready, qk_stored, v_ready, v_stored, s_ready, mix_zero, chain_s, mix_ready, o_ready, o_stored) = (
            c.sem(st, n) for n in ("qk_ready", "qk_stored", "v_ready", "v_stored", "s_ready", "mix_zero", "chain",
                                   "mix_ready", "o_ready", "o_stored"))
        out = c.norm
        with nc.Block() as block:
            @block.tensor
            def _(pe):
                for n, (src, h, half) in enumerate((s, h, f) for s in (c.ctxT, c.xT) for h in range(2)
                                                   for f in range(2)):
                    nc.tensor.matmul(c.psum[:, n, :], wh[:, h, :], src[:, h, half * HALF:(half + 1) * HALF],
                                     start=True, stop=True).then_inc(qk_ready, 1)
                for t in range(NT):
                    pe.wait_ge(qk_stored, 6 if t < 4 else 8)
                    for h in range(2):
                        nc.tensor.matmul(c.psum[:, t // 2, t % 2 * HID + h * HD:t % 2 * HID + (h + 1) * HD],
                                         c.ctxT[:, h, t * P:(t + 1) * P], wh[:, h, :], start=True, stop=True)
                    for k in range(KC):
                        last = nc.tensor.matmul(c.psum[:, 4 + t // 2, t % 2 * HID:(t % 2 + 1) * HID],
                                                c.xT[:, k, t * P:(t + 1) * P], wg[:, k, :], start=k == 0,
                                                stop=k == KC - 1)
                    if t % 2:
                        last.then_inc(v_ready, 1)
                pe.wait_ge(v_stored, 8)
                for h in range(2):
                    for r in range(2):
                        for b in range(BATCH):
                            last = nc.tensor.matmul(c.psum[64 * r:64 * r + 64, 2 * h + r, 0:SEQ],
                                                    kT[:, h, b * SEQ:(b + 1) * SEQ], qT[:, h, b * SEQ:(b + 1) * SEQ],
                                                    start=b == 0, stop=b == BATCH - 1)
                        last.then_inc(s_ready, 1)
                pe.wait_ge(mix_ready, 4)
                for t in range(NT):
                    for h in range(2):
                        last = nc.tensor.matmul(c.psum[:, 4 + t // 2, t % 2 * HID + h * HD:t % 2 * HID + (h + 1) * HD],
                                                mix[:, h, :], v[:, t, h * HD:(h + 1) * HD], start=True, stop=True)
                    if t % 2:
                        last.then_inc(o_ready, 1)

            @block.scalar
            def _(act):
                for n in range(0, 8, 2):
                    act.wait_ge(qk_ready, n + 2)
                    nc.scalar.activation((kT if n < 4 else qT)[:, n // 2 % 2, :],
                                         c.psum[:, n:n + 2, :].rearrange("p b n -> p (b n)"),
                                         ACT.Copy).then_inc(qk_stored, 2)
                for g in range(4):
                    act.wait_ge(v_ready, g + 1)
                    nc.scalar.activation(v[:, 2 * g:2 * g + 2, :],
                                         c.psum[:, g, :].rearrange("p (t n) -> p t n", t=2), ACT.Copy).then_inc(v_stored, 1)
                    nc.scalar.activation(relu[:, 2 * g:2 * g + 2, :],
                                         c.psum[:, 4 + g, :].rearrange("p (t n) -> p t n", t=2),
                                         ACT.Relu).then_inc(v_stored, 1)
                for g in range(4):
                    act.wait_ge(o_ready, g + 1)
                    nc.scalar.activation(out[:, 2 * g:2 * g + 2, :],
                                         c.psum[:, 4 + g, :].rearrange("p (t n) -> p t n", t=2), ACT.Copy).then_inc(o_stored, 1)

            @block.vector
            def _(dve):
                chain = Chain(dve, chain_s)
                chain.after(nc.vector.memset(mix[:], 0.0))
                for h in range(2):
                    for r in range(2):
                        dve.wait_ge(s_ready, 2 * h + r + 1)
                        rows = slice(64 * r, 64 * r + 64)
                        part = mix[rows, h, 64 * r:64 * r + 64]
                        chain.after(nc.vector.scalar_tensor_tensor(
                            out=part, in0=c.psum[rows, 2 * h + r, 0:SEQ], scalar=HD ** -0.5, in1=decay[rows, h, :],
                            op0=ALU.mult, op1=ALU.mult))
                        chain.after(nc.vector.scalar_tensor_tensor(out=part, in0=part, scalar=-1.0, in1=part,
                                                                   op0=ALU.mult, op1=ALU.max))
                        nc.vector.tensor_scalar(part, part, 1.0, None, ALU.max).then_inc(mix_ready, 1)
        normed = v
        layernorm(c, out, normed, None, eps=1e-3)
        yT = qT
        (chain2, y_ready, turned, stored, p_ready, added) = (
            c.sem(st, n) for n in ("chain2", "y_ready", "turned", "y_stored", "p_ready", "added"))
        with nc.Block() as block:
            @block.vector
            def _(dve):
                chain = Chain(dve, chain2)
                for t in range(NT):
                    chain.after(nc.vector.tensor_tensor(normed[:, t, :], normed[:, t, :], gamma[:], ALU.mult))
                    chain.after(nc.vector.tensor_tensor(normed[:, t, :], normed[:, t, :], beta[:], ALU.add))
                    nc.vector.tensor_tensor(normed[:, t, :], normed[:, t, :], relu[:, t, :], ALU.mult).then_inc(y_ready, 1)
                for g in range(4):
                    dve.wait_ge(p_ready, g + 1)
                    nc.vector.scalar_tensor_tensor(
                        out=c.resid[:, 2 * g:2 * g + 2, :], in0=c.psum[:, 4 + g, :].rearrange("p (t n) -> p t n", t=2),
                        scalar=c.gate[:, 1:2], in1=c.resid[:, 2 * g:2 * g + 2, :], op0=ALU.mult,
                        op1=ALU.add).then_inc(added, 1)

            @block.tensor
            def _(pe):
                pe_transpose_tokens(c, pe, normed, y_ready, turned)
                for t in range(NT):
                    if t % 2 == 0:
                        pe.wait_ge(stored, t // 2 + 1)
                    for k in range(KC):
                        last = nc.tensor.matmul(c.psum[:, 4 + t // 2, t % 2 * HID:(t % 2 + 1) * HID],
                                                yT[:, k, t * P:(t + 1) * P], wo[:, k, :], start=k == 0, stop=k == KC - 1)
                    if t % 2:
                        last.then_inc(p_ready, 1)

            @block.scalar
            def _(act):
                act_store_transposed(c, act, yT, turned, stored)



ORDER2 = {
    "pe": order("S0 A12' T14' S1 A13' T15' S2 A14' T0 S3 A15' T1 S4 A0 T2 S5 W' A1 T3 S6 A2 T4 S7 Y' A3 T5 S8 A4 "
               "T6 S9 A5 T7 S10 A6 T8 S11 A7 T9 S12 A8 T10 S13 A9 T11 S14 A10 T12 S15 A11 T13"),
    "act": order("X0 E14' X1 E15' X2 E0 X3 E1 X4 E2 X5 E3 Z' X6 E4 X7 E5 X8 E6 X9 E7 X10 E8 X11 E9 X12 E10 X13 "
                "E11 X14 E12 X15 E13"),
    "dve": order("R14' M0 R15' J' M1 R0 M2 R1 M3 R2 O' M4 R3 M5 R4 M6 L R5 M7 R6 M8 F' R7 M9 R8 I K M10 R9 M11 "
                "R10 M12 R11 M13 R12 M14 R13 M15"),
}


def attn2(c, before):
    nc = c.nc
    H, D = NH, 16
    LN255 = float(np.log(255.0))
    with ExitStack() as st:
        w = []
        wq = load(c, st, w, "L2_wq", [P, KC, HID])
        wkv = load(c, st, w, "L2_wkv", [P, KC, 2 * HID])
        wp = load(c, st, w, "L2_wp", [P, KC, HID])
        bias = c.sb(st, "bias", [P, 2, HID])
        w.append((bias[:, 0], c.dram["L2_xattn_bq"].partition_broadcast(P)))
        w.append((bias[:, 1], c.dram["L2_bk"].partition_broadcast(P)))
        bv = load(c, st, w, "L2_bv", [P, KC])
        bp = c.sb(st, "bp", [P, HID])
        w.append((bp, c.dram["L2_xattn_bp"].partition_broadcast(P)))
        loads = Loads(c, w)
        if before is not None:
            before(c)
        layernorm(c, c.resid, c.norm, c.xT)
        loads.finish()
        qT = c.sb(st, "qT", [P, H // 2, TOK], BF16)
        kT = c.sb(st, "kT", [P, H // 2, TOK], BF16)
        v = c.sb(st, "v", [P, NT, HID], BF16)
        sq = c.sb(st, "sq", [P, NT, 2, H])
        sv = c.sb(st, "sv", [P, 2, KC])
        with ExitStack() as inner:
            qk = c.sb(inner, "qk", [P, NT, 2, HID])
            parts = c.sb(inner, "parts", [P, 2, NT, H, 4, D], BF16)
            inv = c.sb(inner, "inv", [P, NT, 2, H])
            vT = c.sb(inner, "vT", [P, KC, TOK])
            vb = c.sb(inner, "vb", [P, KC, TOK], BF16)
            (chain_s, pool_s, qk_ready, qk_read, v_ready, vT_ready, vb_ready, parts_ready, turned, stored, v_turned,
             v_stored, query_parts, zeros_set) = (c.sem(inner, n) for n in (
                 "chain", "pool_chain", "qk_ready", "qk_read", "v_ready", "vT_ready", "vb_ready", "parts_ready",
                 "turned", "stored", "v_turned", "v_stored", "query_parts", "zeros_set"))
            with nc.Block() as block:
                @block.tensor
                def _(pe):
                    for t in range(NT):
                        for s, (src, w_) in enumerate(((c.xT, wq[:, :, :]), (c.ctxT, wkv[:, :, 0:HID]))):
                            for k in range(KC):
                                last = nc.tensor.matmul(c.psum[:, t, s * HID:(s + 1) * HID],
                                                        src[:, k, t * P:(t + 1) * P], w_[:, k, :], start=k == 0,
                                                        stop=k == KC - 1)
                        last.then_inc(qk_ready, 1)
                    for n, (m, half) in enumerate((m, f) for m in range(KC) for f in range(2)):
                        pe.wait_ge(qk_read, n + 1)
                        for k in range(KC):
                            last = nc.tensor.matmul(c.psum[:, n, :], wkv[:, k, HID + m * P:HID + (m + 1) * P],
                                                    c.ctxT[:, k, half * HALF:(half + 1) * HALF], start=k == 0,
                                                    stop=k == KC - 1)
                        last.then_inc(v_ready, 1)
                    for n in range(2 * NT):
                        s, t = 1 - n // NT, n % NT
                        if t == 0:
                            pe.wait_ge(parts_ready, 1 if s else 2)
                            pe.wait_ge(query_parts, 3)
                            pe.wait_ge(zeros_set, 2)
                        b = 6 + n % 2
                        if n >= 2:
                            pe.wait_ge(stored, n - 1)
                        dst = c.psum[:, b, :].bitcast(BF16)
                        for g in range(H // 2):
                            last = nc.tensor.transpose(
                                dst[:, g * P:(g + 1) * P],
                                parts[:, s, t, 2 * g:2 * g + 2, :, :].rearrange("p h f d -> p (h f d)"), c.identb[:])
                        last.then_inc(turned, 1)
                    pe.wait_ge(vb_ready, KC)
                    pb = c.psum[:, 4:6, :].bitcast(BF16)
                    for t in range(NT):
                        for m in range(KC):
                            last = nc.tensor.transpose(pb[:, t // 4, t % 4 * HID + m * P:t % 4 * HID + (m + 1) * P],
                                                       vb[:, m, t * P:(t + 1) * P], c.identb[:])
                        if t % 4 == 3:
                            last.then_inc(v_turned, 1)

                @block.scalar
                def _(act):
                    for m in range(KC):
                        act.wait_ge(v_ready, 2 * m + 2)
                        nc.scalar.activation(vT[:, m, :], c.psum[:, 2 * m:2 * m + 2, :].rearrange("p b n -> p (b n)"),
                                             ACT.Identity, bias=bv[:, m:m + 1]).then_inc(vT_ready, 1)
                    act.wait_ge(parts_ready, 1)
                    for f in range(3):
                        nc.scalar.activation(parts[:, 1, :, :, f, :],
                                             qk[:, :, 0, :].rearrange("p t (h d) -> p t h d", d=D),
                                             ACT.Copy).then_inc(query_parts, 1)
                    for n in range(2 * NT):
                        s, t = 1 - n // NT, n % NT
                        act.wait_ge(turned, n + 1)
                        nc.scalar.activation((qT if s else kT)[:, :, t * P:(t + 1) * P],
                                             c.psum[:, 6 + n % 2, :].bitcast(BF16).rearrange("p (g n) -> p g n", g=8),
                                             ACT.Copy).then_inc(stored, 1)
                    pb = c.psum[:, 4:6, :].bitcast(BF16)
                    for g in range(2):
                        act.wait_ge(v_turned, g + 1)
                        nc.scalar.activation(v[:, 4 * g:4 * g + 4, :], pb[:, g, :].rearrange("p (t n) -> p t n", t=4),
                                             ACT.Copy).then_inc(v_stored, 1)

                @block.gpsimd
                def _(pool):
                    for s in range(2):
                        nc.gpsimd.memset(parts[:, s, :, :, 3, :], 0.0).then_inc(zeros_set, 1)

                @block.vector
                def _(dve):
                    g, chain = nc.vector, Chain(dve, chain_s)
                    for t in range(NT):
                        dve.wait_ge(qk_ready, t + 1)
                        g.tensor_tensor(qk[:, t], c.psum[:, t, :].rearrange("p (s n) -> p s n", s=2), bias[:],
                                        ALU.add).then_inc(qk_read, 1)
                    dve.wait_ge(qk_read, NT)
                    chain.after(g.tensor_scalar(qk[:, :, 0, :], qk[:, :, 0, :], D ** -0.5, None, ALU.mult))
                    flat = qk[:].rearrange("p t s (h d) -> p (t s h) d", d=D)
                    steps, inverse = sq[:].rearrange("p t s h -> p (t s h)"), inv[:].rearrange("p t s h -> p (t s h)")
                    chain.after(g.tensor_reduce(steps, flat, X, ALU.max, apply_absolute_value=True))
                    chain.after(g.tensor_scalar(steps, steps, 1 / 127.0, 1e-8, ALU.mult, ALU.max))
                    chain.after(g.reciprocal(inverse, steps))
                    chain.after(g.tensor_tensor(flat, flat, bc(inverse, [P, NT * 2 * H, D]), ALU.mult))
                    chain.after(g.tensor_scalar(qk[:], qk[:], ROUND, ROUND, ALU.add, ALU.subtract))
                    dve.sem_inc(parts_ready, 1)
                    keys = qk[:, :, 1, :].rearrange("p t (h d) -> p t h d", d=D)
                    chain.after(g.tensor_tensor(keys, keys, bc(sq[:, :, 1, :], [P, NT, H, D]), ALU.mult))
                    for f in range(3):
                        dst = parts[:, 0, :, :, f, :]
                        chain.after(g.tensor_copy(dst, keys))
                        if f < 2:
                            chain.after(g.tensor_tensor(keys, keys, dst, ALU.subtract))
                    dve.sem_inc(parts_ready, 1)
                    for m in range(KC):
                        dve.wait_ge(vT_ready, m + 1)
                        chain.after(g.tensor_reduce(sv[:, 0, m:m + 1], vT[:, m, :], X, ALU.max,
                                                    apply_absolute_value=True))
                        chain.after(g.tensor_scalar(sv[:, 0, m:m + 1], sv[:, 0, m:m + 1], 1 / 127.0, 1e-8, ALU.mult,
                                                    ALU.max))
                        chain.after(g.reciprocal(sv[:, 1, m:m + 1], sv[:, 0, m:m + 1]))
                        chain.after(g.tensor_scalar(vT[:, m, :], vT[:, m, :], sv[:, 1, m:m + 1], ROUND, ALU.mult,
                                                    ALU.add))
                        g.tensor_scalar(vb[:, m, :], vT[:, m, :], ROUND, None, ALU.subtract).then_inc(vb_ready, 1)
                    chain.after(g.tensor_scalar(bp[:], bp[:], c.gate[:, 2:3], None, ALU.mult))

        (chain_s, early_ready, late_ready, s_ready, m_ready, exp_done, rounded, turned, pt_stored, o_ready, o_scaled,
         ot_ready, ot_stored, y_ready, y_added) = (c.sem(st, n) for n in (
             "chain", "early_ready", "late_ready", "s_ready", "m_ready", "exp_done", "rounded", "turned", "pt_stored",
             "o_ready", "o_scaled", "ot_ready", "ot_stored", "y_ready", "y_added"))
        qt = c.sb(st, "qt", [P, H // 2, P], BF16)
        sqt = c.sb(st, "sqt", [P, 2, H])
        m = c.sb(st, "m", [P, H])
        nb = c.sb(st, "nb", [P, H])
        e = c.sb(st, "e", [P, 2, TOK])
        esum = c.sb(st, "esum", [P, 2, H])
        pi = c.sb(st, "pi", [P, 2, TOK], BF16)
        pT = c.sb(st, "pT", [P, 2, TOK], BF16)
        o = c.sb(st, "o", [P, HID])
        oT = c.sb(st, "oT", [P, KC, P])
        with nc.Block() as block:
            @block.tensor
            def _(pe):
                def scores(i, h):
                    rows = slice(64 * (h % 2), 64 * (h % 2) + 64)
                    if h % 8 == 0:
                        pe.wait_ge(late_ready if h else early_ready, i + 1)
                    wait(pe, exp_done, i * H + h - 1)
                    for f in range(2):
                        last = nc.tensor.matmul(c.psum[:, 2 * (h % 2) + f, :], qt[rows, h // 2, :],
                                                kT[rows, h // 2, f * HALF:(f + 1) * HALF], start=True, stop=True)
                    last.then_inc(s_ready, 1)

                def turn(i, h):
                    pe.wait_ge(rounded, i * H + h + 1)
                    dst = c.psum[:, 4 + h % 2, :].bitcast(BF16)
                    for k in range(NT):
                        last = nc.tensor.transpose(dst[:, k * P:(k + 1) * P], pi[:, h % 2, k * P:(k + 1) * P],
                                                   c.identb[:])
                    last.then_inc(turned, 1)

                def values(i, h):
                    pe.wait_ge(pt_stored, i * H + h + 1)
                    if h == 0:
                        wait(pe, o_scaled, i)
                    for k in range(NT):
                        last = nc.tensor.matmul(c.psum[:, 6, h * D:(h + 1) * D], pT[:, h % 2, k * P:(k + 1) * P],
                                                v[:, k, h * D:(h + 1) * D], start=k == 0, stop=k == NT - 1)
                    if h == H - 1:
                        last.then_inc(o_ready, 1)

                def turn_out(i, _):
                    pe.wait_ge(o_scaled, i + 1)
                    pe.wait_ge(y_added, i + 1)
                    for k in range(KC):
                        last = nc.tensor.transpose(c.psum[:, 7, k * P:(k + 1) * P], o[:, k * P:(k + 1) * P], c.ident[:])
                    last.then_inc(ot_ready, 1)

                def project(i, _):
                    pe.wait_ge(ot_stored, i + 1)
                    for k in range(KC):
                        last = nc.tensor.matmul(c.psum[:, 7, HID:2 * HID], oT[:, k, :], wp[:, k, :], start=k == 0,
                                                stop=k == KC - 1)
                    last.then_inc(y_ready, 1)

                run_tiles(pe, ORDER2["pe"], {"S": scores, "T": turn, "A": values, "W": turn_out, "Y": project})

            @block.scalar
            def _(act):
                def exps(i, h):
                    act.wait_ge(m_ready, i * H + h + 1)
                    nc.scalar.activation(e[:, h % 2, :],
                                         c.psum[:, 2 * (h % 2):2 * (h % 2) + 2, :].rearrange("p b n -> p (b n)"),
                                         ACT.Exp, scale=sqt[:, 0, h:h + 1], bias=nb[:, h:h + 1],
                                         accum_out=esum[:, 0, h:h + 1]).then_inc(exp_done, 1)

                def store(i, h):
                    act.wait_ge(turned, i * H + h + 1)
                    nc.scalar.activation(pT[:, h % 2, :], c.psum[:, 4 + h % 2, :].bitcast(BF16), ACT.Copy
                                         ).then_inc(pt_stored, 1)

                def store_out(i, _):
                    act.wait_ge(ot_ready, i + 1)
                    for k in range(KC):
                        last = nc.scalar.activation(oT[:, k, :], c.psum[:, 7, k * P:(k + 1) * P], ACT.Copy,
                                                    scale=sv[:, 0, k:k + 1])
                    last.then_inc(ot_stored, 1)

                run_tiles(act, ORDER2["act"], {"X": exps, "E": store, "Z": store_out})

            @block.vector
            def _(dve):
                g = nc.vector

                def take(t, half, ready):
                    heads = slice(8 * half, 8 * half + 8)
                    now = sq[:, bass.ds(t, 1), 0, heads].rearrange("p o h -> p (o h)")
                    chain.add(g.tensor_copy(sqt[:, 0, heads], now))
                    chain.add(g.tensor_scalar(sqt[:, 1, heads], now, -1.0, None, ALU.mult))
                    g.tensor_copy(qt[:, 4 * half:4 * half + 4], qT[:, 4 * half:4 * half + 4, bass.ds(t * P, P)]
                                  ).then_inc(ready, 1)
                    chain.join()

                def biggest(i, h):
                    dve.wait_ge(s_ready, i * H + h + 1)
                    chain.after(g.tensor_reduce(m[:, h:h + 1], c.psum[:, 2 * (h % 2):2 * (h % 2) + 2, :], XY, ALU.max))
                    g.tensor_scalar(nb[:, h:h + 1], m[:, h:h + 1], sqt[:, 1, h:h + 1], LN255, ALU.mult, ALU.add
                                    ).then_inc(m_ready, 1)

                def take_next(i, _):
                    take((i + 1) % NT, 0, early_ready)

                def take_late(i, _):
                    take(i, 1, late_ready)

                def round_probs(i, h):
                    dve.wait_ge(exp_done, i * H + h + 1)
                    wait(dve, turned, i * H + h - 1)
                    g.tensor_scalar(pi[:, h % 2, :], e[:, h % 2, :], ROUND, ROUND, ALU.add, ALU.subtract
                                    ).then_inc(rounded, 1)

                def invert_first(i, _):
                    chain.after(g.reciprocal(esum[:, 1, 0:8], esum[:, 0, 0:8]))

                def invert_last(i, _):
                    chain.after(g.reciprocal(esum[:, 1, 8:16], esum[:, 0, 8:16]))

                def scale_out(i, _):
                    dve.wait_ge(o_ready, i + 1)
                    g.tensor_tensor(o[:].rearrange("p (h d) -> p h d", d=D),
                                    c.psum[:, 6, 0:HID].rearrange("p (h d) -> p h d", d=D),
                                    bc(esum[:, 1, :], [P, H, D]), ALU.mult).then_inc(o_scaled, 1)

                def add_out(i, _):
                    dve.wait_ge(y_ready, i + 1)
                    at = c.resid[:, i, :]
                    chain.after(g.scalar_tensor_tensor(out=at, in0=c.psum[:, 7, HID:2 * HID], scalar=c.gate[:, 2:3],
                                                       in1=at, op0=ALU.mult, op1=ALU.add))
                    g.tensor_tensor(at, at, bp[:], ALU.add).then_inc(y_added, 1)

                chain = Chain(dve, chain_s)
                dve.sem_inc(y_added, 1)
                take(0, 0, early_ready)
                cost = {"M": 1, "I": 1, "J": 1, "K": 2, "L": 2, "F": 1}
                chain.per = sum(cost.get(what, 0) for what, _, _ in ORDER2["dve"])
                run_tiles(dve, ORDER2["dve"], {"M": biggest, "R": round_probs, "I": invert_first, "J": invert_last,
                                               "K": take_next, "L": take_late, "O": scale_out, "F": add_out}, chain)


STAGES = tuple(range(8))


def build(nc, dram, out):
    attention, feed_forward = (attn0, attn1, attn2, attn3), (ffn0, ffn1, ffn2, ffn3)
    with ExitStack() as ctx:
        c = Core(nc, ctx, dram)
        parts, before = [], start
        for s in range(4):
            if 2 * s in STAGES:
                parts.append((attention[s], before))
                before = None
            if 2 * s + 1 in STAGES:
                if before is not None:
                    parts.append((before,))
                before = feed_forward[s]
        if before is not None:
            parts.append((before,))
        for n, part in enumerate(parts):
            with c.new_stage():
                if n == 0:
                    start_loads(c)
                part[0](c, *part[1:])
        with c.new_stage():
            finish(c, out)



def laid_out(i):
    c = np.ascontiguousarray
    a = {n: np.asarray(v) for n, v in i.items()}
    o = {}

    def rows(w):
        return c(w.reshape(KC, P, -1).transpose(1, 0, 2))

    def gu(g, u):
        w = np.concatenate([g, u], axis=2)
        return c(w.reshape(len(g), KC, P, -1).transpose(0, 2, 1, 3))

    def cols(w, f):
        return w.reshape(HID, -1, f).transpose(1, 0, 2)

    o["x"] = c(a["x"].reshape(TOK, HID))
    o["ctx_2048"] = c(a["ctx_2048"].reshape(TOK, HID))
    o["g_xattn"], o["g_ffn"] = a["g_xattn"], a["g_ffn"]
    o["L0_router"] = rows(a["L0_ffn_gate_weight"].T)
    o["L0_ffn_similarity"] = a["L0_ffn_similarity"]
    w = a["L0_ffn_gate_up_proj"].transpose(2, 0, 1)
    o["L0_gu"] = gu(cols(w[:, :, :96].reshape(HID, -1), P), cols(w[:, :, 96:].reshape(HID, -1), P))
    o["L0_dn"] = c(a["L0_ffn_down_proj"].transpose(0, 2, 1).reshape(24, P, HID))
    inner = [np.pad(a["L1_ffn_" + n], ((0, 64), (0, 0))) for n in ("gate_w", "up_w")]
    o["L1_gu"] = gu(*(cols(w.T, P) for w in inner))
    dn = np.concatenate([a["L1_ffn_down_w"].T, a["L1_ffn_gate_s"][:, None], a["L1_ffn_up_s"][:, None]], axis=1)
    o["L1_dn"] = c(np.pad(dn, ((0, 64), (0, 0))).reshape(6, P, HID + 2))
    o["L1_ffn_down_s"] = a["L1_ffn_down_s"]
    o["L2_router"] = rows(a["L2_ffn_gate_w"].T)

    def halves(w, n):
        e, h, f = w.shape
        return w.reshape(e, h, n, f // n).transpose(0, 2, 1, 3).reshape(e * n, h, f // n)

    def by_expert(g, d, n):
        e = len(g) // n
        g = g.reshape(e, n, P, -1).transpose(0, 2, 1, 3).reshape(e, P, -1)
        d = d.reshape(e, n, -1, HID).transpose(0, 2, 1, 3).reshape(e, -1, n * HID)
        d = np.pad(d, ((0, 0), (0, P - d.shape[1]), (0, 0)))
        return c(np.concatenate([g, d], axis=2).reshape(e * P, -1))

    o["L2_w"] = by_expert(gu(halves(a["L2_ffn_w_gate"], 2), halves(a["L2_ffn_w_up"], 2)), a["L2_ffn_w_down"], 2)
    o["L2s_gu"] = gu(cols(a["L2_ffn_sw_gate"], 88), cols(a["L2_ffn_sw_up"], 88))
    o["L2s_dn"] = c(a["L2_ffn_sw_down"].reshape(4, 88, HID))
    o["L3_router"] = rows(a["L3_ffn_router_w"].T)
    w = a["L3_ffn_gate_up_proj"]
    o["L3_w"] = by_expert(gu(halves(w[:, :, :512], 4), halves(w[:, :, 512:], 4)), a["L3_ffn_down_proj"], 4)
    o["L3s_gu"] = gu(cols(a["L3_ffn_shared_gate_w"], 128), cols(a["L3_ffn_shared_up_w"], 128))
    o["L3s_dn"] = c(a["L3_ffn_shared_down_w"].reshape(4, 128, HID))

    o["L0_wq"], o["L0_wk"], o["L0_wv"] = rows(a["L0_xattn_Wq"]), rows(a["L0_xattn_Wk"]), rows(a["L0_xattn_Wv"])
    o["L0_wo"] = c(a["L0_xattn_Wo"].reshape(NH, P, HID).transpose(1, 0, 2))
    for n in ("L0_xattn_bq", "L0_xattn_bk", "L0_xattn_bv", "L1_xattn_gn_gamma", "L1_xattn_gn_beta"):
        o[n] = a[n]
    o["L0_norms"] = c(np.stack([a["L0_xattn_qn_w"], a["L0_xattn_kn_w"]], axis=1))
    o["mask"] = c(a["mask_1xSxS2_ff0"][0])
    o["L1_wh"] = c(a["L1_xattn_Wh"].transpose(1, 0, 2))
    o["L1_wg"], o["L1_wo"] = rows(a["L1_xattn_wg_w"]), rows(a["L1_xattn_wo_w"])
    o["L1_decay"] = decay_by_key()
    for n in ("wq", "wqx", "wk", "wv"):
        o["L3_" + n] = rows(a["L3_xattn_" + n].T)
    o["L3_wkvx"] = rows(a["L3_xattn_w_kv_x"].T)
    o["L3_wproj"] = c(a["L3_xattn_wproj"].T.reshape(2 * NH, P, HID).transpose(1, 0, 2))
    o["L3_ln"] = c(np.stack([a["L3_xattn_ln_w"], a["L3_xattn_ln_b"]]).reshape(2, KC, P).transpose(2, 0, 1))
    o["L3_in_scale"] = c(np.stack([a["L3_xattn_" + n + "_in_scale"] for n in ("q", "k", "v", "qx")])
                         .reshape(4, KC, P).transpose(2, 0, 1))
    o["L3_norms"] = c(np.stack([np.stack([a[f"L3_xattn_{n}ln_w"], a[f"L3_xattn_{n}ln_b"]])
                                for n in ("q", "k", "qx", "kx")]).transpose(2, 0, 1))
    o["L3_smooth"] = c(a["L3_xattn_proj_smooth"].reshape(2 * NH, P).T)
    for n in ("wq_scale", "wk_scale", "wv_scale", "wqx_scale", "proj_w_scale", "proj_in_scale"):
        o["L3_xattn_" + n] = c(a["L3_xattn_" + n].reshape(1))
    o["L2_wq"], o["L2_wkv"], o["L2_wp"] = (rows(a["L2_xattn_" + n]) for n in ("Wq", "Wkv", "Wp"))
    o["L2_xattn_bq"], o["L2_xattn_bp"], o["L2_bk"] = a["L2_xattn_bq"], a["L2_xattn_bp"], a["L2_xattn_bkv"][:HID]
    o["L2_bv"] = c(a["L2_xattn_bkv"][HID:].reshape(KC, P).T)
    return o


def kernel(**inputs):
    import concourse.bacc as bacc
    from concourse.bass_utils import run_bass_kernel_spmd

    nc = bacc.Bacc("TRN2", target_bir_lowering=False, num_devices=1)
    arrays, dram = {}, {}
    for name, a in laid_out(inputs).items():
        a = np.ascontiguousarray(a)
        arrays[f"in_{name}"] = a
        dram[name] = nc.dram_tensor(f"in_{name}", a.shape, mybir.dt.from_np(a.dtype), kind="ExternalInput").ap()
    out = nc.dram_tensor("out", (TOK, HID), F32, kind="ExternalOutput").ap()
    for name, tiles, spare in (("L2", 16, 4 * TOK), ("L3", 15, 0)):
        dram[name + "_slots"] = nc.dram_tensor(name + "_slots", (tiles * P + spare, HID), F32, kind="Internal").ap()
        dram[name + "_outs"] = nc.dram_tensor(name + "_outs", (tiles, P, HID), F32, kind="Internal").ap()
    dram["L0_comb"] = nc.dram_tensor("L0_comb", (32, TOK), F32, kind="Internal").ap()
    build(nc, dram, out)
    r = run_bass_kernel_spmd(nc, [arrays], core_ids=[0])
    return r.results[0]["out"].reshape(BATCH, SEQ, HID)
```
